# Optimizing a Trainium2 kernel written in Bass

```python
import numpy as np
import jax
import jax.numpy as jnp

def _softmax(x, axis=-1):
    return jax.nn.softmax(x, axis=axis)
def _gelu(x):
    return jax.nn.gelu(x, approximate=True)
def _silu(x):
    return jax.nn.silu(x)
def _sigmoid(x):
    return jax.nn.sigmoid(x)
def _layernorm(x, axis=-1, eps=1e-5):
    m = jnp.mean(x, axis=axis, keepdims=True)
    v = jnp.var(x, axis=axis, keepdims=True)
    return (x - m) / jnp.sqrt(v + eps)
def _scatter_add(tgt, idx, src, axis=0):
    return tgt.at[idx].add(src)
def _segment_sum(src, seg, n):
    return jax.ops.segment_sum(src, seg, n)

kernel_name = 'mk_vit_tower_d1_tok_img256_2c0ea5'

def setup_inputs(seed: int = 0):
    np.random.seed(seed)
    _w = jnp.asarray
    def _rec_inputs():
        import jax
        import jax.numpy as jnp
        _rk = jax.random.key(seed)
        x = (-7.10856e-05 + 0.999911 * jax.random.normal(jax.random.fold_in(_rk, 1), (4, 64, 512, 64), jnp.float32))
        return x
    x = _rec_inputs()
    def _L0_tok_setup():
        import jax, jax.numpy as jnp
        import numpy as np
        PATCH_LEN = 16
        STRIDE = 8
        PAD = 8
        key = jax.random.key(seed)
        k1, k2 = jax.random.split(key)
        x = jax.random.normal(k1, (32, 64, 512, 64), dtype=jnp.float32)
        in_feat = 64 * (PATCH_LEN // 2 + 1) * 2
        W = jax.random.normal(k2, (256, in_feat), dtype=jnp.float32) * 0.02
        return {'x': x, 'W': W}
    _L0_tok_all = _L0_tok_setup()
    _L0_tok_in = {k: v for k, v in _L0_tok_all.items() if k in ('W', )}
    del _L0_tok_all

    def _L0_attn_setup():
        import math
        import jax, jax.numpy as jnp
        import numpy as np
        EPS_DIV = 1e-07
        EPS_NORM = 1e-12

        def _l2_normalize(x, axis):
            n = jnp.sqrt(jnp.sum(x * x, axis=axis, keepdims=True))
            return x / jnp.maximum(n, EPS_NORM)
        key = jax.random.key(seed)
        ks = jax.random.split(key, 5)
        b, N, C = (8, 4096, 256)
        x = jax.random.normal(ks[0], (b, N, C), dtype=jnp.float32)
        W_qkv = jax.random.normal(ks[1], (C, 3 * C), dtype=jnp.float32) * (1.0 / math.sqrt(C))
        b_qkv = jax.random.normal(ks[2], (3 * C,), dtype=jnp.float32) * 0.02
        W_out = jax.random.normal(ks[3], (C, C), dtype=jnp.float32) * (1.0 / math.sqrt(C))
        b_out = jax.random.normal(ks[4], (C,), dtype=jnp.float32) * 0.02
        return {'x': x, 'W_qkv': W_qkv, 'b_qkv': b_qkv, 'W_out': W_out, 'b_out': b_out}
    _L0_attn_all = _L0_attn_setup()
    _L0_attn_in = {k: v for k, v in _L0_attn_all.items() if k in ('W_qkv', 'b_qkv', 'W_out', 'b_out', )}
    del _L0_attn_all

    def _L0_ffn_setup():
        import jax, jax.numpy as jnp
        import numpy as np
        NUM_EXPERTS = 8
        TOP_K = 2
        B, S, D = (8, 8192, 256)

        def _moe(tokens, router_w, w1, b1, w2, b2):
            N = tokens.shape[0]
            E = router_w.shape[0]
            logits = tokens.astype(jnp.float32) @ router_w.astype(jnp.float32).T
            probs = jax.nn.softmax(logits, axis=-1)
            rw, re = jax.lax.top_k(probs, TOP_K)
            if TOP_K > 1:
                rw = rw / jnp.maximum(rw.sum(-1, keepdims=True), 1e-12)
            rw = rw.astype(tokens.dtype)
            combine = jnp.zeros((N, E), tokens.dtype).at[jnp.arange(N)[:, None], re].set(rw)
            out = tokens
            for e in range(E):
                h = jax.nn.gelu(tokens @ w1[e] + b1[e], approximate=False)
                y = h @ w2[e] + b2[e]
                out = out + combine[:, e:e + 1] * y
            return out
        key = jax.random.key(seed)
        ks = jax.random.split(key, 4)
        scale = 1.0 / np.sqrt(D).astype(np.float32)
        return {'input_embeddings': jax.random.normal(ks[0], (B, S, D), jnp.float32), 'router_w': jax.random.normal(ks[1], (NUM_EXPERTS, D), jnp.float32) * scale, 'w1': jax.random.normal(ks[2], (NUM_EXPERTS, D, D), jnp.float32) * scale, 'b1': jnp.zeros((NUM_EXPERTS, D), jnp.float32), 'w2': jax.random.normal(ks[3], (NUM_EXPERTS, D, D), jnp.float32) * scale, 'b2': jnp.zeros((NUM_EXPERTS, D), jnp.float32)}
    _L0_ffn_all = _L0_ffn_setup()
    _L0_ffn_in = {k: v for k, v in _L0_ffn_all.items() if k in ('router_w', 'w1', 'b1', 'w2', 'b2', )}
    del _L0_ffn_all

    return {
        "x": x,
        "L0_tok_W": _L0_tok_in["W"],
        "L0_attn_W_qkv": _L0_attn_in["W_qkv"],
        "L0_attn_b_qkv": _L0_attn_in["b_qkv"],
        "L0_attn_W_out": _L0_attn_in["W_out"],
        "L0_attn_b_out": _L0_attn_in["b_out"],
        "L0_ffn_router_w": _L0_ffn_in["router_w"],
        "L0_ffn_w1": _L0_ffn_in["w1"],
        "L0_ffn_b1": _L0_ffn_in["b1"],
        "L0_ffn_w2": _L0_ffn_in["w2"],
        "L0_ffn_b2": _L0_ffn_in["b2"],
    }

def reference(x, L0_tok_W, L0_attn_W_qkv, L0_attn_b_qkv, L0_attn_W_out, L0_attn_b_out, L0_ffn_router_w, L0_ffn_w1, L0_ffn_b1, L0_ffn_w2, L0_ffn_b2):
    import jax
    import jax.numpy as jnp
    def _L0_tok_ref(x, W):
        import jax, jax.numpy as jnp
        import numpy as np
        PATCH_LEN = 16
        STRIDE = 8
        PAD = 8
        B, C, T, V = x.shape
        xp = jnp.pad(x, ((0, 0), (0, 0), (0, PAD), (0, 0)), mode='edge')
        Tp = T + PAD
        N = (Tp - PATCH_LEN) // STRIDE + 1
        idx = jnp.arange(N)[:, None] * STRIDE + jnp.arange(PATCH_LEN)[None, :]
        patches = xp[:, :, idx, :]
        patches = jnp.transpose(patches, (0, 4, 2, 3, 1))
        xf = jnp.fft.rfft(patches, axis=-2, norm='ortho')
        F = xf.shape[-2]
        x_real = xf.real.reshape(B, V, N, F * C)
        x_imag = xf.imag.reshape(B, V, N, F * C)
        x_emb = jnp.concatenate([x_real, x_imag], axis=-1)
        x_emb = x_emb @ W.T
        return x_emb.reshape(B, V * N, -1)

    def _L0_attn_ref(x, W_qkv, b_qkv, W_out, b_out):
        import math
        import jax, jax.numpy as jnp
        import numpy as np
        EPS_DIV = 1e-07
        EPS_NORM = 1e-12

        def _l2_normalize(x, axis):
            n = jnp.sqrt(jnp.sum(x * x, axis=axis, keepdims=True))
            return x / jnp.maximum(n, EPS_NORM)
        b, N, C = x.shape
        qkv = x @ W_qkv + b_qkv
        q, k, v = jnp.split(qkv, 3, axis=2)
        q = q - jnp.mean(q, axis=2, keepdims=True)
        k = k - jnp.mean(k, axis=2, keepdims=True)
        q2 = q * q
        k2 = k * k
        q2s = jnp.sum(q2, axis=2, keepdims=True)
        k2s = jnp.sum(k2, axis=2, keepdims=True)
        k2 = _l2_normalize(k2 / (k2s + EPS_DIV), axis=-2)
        q2 = _l2_normalize(q2 / (q2s + EPS_DIV), axis=-1)
        kv = jnp.einsum('bnc,bnd->bcd', k2, v)
        t2 = jnp.einsum('bnc,bcd->bnd', q2, kv) / math.sqrt(N)
        attn = v + t2
        return attn @ W_out + b_out

    def _L0_ffn_ref(input_embeddings, router_w, w1, b1, w2, b2):
        import jax, jax.numpy as jnp
        import numpy as np
        NUM_EXPERTS = 8
        TOP_K = 2
        B, S, D = (8, 8192, 256)

        def _moe(tokens, router_w, w1, b1, w2, b2):
            N = tokens.shape[0]
            E = router_w.shape[0]
            logits = tokens.astype(jnp.float32) @ router_w.astype(jnp.float32).T
            probs = jax.nn.softmax(logits, axis=-1)
            rw, re = jax.lax.top_k(probs, TOP_K)
            if TOP_K > 1:
                rw = rw / jnp.maximum(rw.sum(-1, keepdims=True), 1e-12)
            rw = rw.astype(tokens.dtype)
            combine = jnp.zeros((N, E), tokens.dtype).at[jnp.arange(N)[:, None], re].set(rw)
            out = tokens
            for e in range(E):
                h = jax.nn.gelu(tokens @ w1[e] + b1[e], approximate=False)
                y = h @ w2[e] + b2[e]
                out = out + combine[:, e:e + 1] * y
            return out
        b, s, d = input_embeddings.shape
        tokens = input_embeddings.reshape(b * s, d)
        return _moe(tokens, router_w, w1, b1, w2, b2).reshape(b, s, d)

    h = _L0_tok_ref(x, L0_tok_W)
    h = h + _L0_attn_ref(_layernorm(h, axis=-1), L0_attn_W_qkv, L0_attn_b_qkv, L0_attn_W_out, L0_attn_b_out)
    h = h + _L0_ffn_ref(_layernorm(h, axis=-1), L0_ffn_router_w, L0_ffn_w1, L0_ffn_b1, L0_ffn_w2, L0_ffn_b2)
    return h


_drawn_inputs = setup_inputs


def setup_inputs(seed=0):
    import zlib

    import numpy as np

    out = dict(_drawn_inputs(seed))
    spreads = {'L0_ffn_b1': (0.0, 0.345), 'L0_ffn_b2': (0.0, 0.1)}
    factors = {}
    for name, (base, spread) in spreads.items():
        noise = np.random.default_rng([zlib.crc32(name.encode()), seed]).standard_normal(out[name].shape)
        drawn = base * np.exp(spread * noise) if base else spread * noise
        out[name] = jnp.asarray(drawn.astype(out[name].dtype))
    for name, factor in factors.items():
        out[name] = (out[name] * factor).astype(out[name].dtype)
    return out
```

```python
from contextlib import ExitStack

import concourse.bass as bass
from concourse import mybir

F32 = mybir.dt.float32
F32R = mybir.dt.float32r
F16 = mybir.dt.float16
U32 = mybir.dt.uint32
ALU = mybir.AluOpType
ACT = mybir.ActivationFunctionType
AX = mybir.AxisListType
ds = bass.ds

P = 128
B, C, T, V = 4, 64, 512, 64
D = 256
E = 8
PATCH, STRIDE = 16, 8
NPATCH = T // STRIDE
NT = V * NPATCH
TILES = NT // P
CHUNK_TILES = 4
CHUNKS = TILES // CHUNK_TILES
CT = CHUNK_TILES * P
KC = C * PATCH // P
ROWS = CT // V * STRIDE // 2 + STRIDE // 2
XC = ROWS * V
XQ = XC // 4
DC = D // P
FREQ = [(0, f) for f in range(PATCH // 2 + 1)] + [(1, f) for f in range(1, PATCH // 2)]
KW = len(FREQ) * C // P

WS = 64.0
KS = 256.0
EPS_LN, EPS_DIV, EPS_NORM = 1e-5, 1e-7, 1e-12

BLOCK = 256
REGION = NT // BLOCK
NBLOCKS = 2 * NT // BLOCK + E - 1
PLACES = (E + 1) * NT
SETUP_LOADS = 20
UC = 3
assert NBLOCKS % UC == 0


def build(nc, a, out):
    ctx = ExitStack()
    with ctx:
        def sb(name, shape, dt):
            return ctx.enter_context(nc.sbuf_tensor(name, shape, dt))

        def sem(name):
            return ctx.enter_context(nc.semaphore(name))

        xn2_rows = nc.dram_tensor("xn2_rows", (NT, 2 * D), F16, kind="Internal").ap()
        place_ids = nc.dram_tensor("place_ids", (PLACES, 1), U32, kind="Internal").ap()
        y_rows = nc.dram_tensor("y_rows", (NBLOCKS * BLOCK, D), F32, kind="Internal").ap()

        w_tok = sb("w_tok", [P, 2, KC, D], F32R)
        w_k = sb("w_k", [P, 2, DC, D], F16)
        w_q = sb("w_q", [P, 2, DC, D], F16)
        w_vo = sb("w_vo", [P, 2, DC, D], F16)
        w_vo32 = sb("w_vo32", [P, DC, D], F32)
        w_r = sb("w_r", [P, 2, DC, E], F16)
        w_1 = sb("w_1", [P, 2, E, DC, D], F16)
        w_2 = sb("w_2", [P, 2, E, DC, D], F16)
        bvo = sb("bvo", [P, D], F32)
        row_k = sb("row_k", [P, D], F16)
        row_o = sb("row_o", [P, D], F16)
        row_2 = sb("row_2", [P, E, D], F16)
        col_q = sb("col_q", [P, DC], F32)
        col_1 = sb("col_1", [P, E, DC], F32)
        m_at = sb("m_at", [P, 2, DC, D + 2], F32R)
        ones_r = sb("ones_r", [P, 2], F32R)
        ones32 = sb("ones32", [P, 2], F32)
        first2 = sb("first2", [P, P], F16)
        zeros = sb("zeros", [P, D + 2], F16)
        ident = sb("ident", [P, P], F32)
        ident16 = sb("ident16", [P, P], F16)
        earlier = sb("earlier", [P, P], F16)
        ones16 = sb("ones16", [P, P], F16)
        pick = sb("pick", [P, 2], F32)
        eps_ln = sb("eps_ln", [P, 1], F32)
        iota_e = sb("iota_e", [P, E], F32)
        region0 = sb("region0", [P, E], F32)
        thr = sb("thr", [P, REGION], F32)
        upto = sb("upto", [P, E, E], F32)
        iota_b = sb("iota_b", [P, NBLOCKS], F32)
        ids_0 = sb("ids_0", [P, CHUNK_TILES], F32)
        ids_f = sb("ids_f", [P, CHUNK_TILES], F32)

        h = sb("h", [P, TILES, D], F32)
        xnT = sb("xnT", [P, 2, DC, NT], F16)
        x_raw = sb("x_raw", [P, 4, XQ], F32)
        x_hi = sb("x_hi", [P, 2, XC], F32R)
        x_lo = sb("x_lo", [P, 2, XC], F32R)
        k4acc = sb("k4acc", [P, D], F32)
        scr = sb("scr", [P, 6144], F32)

        def view(at, words, dt=F32):
            v = scr[:, at:at + words]
            return v if dt == F32 else v.bitcast(dt)

        xn32 = view(0, 1024).rearrange("p (t d) -> p t d", t=4)
        xn_hi = view(1024, 1032, F16).rearrange("p (t d) -> p t d", t=8)
        xn_lo = view(2056, 1032, F16).rearrange("p (t d) -> p t d", t=8)
        k2 = view(3088, 512).rearrange("p (t d) -> p t d", t=2)
        k2_hi = view(3600, 256, F16).rearrange("p (t d) -> p t d", t=2)
        k2_lo = view(3856, 256, F16).rearrange("p (t d) -> p t d", t=2)
        k4 = view(4112, 512).rearrange("p (t d) -> p t d", t=2)
        q2 = view(0, 1024).rearrange("p (c t) -> p c t", c=DC)
        q4 = view(1024, 1024).rearrange("p (c t) -> p c t", c=DC)
        q4s = view(2048, 512)
        xn2_32 = view(2560, 1024).rearrange("p (t d) -> p t d", t=4)
        xn2 = view(3584, 2048, F16).rearrange("p (t d) -> p t d", t=8)
        xn2T = view(5632, 512, F16).rearrange("p (t d) -> p t d", t=2)
        kxs = view(2560, 514).rearrange("p (c d) -> p c d", c=DC)
        kxT = view(3584, 512)
        m32 = view(4096, 512).rearrange("p (c d) -> p c d", c=DC)
        q2_hi = x_hi[:, 1, 0:1024].rearrange("p (c t) -> p c t", c=DC)
        q2_lo = x_lo[:, 1, 0:1024].rearrange("p (c t) -> p c t", c=DC)
        q4_hi = x_hi[:, 1, 1024:1536]
        q4_lo = x_lo[:, 1, 1024:1536]
        xg = [view(512 * n, 512, F16).rearrange("p (h d) -> p h d", h=2) for n in range(UC)]
        xT = [view(1536 + 512 * n, 512, F16).rearrange("p (c t) -> p c t", c=4) for n in range(UC)]
        g32 = [view(3072 + 512 * n, 512) for n in range(UC)]
        g_hi = [view(4608 + 512 * n, 256, F16) for n in range(UC)]
        g_lo = [view(4864 + 512 * n, 256, F16) for n in range(UC)]
        yg = [[view(512 * n + 256 * s, 256) for s in range(2)] for n in range(4)]
        mixed = [view(2048 + 256 * n, 256) for n in range(4)]
        summed = [view(3072 + 256 * n, 256) for n in range(4)]

        st = sb("st", [P, 4, 6], F32)
        mv = sb("mv", [P, 4, 2], F32)
        sd = sb("sd", [P, 4], F32)
        rstd = sb("rstd", [P, 4], F32)
        add_by = sb("add_by", [P, 2, 4], F32)
        k2s = sb("k2s", [P, 2], F32)
        k_eps = sb("k_eps", [P, 1], F32)
        k_scale = sb("k_scale", [P, 2], F32)
        q_n = sb("q_n", [P, 2], F32)
        r_tmp = sb("r_tmp", [P, 2, 5], F32)
        att = sb("att", [P, 2, D], F32)
        top = sb("top", [P, 4, 8], F32)
        top_i = sb("top_i", [P, 4, 8], U32)
        e_f = sb("e_f", [P, 4, 2], F32)
        gap = sb("gap", [P, TILES], F32)
        hot = sb("hot", [P, 4, 2, E], F32)
        sel = sb("sel", [P, 4, E], F16)
        before = sb("before", [P, 5, E], F16)
        pos = sb("pos", [P, 4, E], F32)
        hot_pos = sb("hot_pos", [P, 4, 2, E], F32)
        slot_f = sb("slot_f", [P, 4, 2], F32)
        slot_u = sb("slot_u", [P, 4, 2], U32)
        slots = sb("slots", [P, TILES, 2], F32)
        e_all = sb("e_all", [P, TILES, 2], F32)
        rows_at = sb("rows_at", [P, TILES, 2], U32)
        e_shift = sb("e_shift", [P, E], F32)
        id_u = sb("id_u", [P, CHUNK_TILES], U32)
        gate = sb("gate", [P, 3, TILES], F32)
        cnt = sb("cnt", [P, E], F32)
        cmp_t = view(3072, 128).rearrange("p (e r) -> p e r", e=E)
        n_blk = sb("n_blk", [P, E], F32)
        cum_m = view(3200, 64).rearrange("p (e r) -> p e r", e=E)
        cum = sb("cum", [P, E], F32)
        b_cmp = view(3264, 312).rearrange("p (n e) -> p n e", e=E)
        b_cmpn = view(3584, 312).rearrange("p (n e) -> p n e", e=E)
        b_e = sb("b_e", [P, NBLOCKS], F32)
        b_0 = sb("b_0", [P, NBLOCKS], F32)
        b_at = sb("b_at", [P, NBLOCKS], F32)
        blk_at = sb("blk_at", [P, NBLOCKS], U32)
        blk_e = sb("blk_e", [P, NBLOCKS], U32)
        ids_all = sb("ids_all", [P, NBLOCKS, 2], U32)
        ids_now = sb("ids_now", [P, UC, 2], U32)
        slot_now = sb("slot_now", [P, 4, 2], U32)
        minv = sb("minv", [P, 2, DC], F32)

        bank = [ctx.enter_context(nc.psum_tensor(f"bank{n}", [P, 512], F32)) for n in range(8)]

        def half(n, s):
            return bank[n][:, D * s:D * s + D]

        phase_end, waited = sem("phase_end"), sem("waited")
        coef_made, w_made, w_kept = sem("coef_made"), sem("w_made"), sem("w_kept")
        loaded = sem("loaded")
        loaded2 = sem("loaded2")
        x_in = [sem(f"x_in{q}") for q in range(4)]
        x_hi_done, x_lo_done = sem("x_hi_done"), sem("x_lo_done")
        h_made, h_kept = sem("h_made"), sem("h_kept")
        var_made, sd_made = sem("var_made"), sem("sd_made")
        xn_made, xn_hi_made, xn_lo_made = sem("xn_made"), sem("xn_hi_made"), sem("xn_lo_made")
        xn_turned, xnT_hi_made, xnT_lo_made = sem("xn_turned"), sem("xnT_hi_made"), sem("xnT_lo_made")
        k_made, k2_made, k_scaled = sem("k_made"), sem("k2_made"), sem("k_scaled")
        k2_hi_made, k2_lo_made, k4_made = sem("k2_hi_made"), sem("k2_lo_made"), sem("k4_made")
        k4_added, kx_added = sem("k4_added"), sem("kx_added")
        q_made, q2_made, q4_made, q4_summed = sem("q_made"), sem("q2_made"), sem("q4_made"), sem("q4_summed")
        q2_split, q4_hi_made, q4_split = sem("q2_split"), sem("q4_hi_made"), sem("q4_split")
        kx_kept, kx_turned, kxT_kept = sem("kx_kept"), sem("kx_turned"), sem("kxT_kept")
        norms_made, norms_rooted, m_summed, m_ready = (
            sem("norms_made"), sem("norms_rooted"), sem("m_summed"), sem("m_ready"))
        p2_made, p1_made, q_rooted = sem("p2_made"), sem("p1_made"), sem("q_rooted")
        p2_used, p1_used = sem("p2_used"), sem("p1_used")
        var2_made, sd2_made = sem("var2_made"), sem("sd2_made")
        xn2_made, xn2_hi_made, xn2_lo_made = sem("xn2_made"), sem("xn2_hi_made"), sem("xn2_lo_made")
        xn2_stored = [sem(f"xn2_stored{n}") for n in range(8)]
        xn2_turned, xn2T_made, logits_made, logits_read = (
            sem("xn2_turned"), sem("xn2T_made"), sem("logits_made"), sem("logits_read"))
        sel_made, ranks_made, slots_made, ids_stored = (
            sem("sel_made"), sem("ranks_made"), sem("slots_made"), sem("ids_stored"))
        counts_made, exp_made, blocks_made = sem("counts_made"), sem("exp_made"), sem("blocks_made")
        ids_in = sem("ids_in")
        ids_copied = sem("ids_copied")
        xg_in = [sem(f"xg_in{n}") for n in range(UC)]
        xg_turned, xT_made = sem("xg_turned"), sem("xT_made")
        up_made, gelu_made, g_hi_made, g_split = sem("up_made"), sem("gelu_made"), sem("g_hi_made"), sem("g_split")
        down_made, y_made = sem("down_made"), sem("y_made")
        y_stored = [sem(f"y_stored{n}") for n in range(UC)]
        slot_copied = sem("slot_copied")
        y_in = [sem(f"y_in{n}") for n in range(4)]
        out_made = sem("out_made")
        out_stored = [sem(f"out_stored{n}") for n in range(4)]

        def all_meet(eng, k):
            settled(eng)
            eng.drain().then_inc(phase_end, 1)
            eng.wait_ge(phase_end, 5 * k)
            settled(eng)

        def settled(eng):
            eng.sem_inc(waited, 1)

        def three(eng, o, hi, lo, w_hi, w_lo, first, last, free=False):
            eng.matmul(o, hi, w_hi, start=first, stop=False, skip_group_check=free)
            eng.matmul(o, lo, w_hi, start=False, stop=False, skip_group_check=free)
            return eng.matmul(o, hi, w_lo, start=False, stop=last, skip_group_check=free)

        def run(eng, step, last, looped=TILES):
            for n in range(8):
                step(n, n)
            with eng.Fori(1, looped // 8) as it:
                for n in range(8):
                    step(it * 8 + n, 8 + n)
            for n in range(looped, last):
                step(n, n)

        def run_c(eng, step, last):
            for n in range(2 * UC):
                step(n, n)
            with eng.Fori(2, NBLOCKS // UC) as it:
                for n in range(UC):
                    step(it * UC + n, 2 * UC + n)
            for n in range(NBLOCKS, last):
                step(n, n)

        def chunk_of(b, i, n):
            return b * CHUNKS + i // 4

        def stored_before(b, i, n):
            return 16 * (b * (TILES // 8)) + 16 * (i // 8)

        def quarter_in(b, i, n):
            return 16 * (chunk_of(b, i, n) + 2)

        LAST_A = TILES + 6
        LAST_B = TILES + 8

        block = ctx.enter_context(nc.Block())

        @block.sync
        def _(sp):
            def load(o, i):
                sp.dma_start(o, i).then_inc(loaded, 16)
            for name, t in (("ident", ident), ("pick", pick), ("iota_e", iota_e), ("region0", region0),
                            ("thr", thr), ("upto", upto), ("iota_b", iota_b), ("ids_0", ids_0)):
                load(t[:], a["c_" + name])
            c_tri = x_raw[:, 0, 0:P]
            load(c_tri, a["c_tri"])
            load(x_raw[:, 0, 128:256], a["c_coef"])
            load(x_raw[:, 0, 256:320], a["c_pair"])
            f_rows = x_lo[:, 0, 0:2048].bitcast(F32)
            load(scr[:, 0:2048].rearrange("p (q d) -> p q d", q=KW), a["w_tok"])
            load(scr[:, 2048:3584].rearrange("p (c n) -> p c n", c=DC), a["w_qkv"])
            load(scr[:, 3584:4096].rearrange("p (c n) -> p c n", c=DC), a["w_out"])
            load(scr[:, 4096:4608].rearrange("p (c n) -> p c n", c=DC), a["w_vT"])
            load(scr[:, 4608:4624].rearrange("p (c n) -> p c n", c=DC), a["w_r"])
            load(scr[:, 4624:5392], a["b_qkv"])
            load(scr[:, 5392:5648], a["b_out"])
            load(scr[:, 5648:5652], a["b_qv_col"])
            load(col_1[:].rearrange("p e c -> p (e c)"), a["b_1"])
            sp.dma_start(h[:, 0:16, :].rearrange("p (e c) d -> p e c d", e=E), a["w_1"]).then_inc(loaded2, 16)
            sp.dma_start(h[:, 16:32, :].rearrange("p (e c) d -> p e c d", e=E), a["w_2"]).then_inc(loaded2, 16)
            all_meet(sp, 1)
            sp.dma_start(h[:, 0:8, :], a["b_2"]).then_inc(loaded2, 16)
            sp.dma_start(place_ids.rearrange("(p n) o -> p (n o)", p=P), h[:, 8:10, :].rearrange(
                "p t d -> p (t d)")[:, 0:PLACES // P].bitcast(U32)).then_inc(loaded2, 16)
            for q in range(4):
                sp.dma_start(x_raw[:, q, :], a["x"][0][:, q * XQ:(q + 1) * XQ]).then_inc(x_in[q], 16)
            sp.wait_ge(loaded2, 64)
            all_meet(sp, 2)

            with sp.Fori(0, B) as b:
                with sp.Fori(0, CHUNKS) as c:
                    for q in range(4):
                        sp.wait_ge(x_hi_done, 4 * (b * CHUNKS + c) + q + 1)
                        sp.wait_ge(x_lo_done, 4 * (b * CHUNKS + c) + q + 1)
                        sp.dma_start(x_raw[:, q, :], a["x"][ds(b * CHUNKS + c + 1, 1), :, q * XQ:(q + 1) * XQ]
                                     .rearrange("o p n -> (o p) n")).then_inc(x_in[q], 16)
                all_meet(sp, 3 + 4 * b)

                def store_rows(i, n):
                    sp.wait_ge(xn2_hi_made, b * TILES + i + 1)
                    sp.wait_ge(xn2_lo_made, b * TILES + i + 1)
                    sp.dma_start(xn2_rows[ds(i * P, P), :], xn2[:, n % 8, :])\
                      .then_inc(xn2_stored[n % 8], 16)
                run(sp, store_rows, TILES, TILES - 8)
                for n in range(8):
                    sp.wait_ge(xn2_stored[n], 16 * (TILES // 8) * (b + 1))
                all_meet(sp, 4 + 4 * b)

                sp.wait_ge(blocks_made, b + 1)
                settled(sp)
                with sp.Fori(0, NBLOCKS) as i:
                    at = sp.value_load(blk_at[0:1, ds(i, 1)], min_val=0, max_val=PLACES // BLOCK - 1)
                    sp.dma_start(ids_all[:, ds(i, 1), :].rearrange("p o h -> p (o h)"),
                                 place_ids[ds(at * BLOCK, BLOCK), :].rearrange("(p h) o -> p (h o)", p=P))\
                      .then_inc(ids_in, 16)
                with sp.Fori(0, NBLOCKS // UC) as it:
                    for n in range(UC):
                        sp.wait_ge(y_made, b * NBLOCKS + it * UC + n + 1)
                        sp.dma_start(y_rows[ds((it * UC + n) * BLOCK, BLOCK), :].rearrange("(p h) d -> p (h d)", p=P),
                                     g32[n]).then_inc(y_stored[n], 16)
                for n in range(UC):
                    sp.wait_ge(y_stored[n], 16 * (NBLOCKS // UC) * (b + 1))
                all_meet(sp, 5 + 4 * b)

                with sp.Fori(0, CHUNKS) as c:
                    for n in range(4):
                        sp.wait_ge(out_made, b * TILES + c * 4 + n + 1)
                        sp.dma_start(out[ds((b * TILES + c * 4 + n) * P, P), :], summed[n]).then_inc(out_stored[n], 16)
                for n in range(4):
                    sp.wait_ge(out_stored[n], 16 * CHUNKS * (b + 1))
                all_meet(sp, 6 + 4 * b)
            for q in range(4):
                sp.wait_ge(x_in[q], 16 * (B * CHUNKS + 1))

        @block.tensor
        def _(pe):
            f_w = scr[:, 0:2048].rearrange("p (q d) -> p q d", q=KW)
            f_c = xnT[:].rearrange("p a c t -> p (a c t)").bitcast(F32).rearrange(
                "p (q k m) -> p q k m", q=KW, k=KC)
            w_out_f = scr[:, 3584:4096].rearrange("p (c n) -> p c n", c=DC)
            w_vT_f = scr[:, 4096:4608].rearrange("p (c n) -> p c n", c=DC)
            bv_b = x_raw[:, 2, 0:2 * P].rearrange("p (c m) -> p c m", c=DC)
            pe.wait_ge(coef_made, 1)
            for k in range(KC):
                for q in range(KW):
                    mm = pe.matmul(half(k // 2, k % 2), f_c[:, q, k, :], f_w[:, q, :], start=q == 0, stop=q == KW - 1)
                if k % 2:
                    mm.then_inc(w_made, 1)
            for d in range(DC):
                for c in range(DC):
                    mm = pe.matmul(half(4, d), w_vT_f[:, c, d * P:d * P + P], w_out_f[:, c, :], start=c == 0, stop=c == 1)
            mm.then_inc(w_made, 1)
            for c in range(DC):
                mm = pe.matmul(half(5, 0), bv_b[:, c, :], w_out_f[:, c, :], start=c == 0, stop=c == 1)
            mm.then_inc(w_made, 1)
            all_meet(pe, 1)
            all_meet(pe, 2)

            with pe.Fori(0, B) as b:
                for c in range(DC):
                    pe.matmul(bank[4 + c][:, 0:D + 1], zeros[:, 0:P], zeros[:, 0:D + 1], start=True, stop=False,
                              skip_group_check=True)

                def step_a(i, n):
                    g = b * TILES + i
                    if n < TILES:
                        s, par = n % 4, n // 4 % 2
                        if s == 0:
                            pe.wait_ge(x_hi_done, g + 4)
                            pe.wait_ge(x_lo_done, g + 4)
                        if n >= 2:
                            pe.wait_ge(h_kept, g - 1)
                        o = half(n % 2, 0)
                        for k in range(KC):
                            at = k % 4 * XQ + (2 * s + k // 4) * V
                            hi, lo = x_hi[:, par, at:at + P], x_lo[:, par, at:at + P]
                            mm = three(pe, o, hi, lo, w_tok[:, 0, k, :], w_tok[:, 1, k, :], k == 0, k == KC - 1)
                        mm.then_inc(h_made, 1)
                    if 4 <= n < TILES + 4:
                        t = g - 4
                        pe.wait_ge(xn_made, t + 1)
                        if n >= 6:
                            pe.wait_ge(xnT_lo_made, t - 1)
                        for d in range(DC):
                            mm = pe.transpose(half((2, 7)[n % 2], 0)[:, d * P:d * P + P], xn32[:, n % 4, d * P:d * P + P],
                                              ident[:, :])
                        mm.then_inc(xn_turned, 1)
                    if 5 <= n < TILES + 5:
                        t = g - 5
                        pe.wait_ge(xnT_hi_made, t + 1)
                        pe.wait_ge(xnT_lo_made, t + 1)
                        if n >= 7:
                            pe.wait_ge(k2_made, t - 1)
                        o = half((3, 6)[(n - 5) % 2], 0)
                        for d in range(DC):
                            hi, lo = [xnT[:, x, d, ds((i - 5) * P, P)] for x in range(2)]
                            three(pe, o, hi, lo, w_k[:, 0, d, :], w_k[:, 1, d, :], d == 0, False)
                        pe.matmul(o, first2[:, :], row_k[:, :], start=False, stop=True).then_inc(k_made, 1)
                    if n >= 6:
                        t, s, r = g - 6, (n - 6) % 2, (n - 6) % 8
                        pe.wait_ge(k2_hi_made, t + 1)
                        pe.wait_ge(k2_lo_made, t + 1)
                        for c in range(DC):
                            hi, lo = [k[:, s, c * P:c * P + P] for k in (k2_hi, k2_lo)]
                            mm = three(pe, bank[4 + c][:, 0:D + 1], hi, lo, xn_hi[:, r, 0:D + 1], xn_lo[:, r, 0:D + 1],
                                       False, n == TILES + 5, free=True)
                        mm.then_inc(kx_added, 1)
                run(pe, step_a, LAST_A)
                all_meet(pe, 3 + 4 * b)

                def queries(first, before):
                    pe.wait_ge(q2_made, before)
                    for f in range(DC):
                        for d in range(DC):
                            hi, lo = [xnT[:, x, d, ds(first * P, CT)] for x in range(2)]
                            w_hi, w_lo = [w_q[:, x, d, f * P:f * P + P] for x in range(2)]
                            mm = three(pe, bank[6 + f][:, :], w_hi, w_lo, hi, lo, d == 0, d == 1)
                    mm.then_inc(q_made, 1)

                queries(0, b * CHUNKS)
                pe.wait_ge(kx_kept, b + 1)
                for c in range(DC):
                    for d in range(DC):
                        mm = pe.transpose(bank[0][:, d * D + c * P:d * D + c * P + P], kxs[:, c, d * P:d * P + P],
                                          ident[:, :])
                mm.then_inc(kx_turned, 1)
                for c in range(DC):
                    mm = pe.matmul(bank[2][:, 2 * c:2 * c + 2], k4acc[:, c * P:c * P + P], ones32[:, :], start=True, stop=True)
                mm.then_inc(norms_made, 1)
                pe.wait_ge(kxT_kept, b + 1)
                for c in range(DC):
                    for d in range(DC):
                        mm = pe.matmul(half(1, c), kxT[:, d * D + c * P:d * D + c * P + P], w_vo32[:, d, :],
                                       start=d == 0, stop=d == 1)
                mm.then_inc(m_summed, 1)
                pe.wait_ge(m_ready, b + 1)

                def step_b(i, n):
                    g = b * TILES + i
                    if n < TILES:
                        s, u = n % 4, n % 2
                        if s == 0 and n + 4 < TILES:
                            queries(i + 4, step_chunk(b, i) + 1)
                        if s == 0:
                            pe.wait_ge(q2_split, step_chunk(b, i) + 1)
                            pe.wait_ge(q4_split, step_chunk(b, i) + 1)
                        if n >= 2:
                            pe.wait_ge(p2_used, g - 1)
                        o = bank[1 + u][:, 0:D + 2]
                        for c in range(DC):
                            hi, lo = [q[:, c, s * P:s * P + P] for q in (q2_hi, q2_lo)]
                            three(pe, o, hi, lo, m_at[:, 0, c, :], m_at[:, 1, c, :], c == 0, c == 1)
                        if n >= 11 and s == 3:
                            ranks(b, i, u)
                        o = bank[1 + u][:, 260:262]
                        pe.matmul(o, q4_hi[:, s * P:s * P + P], ones_r[:, :], start=True, stop=False)
                        pe.matmul(o, q4_lo[:, s * P:s * P + P], ones_r[:, :], start=False, stop=True).then_inc(p2_made, 1)
                        if n >= 2:
                            pe.wait_ge(p1_used, g - 1)
                        o = half(3 * u, 0)
                        for d in range(DC):
                            hi, lo = [xnT[:, x, d, ds(i * P, P)] for x in range(2)]
                            three(pe, o, hi, lo, w_vo[:, 0, d, :], w_vo[:, 1, d, :], d == 0, False)
                        pe.matmul(o, first2[:, :], row_o[:, :], start=False, stop=True).then_inc(p1_made, 1)
                    if 5 <= n < TILES + 5:
                        t, s = g - 5, (n - 5) % 2
                        pe.wait_ge(xn2_hi_made, t + 1)
                        pe.wait_ge(xn2_lo_made, t + 1)
                        if n >= 6:
                            pe.wait_ge(xn2T_made, t)
                        o = half(4, 0).bitcast(F16)
                        for x in range(4):
                            mm = pe.transpose(o[:, x * P:x * P + P], xn2[:, (n - 5) % 8, x * P:x * P + P], ident16[:, :])
                        mm.then_inc(xn2_turned, 1)
                    if 6 <= n < TILES + 6:
                        t, s, r = g - 6, (n - 6) % 2, (n - 6) % 4
                        pe.wait_ge(xn2T_made, t + 1)
                        if n >= 7:
                            pe.wait_ge(logits_read, t)
                        o = bank[5][:, E * r:E * r + E]
                        for d in range(DC):
                            hi, lo = [xn2T[:, s, (2 * x + d) * P:(2 * x + d) * P + P] for x in range(2)]
                            mm = three(pe, o, hi, lo, w_r[:, 0, d, :], w_r[:, 1, d, :], d == 0, d == 1)
                        mm.then_inc(logits_made, 1)
                    if n >= TILES and n % 4 == 3:
                        pe.wait_ge(p2_used, (b + 1) * TILES)
                        ranks(b, i, n % 2)

                def ranks(b, i, u):
                    pe.wait_ge(sel_made, b * CHUNKS + (i - 11) // 4 + 1)
                    o = bank[1 + u][:, 264:264 + 4 * E]
                    pe.matmul(o, earlier[:, :], sel[:].rearrange("p t e -> p (t e)"), start=True, stop=False)
                    pe.matmul(o, ones16[:, :], before[:, 0:4, :].rearrange("p t e -> p (t e)"), start=False, stop=True)\
                      .then_inc(ranks_made, 1)

                def step_chunk(b, i):
                    return b * CHUNKS + i // 4

                run(pe, step_b, LAST_B, TILES - 8)
                pe.wait_ge(sel_made, (b + 1) * CHUNKS)
                pe.matmul(bank[5][:, 0:E], ones16[:, :], before[:, 4, :], start=True, stop=True).then_inc(counts_made, 1)
                all_meet(pe, 4 + 4 * b)

                pe.wait_ge(blocks_made, b + 1)

                def turn(i, n):
                    if n >= UC or not isinstance(i, int):
                        pe.wait_ge(xT_made, b * NBLOCKS + i)
                    elif n >= 1:
                        pe.wait_ge(xT_made, b * NBLOCKS + i)
                    pe.wait_ge(xg_in[n % UC], 32 * (b * (NBLOCKS // UC) + i // UC) + 32 if isinstance(i, int)
                               else 32 * (b * (NBLOCKS // UC)) + 32 + i // UC * 32)
                    o = bank[0][:, :].bitcast(F16)
                    for hh in range(2):
                        for x in range(4):
                            mm = pe.transpose(o[:, x * BLOCK + hh * P:x * BLOCK + hh * P + P],
                                              xg[n % UC][:, hh, x * P:x * P + P], ident16[:, :])
                    mm.then_inc(xg_turned, 1)

                def up(i, n):
                    s = n % UC
                    e = pe.value_load(blk_e[0:1, ds(i, 1)], min_val=0, max_val=E - 1)
                    pe.wait_ge(xT_made, b * NBLOCKS + i + 1)
                    if n >= UC:
                        pe.wait_ge(gelu_made, b * NBLOCKS + i - UC + 1)
                    for f in range(DC):
                        for d in range(DC):
                            w_hi, w_lo = [w_1[:, x, ds(e, 1), d, f * P:f * P + P].rearrange("p o n -> p (o n)")
                                          for x in range(2)]
                            mm = three(pe, half(1 + s, f), w_hi, w_lo, xT[s][:, d, :], xT[s][:, 2 + d, :],
                                       d == 0, d == 1)
                    mm.then_inc(up_made, 1)

                def down(i, n):
                    s = n % UC
                    e = pe.value_load(blk_e[0:1, ds(i, 1)], min_val=0, max_val=E - 1)
                    pe.wait_ge(g_split, b * NBLOCKS + i + 1)
                    if n >= UC:
                        pe.wait_ge(y_made, b * NBLOCKS + i - UC + 1)
                    for hh in range(2):
                        o = half(4 + s, hh)
                        for f in range(DC):
                            hi, lo = [x[s][:, f * BLOCK + hh * P:f * BLOCK + hh * P + P] for x in (g_hi, g_lo)]
                            w_hi, w_lo = [w_2[:, x, ds(e, 1), f, :].rearrange("p o n -> p (o n)") for x in range(2)]
                            three(pe, o, hi, lo, w_hi, w_lo, f == 0, False)
                        mm = pe.matmul(o, first2[:, :], row_2[:, ds(e, 1), :].rearrange("p o n -> p (o n)"),
                                       start=False, stop=True)
                    mm.then_inc(down_made, 1)

                def step_c(i, n):
                    if n < NBLOCKS:
                        turn(i, n)
                    if 1 <= n <= NBLOCKS:
                        up(i - 1, n - 1)
                    if n >= 2:
                        down(i - 2, n - 2)
                run_c(pe, step_c, NBLOCKS + 2)
                all_meet(pe, 5 + 4 * b)
                all_meet(pe, 6 + 4 * b)

        @block.scalar
        def _(act):
            act.wait_ge(loaded, 16 * SETUP_LOADS)
            for k in range(KC):
                act.wait_ge(w_made, k // 2 + 1)
                ins = act.activation(w_tok[:, 0, k, :], half(k // 2, k % 2), ACT.Copy)
                if k % 2:
                    ins.then_inc(w_kept, 1)
            act.wait_ge(w_made, KC // 2 + 2)
            act.activation(w_vo32[:], bank[4][:, :].rearrange("p (c n) -> p c n", c=DC), ACT.Copy)
            act.activation(bvo[:], half(5, 0), ACT.Copy).then_inc(w_kept, 1)
            act.wait_ge(loaded2, 32)
            act.activation(w_1[:, 0], h[:, 0:16, :].rearrange("p (e c) d -> p e c d", e=E), ACT.Copy, scale=WS)\
               .then_inc(w_kept, 1)
            act.activation(w_2[:, 0], h[:, 16:32, :].rearrange("p (e c) d -> p e c d", e=E), ACT.Copy, scale=WS)\
               .then_inc(w_kept, 1)
            all_meet(act, 1)
            for q in range(4):
                act.wait_ge(x_in[q], 16)
                act.activation(x_hi[:, 0, q * XQ:(q + 1) * XQ], x_raw[:, q, :], ACT.Copy).then_inc(x_hi_done, 1)
            all_meet(act, 2)

            with act.Fori(0, B) as b:
                def step_a(i, n):
                    g = b * TILES + i
                    if n < TILES:
                        q, par = n % 4, n // 4 % 2
                        act.wait_ge(x_in[q], quarter_in(b, i, n))
                        act.wait_ge(h_made, g - q)
                        act.activation(x_hi[:, 1 - par, q * XQ:(q + 1) * XQ], x_raw[:, q, :], ACT.Copy)\
                           .then_inc(x_hi_done, 1)
                    if 4 <= n < TILES + 4:
                        t = g - 4
                        act.wait_ge(xn_turned, t + 1)
                        act.activation(xnT[:, 0, :, ds((i - 4) * P, P)],
                                       half((2, 7)[n % 2], 0).rearrange("p (c t) -> p c t", c=DC), ACT.Copy).then_inc(xnT_hi_made, 1)
                    if n < TILES:
                        act.wait_ge(h_made, g + 1)
                        act.activation(h[:, ds(i, 1), :].rearrange("p o d -> p (o d)"), half(n % 2, 0), ACT.Copy)\
                           .then_inc(h_kept, 1)
                    if 5 <= n < TILES + 5:
                        t, s = g - 5, (n - 5) % 2
                        act.wait_ge(k_made, t + 1)
                        if n >= 7:
                            act.wait_ge(k2_lo_made, t - 1)
                        act.activation(k2[:, s, :], half((3, 6)[s], 0), ACT.Square, scale=1.0 / WS, accum_out=k2s[:, s:s + 1])\
                           .then_inc(k2_made, 1)
                        act.wait_ge(k_scaled, t + 1)
                        if n >= 7:
                            act.wait_ge(kx_added, t - 1)
                        act.activation(k2_hi[:, s, :], k2[:, s, :], ACT.Copy, scale=k_scale[:, s:s + 1]).then_inc(k2_hi_made, 1)
                        if n >= 7:
                            act.wait_ge(k4_added, t - 1)
                        act.activation(k4[:, s, :], k2[:, s, :], ACT.Square, scale=k_scale[:, s:s + 1]).then_inc(k4_made, 1)
                    if n % 4 == 3 and n < TILES:
                        act.wait_ge(var_made, chunk_of(b, i, n) + 1)
                        act.activation(sd[:, :], mv[:, :, 1], ACT.Sqrt, bias=eps_ln[:, 0:1]).then_inc(sd_made, 1)
                        for s in range(4):
                            act.wait_ge(xn_made, g - 3 + s + 1)
                            if n >= 8:
                                act.wait_ge(kx_added, g - 3 + s - 7)
                            act.activation(xn_hi[:, (n - 3 + s) % 8, 0:D], xn32[:, s, :], ACT.Copy).then_inc(xn_hi_made, 1)
                run(act, step_a, LAST_A)
                all_meet(act, 3 + 4 * b)

                def squares(G, c):
                    act.wait_ge(q_made, G + 1)
                    for f in range(DC):
                        ins = act.activation(q2[:, f, :], bank[6 + f][:, :], ACT.Square, scale=1.0 / WS, bias=col_q[:, f:f + 1])
                    ins.then_inc(q2_made, 1)
                    act.drain()
                    act.activation(q4[:].rearrange("p c t -> p (c t)"), q2[:].rearrange("p c t -> p (c t)"), ACT.Square)\
                       .then_inc(q4_made, 1)

                def high_parts(G):
                    act.wait_ge(p2_made, G * 4)
                    act.activation(q2_hi, q2[:], ACT.Copy).then_inc(q4_hi_made, 1)
                    act.wait_ge(q4_summed, G + 1)
                    act.activation(q4_hi, q4s[:], ACT.Copy).then_inc(q4_hi_made, 1)

                squares(b * CHUNKS, 0)
                act.wait_ge(kx_turned, b + 1)
                act.activation(kxT[:], bank[0][:, :], ACT.Copy).then_inc(kxT_kept, 1)
                act.wait_ge(norms_made, b + 1)
                act.activation(minv[:, 0, :], bank[2][:, 0:4:2], ACT.Sqrt).then_inc(norms_rooted, 1)
                high_parts(b * CHUNKS)

                def step_b(i, n):
                    g = b * TILES + i
                    if n < TILES:
                        u = n % 2
                        act.wait_ge(p2_made, g + 1)
                        if n >= 2:
                            act.wait_ge(p2_used, g - 1)
                        act.activation(q_n[:, u:u + 1], bank[1 + u][:, 260:261], ACT.Sqrt).then_inc(q_rooted, 1)
                        if n % 4 == 3 and n + 4 < TILES + 0:
                            squares(chunk_of(b, i, n) + 1, 0)
                            high_parts(chunk_of(b, i, n) + 1)
                    if 5 <= n < TILES + 5:
                        t, s = g - 5, (n - 5) % 2
                        act.wait_ge(xn2_turned, t + 1)
                        if n >= 7:
                            act.wait_ge(logits_made, t - 1)
                        act.activation(xn2T[:, s, :], half(4, 0).bitcast(F16), ACT.Copy).then_inc(xn2T_made, 1)
                    if n % 4 == 3 and n < TILES:
                        act.wait_ge(var2_made, chunk_of(b, i, n) + 1)
                        act.activation(sd[:, :], mv[:, :, 1], ACT.Sqrt, bias=eps_ln[:, 0:1]).then_inc(sd2_made, 1)
                        for s in range(4):
                            act.wait_ge(xn2_made, g - 3 + s + 1)
                            if n >= 8:
                                act.wait_ge(xn2_stored[(n - 3 + s) % 8], stored_before(b, i, n))
                                act.wait_ge(xn2_turned, g - 3 + s - 7)
                            act.activation(xn2[:, (n - 3 + s) % 8, 0:D], xn2_32[:, s, :], ACT.Copy).then_inc(xn2_hi_made, 1)
                run(act, step_b, LAST_B, TILES - 8)
                all_meet(act, 4 + 4 * b)

                act.activation(gate[:, 0, :], gap[:, :], ACT.Exp, scale=-1.0 / WS).then_inc(exp_made, 1)
                act.wait_ge(blocks_made, b + 1)
                settled(act)

                def step_c(i, n):
                    if n < NBLOCKS:
                        s = n % UC
                        e = act.value_load(blk_e[0:1, ds(i, 1)], min_val=0, max_val=E - 1)
                        act.wait_ge(up_made, b * NBLOCKS + i + 1)
                        if n >= UC:
                            act.wait_ge(y_stored[s], 16 * (b * (NBLOCKS // UC)) + 16 * (i // UC))
                        for f in range(DC):
                            ins = act.activation(g32[s][:, f * BLOCK:f * BLOCK + BLOCK], half(1 + s, f), ACT.Gelu,
                                                 scale=1.0 / WS,
                                                 bias=col_1[:, ds(e, 1), f:f + 1].rearrange("p o n -> p (o n)"))
                        ins.then_inc(gelu_made, 1)
                    if n >= 1:
                        s = (n - 1) % UC
                        act.wait_ge(down_made, b * NBLOCKS + i - 1 + 1)
                        act.activation(g32[s][:, :], bank[4 + s][:, :], ACT.Copy, scale=1.0 / WS).then_inc(y_made, 1)
                run_c(act, step_c, NBLOCKS + 1)
                all_meet(act, 5 + 4 * b)
                all_meet(act, 6 + 4 * b)

        @block.vector
        def _(dve):
            f_c = xnT[:].rearrange("p a c t -> p (a c t)").bitcast(F32)
            coef = x_raw[:, 0, 128:256]
            pair = x_raw[:, 0, 256:320]
            dve.memset(ones_r[:, :].bitcast(F32), 1.0)
            dve.memset(ones32[:, :], 1.0)
            dve.memset(ones16[:, :], 1.0)
            dve.memset(zeros[:, :], 0.0)
            dve.memset(eps_ln[:, :], EPS_LN)
            dve.memset(m_at[:, 0, :, D:D + 1].bitcast(F32), 1.0)
            dve.memset(m_at[:, 0, :, D + 1:D + 2].bitcast(F32), 0.0)
            dve.memset(m_at[:, 1, :, D:D + 2].bitcast(F32), 0.0)
            dve.drain()
            dve.wait_ge(loaded, 16 * SETUP_LOADS)
            bv_col = scr[:, 5648:5652]
            for c in range(DC):
                dve.tensor_copy(x_raw[:, 2, c * P:c * P + P], bv_col[:, 2 + c:3 + c].to_broadcast([P, P]))
            dve.tensor_tensor(f_c.rearrange("p (n c) -> p n c", c=C),
                              coef.unsqueeze(2).to_broadcast([P, P, C]),
                              pair.unsqueeze(1).to_broadcast([P, P, C]), ALU.mult).then_inc(coef_made, 1)
            dve.tensor_copy(ident16[:, :], ident[:, :])
            dve.tensor_copy(earlier[:, :], x_raw[:, 0, 0:P])
            dve.tensor_scalar(first2[:, :], ones16[:, :], pick[:, 0:1], None, ALU.mult)
            dve.drain()
            dve.scalar_tensor_tensor(out=first2[:, :], in0=ones16[:, :], scalar=pick[:, 1:2], in1=first2[:, :],
                                     op0=ALU.mult, op1=ALU.add)
            w_qkv = scr[:, 2048:3584].rearrange("p (c n) -> p c n", c=DC)
            w_r32 = scr[:, 4608:4624].rearrange("p (c n) -> p c n", c=DC)
            b_qkv = scr[:, 4624:5392]
            b_out = scr[:, 5392:5648]
            means = r_tmp[:].rearrange("p a b -> p (a b)")
            tmp = x_raw[:, 1, 0:D]

            for x in range(2):
                for c in range(DC):
                    dve.tensor_reduce(means[:, 2 * x + c:2 * x + c + 1], w_qkv[:, c, x * D:x * D + D], AX.X, ALU.add)
                dve.tensor_reduce(means[:, 4 + x:5 + x], b_qkv[:, x * D:x * D + D], AX.X, ALU.add)
            dve.drain()
            dve.tensor_scalar(means[:, 0:6], means[:, 0:6], 1.0 / D, None, ALU.mult)
            dve.drain()
            for x, w in ((0, w_q), (1, w_k)):
                for c in range(DC):
                    dve.tensor_scalar(w_qkv[:, c, x * D:x * D + D], w_qkv[:, c, x * D:x * D + D],
                                      means[:, 2 * x + c:2 * x + c + 1], WS, ALU.subtract, ALU.mult)
            dve.tensor_scalar(w_r32, w_r32, WS, None, ALU.mult)
            dve.tensor_scalar(b_qkv[:, D:2 * D], b_qkv[:, D:2 * D], means[:, 5:6], WS, ALU.subtract, ALU.mult)
            dve.tensor_scalar(col_q[:, :], bv_col[:, 0:2], means[:, 4:5], None, ALU.subtract)
            dve.drain()

            def split(hi, lo, x):
                dve.drain()
                dve.tensor_copy(hi, x)
                dve.drain()
                dve.tensor_tensor(lo, x, hi, ALU.subtract)

            def rows(o, x, hi, lo):
                split(hi, lo, x)
                dve.drain()
                dve.tensor_scalar(o, hi, pick[:, 0:1], None, ALU.mult)
                dve.drain()
                dve.scalar_tensor_tensor(out=o, in0=lo, scalar=pick[:, 1:2], in1=o, op0=ALU.mult, op1=ALU.add)
            split(w_q[:, 0], w_q[:, 1], w_qkv[:, :, 0:D])
            split(w_k[:, 0], w_k[:, 1], w_qkv[:, :, D:2 * D])
            split(w_r[:, 0], w_r[:, 1], w_r32)
            hi16, lo16 = [x_raw[:, 3, 128 * x:128 * x + 128].bitcast(F16) for x in range(2)]
            rows(row_k[:, :], b_qkv[:, D:2 * D], hi16, lo16)
            for k in range(KC):
                dve.wait_ge(w_kept, k // 2 + 1)
                dve.tensor_tensor(w_tok[:, 1, k, :], half(k // 2, k % 2), w_tok[:, 0, k, :].bitcast(F32), ALU.subtract)
            dve.wait_ge(w_kept, KC // 2 + 1)
            dve.drain()
            dve.tensor_scalar(scr[:, 3072:3584], w_vo32[:].rearrange("p c n -> p (c n)"), WS, None, ALU.mult)
            dve.tensor_tensor(tmp, bvo[:, :], b_out, ALU.add)
            dve.drain()
            dve.tensor_scalar(tmp, tmp, WS, None, ALU.mult)
            dve.drain()
            split(w_vo[:, 0], w_vo[:, 1], scr[:, 3072:3584].rearrange("p (c n) -> p c n", c=DC))
            rows(row_o[:, :], tmp, hi16, lo16)
            for x, w in ((0, w_1), (1, w_2)):
                dve.wait_ge(w_kept, KC // 2 + 2 + x)
                dve.scalar_tensor_tensor(out=w[:, 1].rearrange("p e c d -> p (e c d)"),
                                         in0=h[:, 16 * x:16 * x + 16, :].rearrange("p t d -> p (t d)"), scalar=WS,
                                         in1=w[:, 0].rearrange("p e c d -> p (e c d)"), op0=ALU.mult, op1=ALU.subtract)
            dve.drain()
            dve.memset(h[:, 8:10, :].bitcast(U32), 0)
            all_meet(dve, 1)
            for q in range(4):
                dve.wait_ge(x_hi_done, q + 1)
                dve.tensor_tensor(x_lo[:, 0, q * XQ:(q + 1) * XQ], x_raw[:, q, :],
                                  x_hi[:, 0, q * XQ:(q + 1) * XQ].bitcast(F32), ALU.subtract).then_inc(x_lo_done, 1)
            dve.wait_ge(loaded2, 64)
            b2 = h[:, 0:8, :].rearrange("p t d -> p (t d)")
            dve.tensor_scalar(b2, b2, WS, None, ALU.mult)
            dve.drain()
            rows(row_2[:].rearrange("p e d -> p (e d)"), b2, h[:, 10:14, :].rearrange("p t d -> p (t d)").bitcast(F16),
                 h[:, 14:18, :].rearrange("p t d -> p (t d)").bitcast(F16))
            all_meet(dve, 2)

            def layernorm(stats_n, sem_var, sem_sd, wait_sd):
                dve.drain()
                for s in range(4):
                    ins = dve.bn_aggr(mv[:, s, :], st[:, s, :])
                ins.then_inc(sem_var, 1)
                dve.wait_ge(sem_sd, wait_sd)
                dve.reciprocal(rstd[:, :], sd[:, :])
                dve.drain()

            with dve.Fori(0, B) as b:
                def step_a(i, n):
                    g = b * TILES + i
                    if 4 <= n < TILES + 4:
                        t = g - 4
                        dve.wait_ge(xnT_hi_made, t + 1)
                        dve.tensor_tensor(xnT[:, 1, :, ds((i - 4) * P, P)],
                                          half((2, 7)[n % 2], 0).rearrange("p (c t) -> p c t", c=DC),
                                          xnT[:, 0, :, ds((i - 4) * P, P)], ALU.subtract).then_inc(xnT_lo_made, 1)
                    if n < TILES:
                        q, par = n % 4, n // 4 % 2
                        dve.wait_ge(x_hi_done, 4 * chunk_of(b, i, n) + 4 + q + 1)
                        dve.tensor_tensor(x_lo[:, 1 - par, q * XQ:(q + 1) * XQ], x_raw[:, q, :],
                                          x_hi[:, 1 - par, q * XQ:(q + 1) * XQ].bitcast(F32), ALU.subtract)\
                           .then_inc(x_lo_done, 1)
                        dve.wait_ge(h_kept, g + 1)
                        dve.bn_stats(st[:, n % 4, :], h[:, ds(i, 1), :].rearrange("p o d -> p (o d)"))
                    if 5 <= n < TILES + 5:
                        t, s = g - 5, (n - 5) % 2
                        dve.wait_ge(k2_made, t + 1)
                        dve.tensor_scalar(k_eps[:, :], k2s[:, s:s + 1], EPS_DIV, 1.0 / KS, ALU.add, ALU.mult)
                        dve.drain()
                        if n >= 7:
                            dve.wait_ge(k4_made, t - 1)
                        dve.reciprocal(k_scale[:, s:s + 1], k_eps[:, :]).then_inc(k_scaled, 1)
                        dve.wait_ge(k2_hi_made, t + 1)
                        dve.scalar_tensor_tensor(out=k2_lo[:, s, :], in0=k2[:, s, :], scalar=k_scale[:, s:s + 1],
                                                 in1=k2_hi[:, s, :], op0=ALU.mult, op1=ALU.subtract).then_inc(k2_lo_made, 1)
                    if n % 4 == 3 and n < TILES:
                        layernorm(n, var_made, sd_made, chunk_of(b, i, n) + 1)
                        for s in range(4):
                            if n >= 4:
                                dve.wait_ge(xn_turned, g - 3 + s - 3)
                                dve.wait_ge(xn_hi_made, g - 3 + s - 3)
                            dve.tensor_scalar(xn32[:, s, :], h[:, ds(i - 3 + s, 1), :].rearrange("p o d -> p (o d)"),
                                              mv[:, s, 0:1], rstd[:, s:s + 1], ALU.subtract, ALU.mult).then_inc(xn_made, 1)
                        for s in range(4):
                            dve.wait_ge(xn_hi_made, g - 3 + s + 1)
                            dve.tensor_tensor(xn_lo[:, (n - 3 + s) % 8, 0:D], xn32[:, s, :], xn_hi[:, (n - 3 + s) % 8, 0:D],
                                              ALU.subtract).then_inc(xn_lo_made, 1)
                dve.memset(xn_hi[:, :, D:D + 1], 1.0)
                dve.memset(xn_lo[:, :, D:D + 1], 0.0)
                run(dve, step_a, LAST_A)
                all_meet(dve, 3 + 4 * b)

                def split_queries(G):
                    dve.wait_ge(q4_hi_made, 2 * G + 1)
                    dve.tensor_tensor(q2_lo, q2[:], q2_hi.bitcast(F32), ALU.subtract).then_inc(q2_split, 1)
                    dve.wait_ge(q4_made, G + 1)
                    dve.tensor_tensor(q4s[:], q4[:, 0, :], q4[:, 1, :], ALU.add).then_inc(q4_summed, 1)
                    dve.wait_ge(q4_hi_made, 2 * G + 2)
                    dve.tensor_tensor(q4_lo, q4s[:], q4_hi.bitcast(F32), ALU.subtract).then_inc(q4_split, 1)

                for c in range(DC):
                    ins = dve.tensor_copy(kxs[:, c, :], bank[4 + c][:, 0:D + 1])
                ins.then_inc(kx_kept, 1)
                dve.memset(before[:, 4, :], 0.0)
                dve.tensor_copy(ids_f[:, :], ids_0[:, :])
                split_queries(b * CHUNKS)
                dve.wait_ge(norms_rooted, b + 1)
                dve.tensor_scalar(minv[:, 1, :], minv[:, 0, :], 1.0 / KS, EPS_NORM, ALU.mult, ALU.max)
                dve.drain()
                dve.reciprocal(minv[:, 0, :], minv[:, 1, :])
                dve.drain()
                dve.tensor_scalar(minv[:, 1, :], minv[:, 0, :], 1.0 / (KS * float(NT) ** 0.5), None, ALU.mult)
                dve.wait_ge(m_summed, b + 1)
                for c in range(DC):
                    dve.scalar_tensor_tensor(out=m32[:, c, :], in0=bvo[:, :], scalar=kxs[:, c, D:D + 1], in1=half(1, c),
                                             op0=ALU.mult, op1=ALU.add)
                dve.drain()
                for c in range(DC):
                    dve.tensor_scalar(m_at[:, 0, c, 0:D], m32[:, c, :], minv[:, 1, c:c + 1], None, ALU.mult)
                dve.drain()
                for c in range(DC):
                    ins = dve.scalar_tensor_tensor(out=m_at[:, 1, c, 0:D], in0=m32[:, c, :], scalar=minv[:, 1, c:c + 1],
                                                   in1=m_at[:, 0, c, 0:D].bitcast(F32), op0=ALU.mult, op1=ALU.subtract)
                ins.then_inc(m_ready, 1)

                def places_at(b, i, u):
                    dve.wait_ge(ranks_made, b * CHUNKS + (i - 11) // 4 + 1)
                    dve.tensor_tensor(pos[:, :, :], bank[1 + u][:, 264:264 + 4 * E].rearrange("p (t e) -> p t e", e=E),
                                      region0[:, :].unsqueeze(1).to_broadcast([P, 4, E]), ALU.add)

                def step_b(i, n):
                    g = b * TILES + i
                    if n < TILES:
                        u = n % 2
                        dve.wait_ge(q_rooted, g + 1)
                        p2 = bank[1 + u]
                        if n >= 11 and n % 4 == 3:
                            places_at(b, i, u)
                        dve.tensor_scalar(r_tmp[:, u, 0:1], p2[:, D:D + 1], EPS_DIV, None, ALU.add)
                        dve.drain()
                        dve.reciprocal(r_tmp[:, u, 1:2], r_tmp[:, u, 0:1])
                        dve.drain()
                        dve.tensor_scalar(r_tmp[:, u, 2:3], q_n[:, u:u + 1], r_tmp[:, u, 1:2], EPS_NORM, ALU.mult, ALU.max)
                        dve.drain()
                        dve.reciprocal(r_tmp[:, u, 3:4], r_tmp[:, u, 2:3])
                        dve.drain()
                        dve.tensor_scalar(r_tmp[:, u, 4:5], r_tmp[:, u, 3:4], r_tmp[:, u, 1:2], None, ALU.mult)
                        dve.drain()
                        hi_ = h[:, ds(i, 1), :].rearrange("p o d -> p (o d)")
                        dve.scalar_tensor_tensor(out=att[:, u, :], in0=p2[:, 0:D], scalar=r_tmp[:, u, 4:5], in1=hi_,
                                                 op0=ALU.mult, op1=ALU.add).then_inc(p2_used, 1)
                        dve.drain()
                        dve.wait_ge(p1_made, g + 1)
                        dve.scalar_tensor_tensor(out=hi_, in0=half(3 * u, 0), scalar=1.0 / WS, in1=att[:, u, :],
                                                 op0=ALU.mult, op1=ALU.add).then_inc(p1_used, 1)
                        dve.drain()
                        dve.bn_stats(st[:, n % 4, :], hi_)
                        if n % 4 == 3 and n + 4 < TILES + 0:
                            split_queries(chunk_of(b, i, n) + 1)
                    if 6 <= n < TILES + 6:
                        t, s = g - 6, (n - 6) % 4
                        dve.wait_ge(logits_made, t + 1)
                        o = bank[5][:, E * s:E * s + E]
                        settled(dve)
                        dve.max(top[:, s, :], o)
                        dve.drain()
                        dve.max_index(top_i[:, s, :], top[:, s, :], o).then_inc(logits_read, 1)
                    if n >= 9 and n % 4 == 1:
                        dve.drain()
                        dve.tensor_tensor(gap[:, ds(i - 9, 4)], top[:, :, 0], top[:, :, 1], ALU.subtract)
                        dve.tensor_copy(e_f[:, :, :], top_i[:, :, 0:2])
                        dve.tensor_copy(e_all[:, ds(i - 9, 4), :], top_i[:, :, 0:2])
                        dve.tensor_copy(before[:, 0, :], before[:, 4, :])
                        dve.drain()
                        dve.tensor_tensor(hot[:].rearrange("p t s e -> p (t s) e"),
                                          iota_e[:, :].unsqueeze(1).to_broadcast([P, 8, E]),
                                          e_f[:].rearrange("p t s -> p (t s)").unsqueeze(2).to_broadcast([P, 8, E]),
                                          ALU.is_equal)
                        dve.drain()
                        dve.tensor_tensor(sel[:, :, :], hot[:, :, 0, :], hot[:, :, 1, :], ALU.add)
                        dve.drain()
                        for s in range(4):
                            ins = dve.tensor_tensor(before[:, s + 1, :], before[:, s, :], sel[:, s, :], ALU.add)
                            if s < 3:
                                dve.drain()
                        ins.then_inc(sel_made, 1)
                    if n >= 11 and n % 4 == 3:
                        G = chunk_of(b, i - 8, n)
                        if n >= TILES:
                            places_at(b, i, n % 2)
                        dve.drain()
                        dve.tensor_tensor(hot_pos[:, :, :, :], hot[:, :, :, :],
                                          pos[:, :, :].unsqueeze(2).to_broadcast([P, 4, 2, E]), ALU.mult)
                        dve.drain()
                        dve.tensor_reduce(slot_f[:, :, :], hot_pos[:, :, :, :], AX.X, ALU.add)
                        dve.drain()
                        dve.wait_ge(ids_stored, 128 * G)
                        dve.tensor_copy(slots[:, ds(i - 11, 4), :], slot_f[:, :, :])
                        dve.tensor_copy(id_u[:, :], ids_f[:, :])
                        dve.tensor_copy(slot_u[:, :, :], slot_f[:, :, :]).then_inc(slots_made, 1)
                        dve.tensor_scalar(ids_f[:, :], ids_f[:, :], float(CT), None, ALU.add)
                    if n % 4 == 3 and n < TILES:
                        layernorm(n, var2_made, sd2_made, chunk_of(b, i, n) + 1)
                        for s in range(4):
                            if n >= 4:
                                dve.wait_ge(xn2_hi_made, g - 3 + s - 3)
                            dve.tensor_scalar(xn2_32[:, s, :], h[:, ds(i - 3 + s, 1), :].rearrange("p o d -> p (o d)"),
                                              mv[:, s, 0:1], rstd[:, s:s + 1], ALU.subtract, ALU.mult).then_inc(xn2_made, 1)
                        for s in range(4):
                            dve.wait_ge(xn2_hi_made, g - 3 + s + 1)
                            dve.tensor_tensor(xn2[:, (n - 3 + s) % 8, D:2 * D], xn2_32[:, s, :], xn2[:, (n - 3 + s) % 8, 0:D],
                                              ALU.subtract).then_inc(xn2_lo_made, 1)
                        dve.tensor_scalar(add_by[:, 0, :], rstd[:, :], 1.0, None, ALU.add)
                        dve.tensor_tensor(add_by[:, 1, :], mv[:, :, 0], rstd[:, :], ALU.mult)
                        dve.drain()
                        for s in range(4):
                            hi_ = h[:, ds(i - 3 + s, 1), :].rearrange("p o d -> p (o d)")
                            dve.tensor_scalar(hi_, hi_, add_by[:, 0, s:s + 1], add_by[:, 1, s:s + 1], ALU.mult, ALU.subtract)
                run(dve, step_b, LAST_B, TILES - 8)
                all_meet(dve, 4 + 4 * b)

                dve.tensor_copy(cnt[:, :], bank[5][:, 0:E])
                dve.drain()
                dve.tensor_tensor(cmp_t[:, :, :], cnt[:, :].unsqueeze(2).to_broadcast([P, E, REGION]),
                                  thr[:, :].unsqueeze(1).to_broadcast([P, E, REGION]), ALU.is_gt)
                dve.drain()
                dve.tensor_reduce(n_blk[:, :], cmp_t[:, :, :], AX.X, ALU.add)
                dve.drain()
                dve.tensor_tensor(cum_m[:, :, :], n_blk[:, :].unsqueeze(1).to_broadcast([P, E, E]), upto[:, :, :], ALU.mult)
                dve.drain()
                dve.tensor_reduce(cum[:, :], cum_m[:, :, :], AX.X, ALU.add)
                dve.drain()
                dve.tensor_tensor(b_cmp[:, :, :], iota_b[:, :].unsqueeze(2).to_broadcast([P, NBLOCKS, E]),
                                  cum[:, :].unsqueeze(1).to_broadcast([P, NBLOCKS, E]), ALU.is_ge)
                dve.drain()
                dve.tensor_tensor(b_cmpn[:, :, :], b_cmp[:, :, :], n_blk[:, :].unsqueeze(1).to_broadcast([P, NBLOCKS, E]),
                                  ALU.mult)
                dve.tensor_reduce(b_e[:, :], b_cmp[:, :, :], AX.X, ALU.add)
                dve.drain()
                dve.tensor_reduce(b_0[:, :], b_cmpn[:, :, :], AX.X, ALU.add)
                dve.tensor_scalar(blk_e[:, :], b_e[:, :], float(E - 1), None, ALU.min)
                dve.drain()
                dve.tensor_tensor(b_at[:, :], iota_b[:, :], b_0[:, :], ALU.subtract)
                dve.drain()
                dve.scalar_tensor_tensor(out=b_0[:, :], in0=b_e[:, :], scalar=float(REGION), in1=b_at[:, :],
                                         op0=ALU.mult, op1=ALU.add)
                dve.drain()
                dve.tensor_copy(blk_at[:, :], b_0[:, :]).then_inc(blocks_made, 1)
                dve.wait_ge(exp_made, b + 1)
                dve.tensor_scalar(gate[:, 2, :], gate[:, 0, :], 1.0, None, ALU.add)
                dve.drain()
                dve.reciprocal(gate[:, 1, :], gate[:, 2, :])
                dve.drain()
                dve.tensor_tensor(gate[:, 2, :], gate[:, 0, :], gate[:, 1, :], ALU.mult)
                dve.tensor_tensor(e_shift[:, :], cum[:, :], n_blk[:, :], ALU.subtract)
                dve.drain()
                dve.scalar_tensor_tensor(out=e_shift[:, :], in0=e_shift[:, :], scalar=float(BLOCK), in1=region0[:, :],
                                         op0=ALU.mult, op1=ALU.subtract)
                is_e, shift = [x_raw[:, x, 0:2 * TILES * E].rearrange("p (t e) -> p t e", e=E) for x in range(2)]
                dve.tensor_tensor(is_e, iota_e[:, :].unsqueeze(1).to_broadcast([P, 2 * TILES, E]),
                                  e_all[:].rearrange("p t s -> p (t s)").unsqueeze(2).to_broadcast([P, 2 * TILES, E]),
                                  ALU.is_equal)
                dve.drain()
                dve.tensor_tensor(shift, is_e, e_shift[:, :].unsqueeze(1).to_broadcast([P, 2 * TILES, E]), ALU.mult)
                dve.drain()
                dve.tensor_reduce(x_raw[:, 2, 0:2 * TILES], shift, AX.X, ALU.add)
                dve.drain()
                dve.tensor_tensor(rows_at[:].rearrange("p t s -> p (t s)"), x_raw[:, 2, 0:2 * TILES],
                                  slots[:].rearrange("p t s -> p (t s)"), ALU.add)

                def step_c(i, n):
                    if n < NBLOCKS:
                        s = n % UC
                        dve.wait_ge(xg_turned, b * NBLOCKS + i + 1)
                        if n >= UC:
                            dve.wait_ge(up_made, b * NBLOCKS + i - UC + 1)
                        dve.tensor_copy(xT[s].rearrange("p c t -> p (c t)"), bank[0][:, :].bitcast(F16)).then_inc(xT_made, 1)
                    if n >= 1:
                        s = (n - 1) % UC
                        dve.wait_ge(gelu_made, b * NBLOCKS + i - 1 + 1)
                        if n >= UC + 1:
                            dve.wait_ge(down_made, b * NBLOCKS + i - 1 - UC + 1)
                        dve.tensor_copy(g_hi[s], g32[s])
                        dve.drain()
                        dve.tensor_tensor(g_lo[s], g32[s], g_hi[s], ALU.subtract).then_inc(g_split, 1)
                run_c(dve, step_c, NBLOCKS + 1)
                all_meet(dve, 5 + 4 * b)

                with dve.Fori(0, CHUNKS) as c:
                    for s in range(4):
                        t = c * 4 + s
                        dve.wait_ge(y_in[s], 32 * (b * CHUNKS + c) + 32)
                        dve.scalar_tensor_tensor(out=mixed[s], in0=yg[s][0], scalar=gate[:, 1, ds(t, 1)],
                                                 in1=h[:, ds(t, 1), :].rearrange("p o d -> p (o d)"), op0=ALU.mult, op1=ALU.add)
                        dve.drain()
                        dve.wait_ge(out_stored[s], 16 * (b * CHUNKS + c))
                        dve.scalar_tensor_tensor(out=summed[s], in0=yg[s][1], scalar=gate[:, 2, ds(t, 1)],
                                                 in1=mixed[s], op0=ALU.mult, op1=ALU.add).then_inc(out_made, 1)
                all_meet(dve, 6 + 4 * b)

        @block.gpsimd
        def _(pool):
            all_meet(pool, 1)
            all_meet(pool, 2)
            with pool.Fori(0, B) as b:
                pool.memset(k4acc[:, :], 0.0)
                pool.drain()

                def step_a(i, n):
                    if 5 <= n < TILES + 5:
                        t = b * TILES + i - 5
                        pool.wait_ge(k4_made, t + 1)
                        settled(pool)
                        pool.tensor_tensor(k4acc[:, :], k4acc[:, :], k4[:, (n - 5) % 2, :], ALU.add).then_inc(k4_added, 1)
                        pool.drain()
                run(pool, step_a, LAST_A)
                all_meet(pool, 3 + 4 * b)

                with pool.Fori(0, CHUNKS) as c:
                    pool.wait_ge(slots_made, b * CHUNKS + c + 1)
                    settled(pool)
                    for s in range(4):
                        for x in range(2):
                            pool.indirect_dma_start(place_ids, bass.IndirectOffsetOnAxis(slot_u[:, s, x:x + 1], 0),
                                                    id_u[:, s:s + 1], None).then_inc(ids_stored, 16)
                pool.wait_ge(ids_stored, 128 * CHUNKS * (b + 1))
                settled(pool)
                all_meet(pool, 4 + 4 * b)

                pool.wait_ge(ids_in, 16 * NBLOCKS * (b + 1))
                settled(pool)
                def gather_blocks(it, first):
                    for n in range(UC):
                        pool.wait_ge(xg_in[n], 32 * (b * (NBLOCKS // UC) + it))
                        settled(pool)
                        pool.tensor_copy(ids_now[:, n, :], ids_all[:, ds(it * UC + n, 1), :].rearrange("p o h -> p (o h)"))\
                            .then_inc(ids_copied, 1)
                        pool.wait_ge(ids_copied, b * NBLOCKS + it * UC + n + 1)
                        settled(pool)
                        if not first:
                            pool.wait_ge(xg_turned, b * NBLOCKS + it * UC + n - UC + 1)
                            settled(pool)
                        for hh in range(2):
                            pool.indirect_dma_start(xg[n][:, hh, :], None, xn2_rows,
                                                    bass.IndirectOffsetOnAxis(ids_now[:, n, hh:hh + 1], 0))\
                                .then_inc(xg_in[n], 16)
                gather_blocks(0, True)
                with pool.Fori(1, NBLOCKS // UC) as it:
                    gather_blocks(it, False)
                all_meet(pool, 5 + 4 * b)

                def gather_results(c, first):
                    for s in range(4):
                        pool.wait_ge(y_in[s], 32 * (b * CHUNKS + c))
                        settled(pool)
                        pool.tensor_copy(slot_now[:, s, :], rows_at[:, ds(c * 4 + s, 1), :].rearrange("p o h -> p (o h)"))\
                            .then_inc(slot_copied, 1)
                        pool.wait_ge(slot_copied, b * TILES + c * 4 + s + 1)
                        settled(pool)
                        if not first:
                            pool.wait_ge(out_made, b * TILES + c * 4 + s - 3)
                            settled(pool)
                        for x in range(2):
                            pool.indirect_dma_start(yg[s][x], None, y_rows,
                                                    bass.IndirectOffsetOnAxis(slot_now[:, s, x:x + 1], 0))\
                                .then_inc(y_in[s], 16)
                gather_results(0, True)
                with pool.Fori(1, CHUNKS) as c:
                    gather_results(c, False)
                all_meet(pool, 6 + 4 * b)


def kernel(x, L0_tok_W, L0_attn_W_qkv, L0_attn_b_qkv, L0_attn_W_out, L0_attn_b_out, L0_ffn_router_w,
           L0_ffn_w1, L0_ffn_b1, L0_ffn_w2, L0_ffn_b2):
    import numpy as np
    import concourse.bacc as bacc
    from concourse.bass_utils import run_bass_kernel_spmd

    def cols(w, n):
        return w.reshape(n, P, -1).transpose(1, 0, 2)

    x = np.asarray(x)
    xp = np.pad(x, ((0, 0), (0, 0), (0, PATCH - STRIDE), (0, 0)), mode="edge")
    steps = 2 * (ROWS - STRIDE // 2)
    chunks = [xp[b, :, c * steps:c * steps + 2 * ROWS, :].reshape(C, ROWS // 4, 4, 2, V)
              .transpose(3, 0, 2, 1, 4).reshape(P, XC)
              for b in range(B) for c in range(CHUNKS)]
    chunks.append(chunks[0])
    w = np.asarray(L0_tok_W).reshape(D, 2, PATCH // 2 + 1, C)
    w_tok = np.stack([w[:, r, f, :].T for r, f in FREQ])
    w_qkv, w_out = np.asarray(L0_attn_W_qkv), np.asarray(L0_attn_W_out)
    b_qkv = np.asarray(L0_attn_b_qkv)
    b_col = b_qkv.reshape(3, DC, P)
    arrays = {
        "x": np.stack(chunks),
        "w_tok": cols(w_tok.reshape(len(FREQ) * C, D), KW),
        "w_qkv": cols(w_qkv, DC),
        "w_out": cols(w_out, DC),
        "w_vT": cols(w_qkv[:, 2 * D:].T, DC),
        "w_r": cols(np.asarray(L0_ffn_router_w).T, DC),
        "b_qkv": np.broadcast_to(b_qkv, (P, 3 * D)),
        "b_out": np.broadcast_to(np.asarray(L0_attn_b_out), (P, D)),
        "b_qv_col": np.concatenate([b_col[0], b_col[2]]).T,
        "b_1": np.asarray(L0_ffn_b1).reshape(E * DC, P).T,
        "b_2": np.broadcast_to(np.asarray(L0_ffn_b2).reshape(1, E, D), (P, E, D)),
        "w_1": np.asarray(L0_ffn_w1).reshape(E, DC, P, D).transpose(2, 0, 1, 3),
        "w_2": np.asarray(L0_ffn_w2).reshape(E, DC, P, D).transpose(2, 0, 1, 3),
    }
    p = np.arange(P)
    coef = np.zeros((P, KW, PATCH))
    for n, (r, f) in enumerate(FREQ):
        angle = 2 * np.pi * ((f * np.arange(PATCH)) % PATCH) / PATCH
        coef[(n % 2) * C:(n % 2 + 1) * C, n // 2] = (-np.sin(angle) if r else np.cos(angle)) / np.sqrt(PATCH)
    e = np.arange(E)
    constants = {
        "ident": np.eye(P),
        "tri": p[:, None] < p[None, :],
        "coef": coef.reshape(P, P),
        "pair": (p[:, None] % C) == np.arange(C)[None, :],
        "pick": p[:, None] == np.arange(2)[None, :],
        "iota_e": np.broadcast_to(e, (P, E)),
        "region0": np.broadcast_to(e * NT, (P, E)),
        "thr": np.broadcast_to(np.arange(REGION) * BLOCK, (P, REGION)),
        "upto": np.broadcast_to(e[None, :] <= e[:, None], (P, E, E)),
        "iota_b": np.broadcast_to(np.arange(NBLOCKS), (P, NBLOCKS)),
        "ids_0": p[:, None] + P * np.arange(CHUNK_TILES)[None, :],
    }
    arrays.update({"c_" + k: np.asarray(v, np.float32) for k, v in constants.items()})
    arrays = {k: np.ascontiguousarray(v) for k, v in arrays.items()}

    nc = bacc.Bacc("TRN2", target_bir_lowering=False, num_devices=1, dynamic_dma_scratch_size=8192)
    ins = {k: nc.dram_tensor(k + "_in", v.shape, F32, kind="ExternalInput").ap() for k, v in arrays.items()}
    out = nc.dram_tensor("out", (B * NT, D), F32, kind="ExternalOutput").ap()
    build(nc, ins, out)
    r = run_bass_kernel_spmd(nc, [{k + "_in": v for k, v in arrays.items()}], core_ids=[0])
    got = r.results[0]["out"]
    return got.reshape(B, NPATCH, V, D).transpose(0, 2, 1, 3).reshape(B, NT, D)
```

```python
from contextlib import ExitStack

import concourse.bass as bass
from concourse import mybir

F32 = mybir.dt.float32
F32R = mybir.dt.float32r
F16 = mybir.dt.float16
U32 = mybir.dt.uint32
ALU = mybir.AluOpType
ACT = mybir.ActivationFunctionType
AX = mybir.AxisListType
ds = bass.ds

P = 128
B, C, T, V = 4, 64, 512, 64
D = 256
E = 8
PATCH, STRIDE = 16, 8
NPATCH = T // STRIDE
NT = V * NPATCH
TILES = NT // P
CHUNK_TILES = 4
CHUNKS = TILES // CHUNK_TILES
CT = CHUNK_TILES * P
KC = C * PATCH // P
ROWS = CT // V * STRIDE // 2 + STRIDE // 2
XC = ROWS * V
XQ = XC // 4
DC = D // P
FREQ = [(0, f) for f in range(PATCH // 2 + 1)] + [(1, f) for f in range(1, PATCH // 2)]
KW = len(FREQ) * C // P

WS = 64.0
KS = 256.0
EPS_LN, EPS_DIV, EPS_NORM = 1e-5, 1e-7, 1e-12

BLOCK = 256
REGION = NT // BLOCK
NBLOCKS = 2 * NT // BLOCK + E - 1
PLACES = (E + 1) * NT
SETUP_LOADS = 20
UC = 3
assert NBLOCKS % UC == 0


def build(nc, a, out):
    ctx = ExitStack()
    with ctx:
        def sb(name, shape, dt):
            return ctx.enter_context(nc.sbuf_tensor(name, shape, dt))

        def sem(name):
            return ctx.enter_context(nc.semaphore(name))

        xn2_rows = nc.dram_tensor("xn2_rows", (NT, 2 * D), F16, kind="Internal").ap()
        place_ids = nc.dram_tensor("place_ids", (PLACES, 1), U32, kind="Internal").ap()
        y_rows = nc.dram_tensor("y_rows", (NBLOCKS * BLOCK, D), F32, kind="Internal").ap()

        w_tok = sb("w_tok", [P, 2, KC, D], F32R)
        w_k = sb("w_k", [P, 2, DC, D], F16)
        w_q = sb("w_q", [P, 2, DC, D], F16)
        w_vo = sb("w_vo", [P, 2, DC, D], F16)
        w_vo32 = sb("w_vo32", [P, DC, D], F32)
        w_r = sb("w_r", [P, 2, DC, E], F16)
        w_1 = sb("w_1", [P, 2, E, DC, D], F16)
        w_2 = sb("w_2", [P, 2, E, DC, D], F16)
        bvo = sb("bvo", [P, D], F32)
        row_k = sb("row_k", [P, D], F16)
        row_o = sb("row_o", [P, D], F16)
        row_2 = sb("row_2", [P, E, D], F16)
        col_q = sb("col_q", [P, DC], F32)
        col_1 = sb("col_1", [P, E, DC], F32)
        m_at = sb("m_at", [P, 2, DC, D], F32R)
        ones_r = sb("ones_r", [P, 2], F32R)
        ones32 = sb("ones32", [P, 2], F32)
        first2 = sb("first2", [P, P], F16)
        zeros = sb("zeros", [P, D + 2], F16)
        ident = sb("ident", [P, P], F32)
        ident16 = sb("ident16", [P, P], F16)
        earlier = sb("earlier", [P, P], F16)
        ones16 = sb("ones16", [P, P], F16)
        pick = sb("pick", [P, 2], F32)
        eps_ln = sb("eps_ln", [P, 1], F32)
        iota_e = sb("iota_e", [P, E], F32)
        region0 = sb("region0", [P, E], F32)
        thr = sb("thr", [P, REGION], F32)
        upto = sb("upto", [P, E, E], F32)
        iota_b = sb("iota_b", [P, NBLOCKS], F32)
        ids_0 = sb("ids_0", [P, CHUNK_TILES], F32)
        ids_f = sb("ids_f", [P, CHUNK_TILES], F32)

        h = sb("h", [P, TILES, D], F32)
        xnT = sb("xnT", [P, 2, DC, NT], F16)
        x_raw = sb("x_raw", [P, 4, XQ], F32)
        x_hi = sb("x_hi", [P, 2, XC], F32R)
        x_lo = sb("x_lo", [P, 2, XC], F32R)
        k4acc = sb("k4acc", [P, D], F32)
        scr = sb("scr", [P, 6144], F32)

        def view(at, words, dt=F32):
            v = scr[:, at:at + words]
            return v if dt == F32 else v.bitcast(dt)

        xn32 = view(0, 1024).rearrange("p (t d) -> p t d", t=4)
        xn_hi = view(1024, 1032, F16).rearrange("p (t d) -> p t d", t=8)
        xn_lo = view(2056, 1032, F16).rearrange("p (t d) -> p t d", t=8)
        k2 = view(3088, 512).rearrange("p (t d) -> p t d", t=2)
        k2_hi = view(3600, 256, F16).rearrange("p (t d) -> p t d", t=2)
        k2_lo = view(3856, 256, F16).rearrange("p (t d) -> p t d", t=2)
        k4 = view(4112, 512).rearrange("p (t d) -> p t d", t=2)
        q2 = view(0, 1024).rearrange("p (c t) -> p c t", c=DC)
        q4 = view(1024, 1024).rearrange("p (c t) -> p c t", c=DC)
        q4s = view(2048, 512)
        xn2_32 = view(2560, 1024).rearrange("p (t d) -> p t d", t=4)
        xn2 = view(3584, 2048, F16).rearrange("p (t d) -> p t d", t=8)
        xn2T = view(5632, 512, F16).rearrange("p (t d) -> p t d", t=2)
        kxs = view(2560, 514).rearrange("p (c d) -> p c d", c=DC)
        kxT = view(3584, 512)
        m32 = view(4096, 512).rearrange("p (c d) -> p c d", c=DC)
        q2_hi = x_hi[:, 1, 0:1024].rearrange("p (c t) -> p c t", c=DC)
        q2_lo = x_lo[:, 1, 0:1024].rearrange("p (c t) -> p c t", c=DC)
        q4_hi = x_hi[:, 1, 1024:1536]
        q4_lo = x_lo[:, 1, 1024:1536]
        xg = [view(512 * n, 512, F16).rearrange("p (h d) -> p h d", h=2) for n in range(UC)]
        xT = [view(1536 + 512 * n, 512, F16).rearrange("p (c t) -> p c t", c=4) for n in range(UC)]
        g32 = [view(3072 + 512 * n, 512) for n in range(UC)]
        g_hi = [view(4608 + 512 * n, 256, F16) for n in range(UC)]
        g_lo = [view(4864 + 512 * n, 256, F16) for n in range(UC)]
        yg = [[view(512 * n + 256 * s, 256) for s in range(2)] for n in range(4)]
        mixed = [view(2048 + 256 * n, 256) for n in range(4)]
        summed = [view(3072 + 256 * n, 256) for n in range(4)]

        st = sb("st", [P, 4, 6], F32)
        mv = sb("mv", [P, 4, 2], F32)
        sd = sb("sd", [P, 4], F32)
        rstd = sb("rstd", [P, 4], F32)
        norm_by = sb("norm_by", [P, 2, 4], F32)
        k2s = sb("k2s", [P, 2], F32)
        k_eps = sb("k_eps", [P, 1], F32)
        k_scale = sb("k_scale", [P, 2], F32)
        q_n = sb("q_n", [P, 4], F32)
        q_guard = sb("q_guard", [P, 4], F32)
        r_q = sb("r_q", [P, 4], F32)
        w_means = sb("w_means", [P, 6], F32)
        att = sb("att", [P, 2, D], F32)
        top = sb("top", [P, 4, 8], F32)
        top_i = sb("top_i", [P, 4, 8], U32)
        gap = sb("gap", [P, TILES], F32)
        e_now = sb("e_now", [P, 4, 2], F32)
        hot = sb("hot", [P, 4, 2, E], F32)
        sel = sb("sel", [P, 4, E], F16)
        chunk_sel = sb("chunk_sel", [P, E], F32)
        before = sb("before", [P, E], F16)
        pos = sb("pos", [P, 4, E], F32)
        hot_pos = sb("hot_pos", [P, 4, 2, E], F32)
        slot_f = sb("slot_f", [P, 4, 2], F32)
        slot_u = sb("slot_u", [P, 4, 2], U32)
        slots = sb("slots", [P, TILES, 2], F32)
        e_all = sb("e_all", [P, TILES, 2], F32)
        rows_at = sb("rows_at", [P, TILES, 2], U32)
        e_shift = sb("e_shift", [P, E], F32)
        id_u = sb("id_u", [P, CHUNK_TILES], U32)
        gate = sb("gate", [P, 3, TILES], F32)
        cnt = sb("cnt", [P, E], F32)
        cmp_t = view(3072, 128).rearrange("p (e r) -> p e r", e=E)
        n_blk = sb("n_blk", [P, E], F32)
        cum_m = view(3200, 64).rearrange("p (e r) -> p e r", e=E)
        cum = sb("cum", [P, E], F32)
        b_cmp = view(3264, 312).rearrange("p (n e) -> p n e", e=E)
        c_cmp = sb("c_cmp", [P, 2, E], F32)
        c_sum = sb("c_sum", [P, 3], F32)
        blk_at = sb("blk_at", [P, 1], U32)
        ids_rows = view(3584, 256, U32)
        ids_rows32 = view(3840, 256)
        b_e = sb("b_e", [P, NBLOCKS], F32)
        blk_e = sb("blk_e", [P, NBLOCKS], U32)
        ids_all = sb("ids_all", [P, NBLOCKS, 2], U32)
        ids_now = sb("ids_now", [P, UC, 2], U32)
        slot_now = sb("slot_now", [P, 4, 2], U32)
        minv = sb("minv", [P, 2, DC], F32)

        bank = [ctx.enter_context(nc.psum_tensor(f"bank{n}", [P, 512], F32)) for n in range(8)]

        def half(n, s):
            return bank[n][:, D * s:D * s + D]

        phase_end, waited = sem("phase_end"), sem("waited")
        coef_made, w_made, w_kept = sem("coef_made"), sem("w_made"), sem("w_kept")
        loaded = sem("loaded")
        loaded2 = sem("loaded2")
        x_in = [sem(f"x_in{q}") for q in range(4)]
        x_hi_done, x_lo_done = sem("x_hi_done"), sem("x_lo_done")
        h_made, h_kept = sem("h_made"), sem("h_kept")
        var_made, sd_made = sem("var_made"), sem("sd_made")
        xn_made, xn_hi_made, xn_lo_made = sem("xn_made"), sem("xn_hi_made"), sem("xn_lo_made")
        xn_turned, xnT_hi_made, xnT_lo_made = sem("xn_turned"), sem("xnT_hi_made"), sem("xnT_lo_made")
        k_made, k2_made, k_scaled = sem("k_made"), sem("k2_made"), sem("k_scaled")
        k2_hi_made, k2_lo_made, k4_made = sem("k2_hi_made"), sem("k2_lo_made"), sem("k4_made")
        k4_added, kx_added = sem("k4_added"), sem("kx_added")
        q_made, q2_made, q4_made, q4_summed = sem("q_made"), sem("q2_made"), sem("q4_made"), sem("q4_summed")
        q2_hi_made, q2_split, q4_hi_made, q4_split = sem("q2_hi_made"), sem("q2_split"), sem("q4_hi_made"), sem("q4_split")
        s4_made = sem("s4_made")
        kx_kept, kx_turned, kxT_kept = sem("kx_kept"), sem("kx_turned"), sem("kxT_kept")
        norms_made, norms_rooted, m_summed, m_ready = (
            sem("norms_made"), sem("norms_rooted"), sem("m_summed"), sem("m_ready"))
        p2_made, p1_made, q_rooted = sem("p2_made"), sem("p1_made"), sem("q_rooted")
        p2_used, p1_used = sem("p2_used"), sem("p1_used")
        var2_made, sd2_made, rstd2_made, h_added = sem("var2_made"), sem("sd2_made"), sem("rstd2_made"), sem("h_added")
        xn2_made, xn2_hi_made, xn2_lo_made = sem("xn2_made"), sem("xn2_hi_made"), sem("xn2_lo_made")
        xn2_stored = [sem(f"xn2_stored{n}") for n in range(8)]
        xn2_turned, xn2T_made, logits_made, logits_read = (
            sem("xn2_turned"), sem("xn2T_made"), sem("logits_made"), sem("logits_read"))
        sel_made, ranks_made, slots_made, ids_stored = (
            sem("sel_made"), sem("ranks_made"), sem("slots_made"), sem("ids_stored"))
        counts_made, exp_made, blocks_made = sem("counts_made"), sem("exp_made"), sem("blocks_made")
        before_made = sem("before_made")
        block_rows_made, ids_in, ids_read, ids_turned, ids_kept = (
            sem("block_rows_made"), sem("ids_in"), sem("ids_read"), sem("ids_turned"), sem("ids_kept"))
        ids_copied = sem("ids_copied")
        xg_in = [sem(f"xg_in{n}") for n in range(UC)]
        xg_turned, xT_made = sem("xg_turned"), sem("xT_made")
        up_made, gelu_made, g_hi_made, g_split = sem("up_made"), sem("gelu_made"), sem("g_hi_made"), sem("g_split")
        down_made, y_made = sem("down_made"), sem("y_made")
        y_stored = [sem(f"y_stored{n}") for n in range(UC)]
        slot_copied = sem("slot_copied")
        y_in = [sem(f"y_in{n}") for n in range(4)]
        out_made = sem("out_made")
        out_stored = [sem(f"out_stored{n}") for n in range(4)]

        def all_meet(eng, k):
            settled(eng)
            eng.drain().then_inc(phase_end, 1)
            eng.wait_ge(phase_end, 5 * k)
            settled(eng)

        def settled(eng):
            eng.sem_inc(waited, 1)

        def three(eng, o, hi, lo, w_hi, w_lo, first, last, free=False):
            eng.matmul(o, hi, w_hi, start=first, stop=False, skip_group_check=free)
            eng.matmul(o, lo, w_hi, start=False, stop=False, skip_group_check=free)
            return eng.matmul(o, hi, w_lo, start=False, stop=last, skip_group_check=free)

        def run(eng, step, last, looped=TILES):
            for n in range(8):
                step(n, n)
            with eng.Fori(1, looped // 8) as it:
                for n in range(8):
                    step(it * 8 + n, 8 + n)
            for n in range(looped, last):
                step(n, n)

        def run_c(eng, step, last):
            for n in range(2 * UC):
                step(n, n)
            with eng.Fori(2, NBLOCKS // UC) as it:
                for n in range(UC):
                    step(it * UC + n, 2 * UC + n)
            for n in range(NBLOCKS, last):
                step(n, n)

        def chunk_of(b, i, n):
            return b * CHUNKS + i // 4

        def quarter_in(b, i, n):
            return 16 * (chunk_of(b, i, n) + 2)

        LAST_A = TILES + 6
        LAST_B = TILES + 8

        block = ctx.enter_context(nc.Block())

        @block.sync
        def _(sp):
            def load(o, i):
                sp.dma_start(o, i).then_inc(loaded, 16)
            for name, t in (("ident", ident), ("pick", pick), ("iota_e", iota_e), ("region0", region0),
                            ("thr", thr), ("upto", upto), ("iota_b", iota_b), ("ids_0", ids_0)):
                load(t[:], a["c_" + name])
            c_tri = x_raw[:, 0, 0:P]
            load(c_tri, a["c_tri"])
            load(x_raw[:, 0, 128:256], a["c_coef"])
            load(x_raw[:, 0, 256:320], a["c_pair"])
            f_rows = x_lo[:, 0, 0:2048].bitcast(F32)
            load(scr[:, 0:2048].rearrange("p (q d) -> p q d", q=KW), a["w_tok"])
            load(scr[:, 2048:3584].rearrange("p (c n) -> p c n", c=DC), a["w_qkv"])
            load(scr[:, 3584:4096].rearrange("p (c n) -> p c n", c=DC), a["w_out"])
            load(scr[:, 4096:4608].rearrange("p (c n) -> p c n", c=DC), a["w_vT"])
            load(scr[:, 4608:4624].rearrange("p (c n) -> p c n", c=DC), a["w_r"])
            load(scr[:, 4624:5392], a["b_qkv"])
            load(scr[:, 5392:5648], a["b_out"])
            load(scr[:, 5648:5652], a["b_qv_col"])
            load(col_1[:].rearrange("p e c -> p (e c)"), a["b_1"])
            sp.dma_start(h[:, 0:16, :].rearrange("p (e c) d -> p e c d", e=E), a["w_1"]).then_inc(loaded2, 16)
            sp.dma_start(h[:, 16:32, :].rearrange("p (e c) d -> p e c d", e=E), a["w_2"]).then_inc(loaded2, 16)
            all_meet(sp, 1)
            sp.dma_start(h[:, 0:8, :], a["b_2"]).then_inc(loaded2, 16)
            sp.dma_start(place_ids.rearrange("(p n) o -> p (n o)", p=P), h[:, 8:10, :].rearrange(
                "p t d -> p (t d)")[:, 0:PLACES // P].bitcast(U32)).then_inc(loaded2, 16)
            for q in range(4):
                sp.dma_start(x_raw[:, q, :], a["x"][0][:, q * XQ:(q + 1) * XQ]).then_inc(x_in[q], 16)
            sp.wait_ge(loaded2, 64)
            all_meet(sp, 2)

            with sp.Fori(0, B) as b:
                with sp.Fori(0, CHUNKS) as c:
                    for q in range(4):
                        sp.wait_ge(x_hi_done, 4 * (b * CHUNKS + c) + q + 1)
                        sp.wait_ge(x_lo_done, 4 * (b * CHUNKS + c) + q + 1)
                        sp.dma_start(x_raw[:, q, :], a["x"][ds(b * CHUNKS + c + 1, 1), :, q * XQ:(q + 1) * XQ]
                                     .rearrange("o p n -> (o p) n")).then_inc(x_in[q], 16)
                all_meet(sp, 3 + 4 * b)

                def store_rows(i, n):
                    sp.wait_ge(xn2_hi_made, b * TILES + i + 1)
                    sp.wait_ge(xn2_lo_made, b * TILES + i + 1)
                    sp.dma_start(xn2_rows[ds(i * P, P), :], xn2[:, n % 8, :])\
                      .then_inc(xn2_stored[n % 8], 16)
                run(sp, store_rows, TILES, TILES - 8)
                for n in range(8):
                    sp.wait_ge(xn2_stored[n], 16 * (TILES // 8) * (b + 1))
                all_meet(sp, 4 + 4 * b)

                with sp.Fori(0, NBLOCKS // UC) as it:
                    for n in range(UC):
                        sp.wait_ge(y_made, b * NBLOCKS + it * UC + n + 1)
                        sp.dma_start(y_rows[ds((it * UC + n) * BLOCK, BLOCK), :].rearrange("(h p) d -> p h d", p=P),
                                     g32[n].rearrange("p (h d) -> p h d", h=2)).then_inc(y_stored[n], 16)
                for n in range(UC):
                    sp.wait_ge(y_stored[n], 16 * (NBLOCKS // UC) * (b + 1))
                all_meet(sp, 5 + 4 * b)

                with sp.Fori(0, CHUNKS) as c:
                    for n in range(4):
                        sp.wait_ge(out_made, b * TILES + c * 4 + n + 1)
                        sp.dma_start(out[ds((b * TILES + c * 4 + n) * P, P), :], summed[n]).then_inc(out_stored[n], 16)
                for n in range(4):
                    sp.wait_ge(out_stored[n], 16 * CHUNKS * (b + 1))
                all_meet(sp, 6 + 4 * b)
            for q in range(4):
                sp.wait_ge(x_in[q], 16 * (B * CHUNKS + 1))

        @block.tensor
        def _(pe):
            f_w = scr[:, 0:2048].rearrange("p (q d) -> p q d", q=KW)
            f_c = xnT[:].rearrange("p a c t -> p (a c t)").bitcast(F32).rearrange(
                "p (q k m) -> p q k m", q=KW, k=KC)
            w_out_f = scr[:, 3584:4096].rearrange("p (c n) -> p c n", c=DC)
            w_vT_f = scr[:, 4096:4608].rearrange("p (c n) -> p c n", c=DC)
            bv_b = x_raw[:, 2, 0:2 * P].rearrange("p (c m) -> p c m", c=DC)
            pe.wait_ge(coef_made, 1)
            for k in range(KC):
                for q in range(KW):
                    mm = pe.matmul(half(k // 2, k % 2), f_c[:, q, k, :], f_w[:, q, :], start=q == 0, stop=q == KW - 1)
                if k % 2:
                    mm.then_inc(w_made, 1)
            for d in range(DC):
                for c in range(DC):
                    mm = pe.matmul(half(4, d), w_vT_f[:, c, d * P:d * P + P], w_out_f[:, c, :], start=c == 0, stop=c == 1)
            mm.then_inc(w_made, 1)
            for c in range(DC):
                mm = pe.matmul(half(5, 0), bv_b[:, c, :], w_out_f[:, c, :], start=c == 0, stop=c == 1)
            mm.then_inc(w_made, 1)
            all_meet(pe, 1)
            all_meet(pe, 2)

            with pe.Fori(0, B) as b:
                for c in range(DC):
                    pe.matmul(bank[4 + c][:, 0:D + 1], zeros[:, 0:P], zeros[:, 0:D + 1], start=True, stop=False,
                              skip_group_check=True)

                def step_a(i, n):
                    g = b * TILES + i
                    if n < TILES:
                        s, par = n % 4, n // 4 % 2
                        if s == 0:
                            pe.wait_ge(x_hi_done, g + 4)
                            pe.wait_ge(x_lo_done, g + 4)
                        if n >= 2:
                            pe.wait_ge(h_kept, g - 1)
                        o = half(n % 2, 0)
                        for k in range(KC):
                            at = k % 4 * XQ + (2 * s + k // 4) * V
                            hi, lo = x_hi[:, par, at:at + P], x_lo[:, par, at:at + P]
                            mm = three(pe, o, hi, lo, w_tok[:, 0, k, :], w_tok[:, 1, k, :], k == 0, k == KC - 1)
                        mm.then_inc(h_made, 1)
                    if 4 <= n < TILES + 4:
                        t = g - 4
                        pe.wait_ge(xn_made, t + 1)
                        if n >= 6:
                            pe.wait_ge(xnT_lo_made, t - 1)
                        for d in range(DC):
                            mm = pe.transpose(half((2, 7)[n % 2], 0)[:, d * P:d * P + P], xn32[:, n % 4, d * P:d * P + P],
                                              ident[:, :])
                        mm.then_inc(xn_turned, 1)
                    if 5 <= n < TILES + 5:
                        t = g - 5
                        pe.wait_ge(xnT_hi_made, t + 1)
                        pe.wait_ge(xnT_lo_made, t + 1)
                        if n >= 7:
                            pe.wait_ge(k2_made, t - 1)
                        o = half((3, 6)[(n - 5) % 2], 0)
                        for d in range(DC):
                            hi, lo = [xnT[:, x, d, ds((i - 5) * P, P)] for x in range(2)]
                            three(pe, o, hi, lo, w_k[:, 0, d, :], w_k[:, 1, d, :], d == 0, False)
                        pe.matmul(o, first2[:, :], row_k[:, :], start=False, stop=True).then_inc(k_made, 1)
                    if n >= 6:
                        t, s, r = g - 6, (n - 6) % 2, (n - 6) % 8
                        pe.wait_ge(k2_hi_made, t + 1)
                        pe.wait_ge(k2_lo_made, t + 1)
                        for c in range(DC):
                            hi, lo = [k[:, s, c * P:c * P + P] for k in (k2_hi, k2_lo)]
                            mm = three(pe, bank[4 + c][:, 0:D + 1], hi, lo, xn_hi[:, r, 0:D + 1], xn_lo[:, r, 0:D + 1],
                                       False, n == TILES + 5, free=True)
                        mm.then_inc(kx_added, 1)
                run(pe, step_a, LAST_A)
                all_meet(pe, 3 + 4 * b)

                def queries(first, before):
                    pe.wait_ge(q2_made, before)
                    for f in range(DC):
                        for d in range(DC):
                            hi, lo = [xnT[:, x, d, ds(first * P, CT)] for x in range(2)]
                            w_hi, w_lo = [w_q[:, x, d, f * P:f * P + P] for x in range(2)]
                            mm = three(pe, bank[6 + f][:, :], w_hi, w_lo, hi, lo, d == 0, d == 1)
                    mm.then_inc(q_made, 1)

                queries(0, b * CHUNKS)
                pe.wait_ge(kx_kept, b + 1)
                for c in range(DC):
                    for d in range(DC):
                        mm = pe.transpose(bank[0][:, d * D + c * P:d * D + c * P + P], kxs[:, c, d * P:d * P + P],
                                          ident[:, :])
                mm.then_inc(kx_turned, 1)
                for c in range(DC):
                    mm = pe.matmul(bank[2][:, 2 * c:2 * c + 2], k4acc[:, c * P:c * P + P], ones32[:, :], start=True, stop=True)
                mm.then_inc(norms_made, 1)
                pe.wait_ge(kxT_kept, b + 1)
                for c in range(DC):
                    for d in range(DC):
                        mm = pe.matmul(half(1, c), kxT[:, d * D + c * P:d * D + c * P + P], w_vo32[:, d, :],
                                       start=d == 0, stop=d == 1)
                mm.then_inc(m_summed, 1)
                pe.wait_ge(m_ready, b + 1)

                def step_b(i, n):
                    g = b * TILES + i
                    if n < TILES:
                        s, u = n % 4, n % 2
                        if s == 0:
                            if n + 4 < TILES:
                                queries(i + 4, step_chunk(b, i) + 1)
                            pe.wait_ge(q4_split, step_chunk(b, i) + 1)
                            if n >= 8:
                                pe.wait_ge(xn2T_made, g - 5)
                            for t in range(4):
                                o = bank[4][:, D + 2 * t:D + 2 * t + 2]
                                pe.matmul(o, q4_hi[:, t * P:t * P + P], ones_r[:, :], start=True, stop=False)
                                mm = pe.matmul(o, q4_lo[:, t * P:t * P + P], ones_r[:, :], start=False, stop=True)
                            mm.then_inc(s4_made, 1)
                            pe.wait_ge(q2_split, step_chunk(b, i) + 1)
                        if n >= 2:
                            pe.wait_ge(p2_used, g - 1)
                        if n >= 11 and s == 3:
                            ranks(b, i, u)
                        o = half(1 + u, 0)
                        for c in range(DC):
                            hi, lo = [q[:, c, s * P:s * P + P] for q in (q2_hi, q2_lo)]
                            mm = three(pe, o, hi, lo, m_at[:, 0, c, :], m_at[:, 1, c, :], c == 0, c == 1)
                        mm.then_inc(p2_made, 1)
                        if n >= 2:
                            pe.wait_ge(p1_used, g - 1)
                        o = half(3 * u, 0)
                        for d in range(DC):
                            hi, lo = [xnT[:, x, d, ds(i * P, P)] for x in range(2)]
                            three(pe, o, hi, lo, w_vo[:, 0, d, :], w_vo[:, 1, d, :], d == 0, False)
                        pe.matmul(o, first2[:, :], row_o[:, :], start=False, stop=True).then_inc(p1_made, 1)
                    if 5 <= n < TILES + 5:
                        t, s = g - 5, (n - 5) % 2
                        pe.wait_ge(xn2_lo_made, t + 1)
                        if n >= 6:
                            pe.wait_ge(xn2T_made, t)
                        if n < TILES and n % 4 == 0:
                            pe.wait_ge(q_rooted, step_chunk(b, i) + 1)
                        o = half(4, 0).bitcast(F16)
                        for x in range(4):
                            mm = pe.transpose(o[:, x * P:x * P + P], xn2[:, (n - 5) % 8, x * P:x * P + P], ident16[:, :])
                        mm.then_inc(xn2_turned, 1)
                    if 6 <= n < TILES + 6:
                        t, s, r = g - 6, (n - 6) % 2, (n - 6) % 4
                        pe.wait_ge(xn2T_made, t + 1)
                        if n >= 10 and r == 0:
                            pe.wait_ge(logits_read, b * CHUNKS + (i - 10) // 4 + 1)
                        o = bank[5][:, E * r:E * r + E]
                        for d in range(DC):
                            hi, lo = [xn2T[:, s, (2 * x + d) * P:(2 * x + d) * P + P] for x in range(2)]
                            mm = three(pe, o, hi, lo, w_r[:, 0, d, :], w_r[:, 1, d, :], d == 0, d == 1)
                        mm.then_inc(logits_made, 1)
                    if n >= TILES and n % 4 == 3:
                        pe.wait_ge(p2_used, (b + 1) * TILES)
                        ranks(b, i, n % 2)

                def ranks(b, i, u):
                    pe.wait_ge(sel_made, b * CHUNKS + (i - 11) // 4 + 1)
                    pe.wait_ge(before_made, b * CHUNKS + (i - 11) // 4)
                    o = bank[1 + u][:, D:D + 4 * E].rearrange("p (t e) -> p t e", e=E)
                    pe.matmul(o, earlier[:, :], sel[:, :, :], start=True, stop=False)
                    for t in range(3):
                        pe.matmul(o[:, t + 1:4, :], ones16[:, :], sel[:, t, :].unsqueeze(1).to_broadcast([P, 3 - t, E]),
                                  start=False, stop=False)
                    pe.matmul(o, ones16[:, :], before[:, :].unsqueeze(1).to_broadcast([P, 4, E]), start=False, stop=True)\
                      .then_inc(ranks_made, 1)

                def step_chunk(b, i):
                    return b * CHUNKS + i // 4

                run(pe, step_b, LAST_B, TILES - 8)
                pe.wait_ge(before_made, (b + 1) * CHUNKS)
                pe.matmul(bank[5][:, 0:E], ones16[:, :], before[:, :], start=True, stop=True).then_inc(counts_made, 1)
                all_meet(pe, 4 + 4 * b)

                pe.wait_ge(ids_read, b + 1)
                for hh in range(2):
                    mm = pe.transpose(bank[7][:, hh * P:hh * P + P], ids_rows32[:, hh * P:hh * P + P], ident[:, :])
                mm.then_inc(ids_turned, 1)
                pe.wait_ge(blocks_made, b + 1)

                def turn(i, n):
                    if n >= UC or not isinstance(i, int):
                        pe.wait_ge(xT_made, b * NBLOCKS + i)
                    elif n >= 1:
                        pe.wait_ge(xT_made, b * NBLOCKS + i)
                    pe.wait_ge(xg_in[n % UC], 32 * (b * (NBLOCKS // UC) + i // UC) + 32 if isinstance(i, int)
                               else 32 * (b * (NBLOCKS // UC)) + 32 + i // UC * 32)
                    o = bank[0][:, :].bitcast(F16)
                    for hh in range(2):
                        for x in range(4):
                            mm = pe.transpose(o[:, x * BLOCK + hh * P:x * BLOCK + hh * P + P],
                                              xg[n % UC][:, hh, x * P:x * P + P], ident16[:, :])
                    mm.then_inc(xg_turned, 1)

                def expert(i):
                    return pe.value_load(blk_e[0:1, ds(i, 1)], min_val=0, max_val=E - 1)

                def up(i, n, e):
                    s = n % UC
                    pe.wait_ge(xT_made, b * NBLOCKS + i + 1)
                    if n >= UC:
                        pe.wait_ge(gelu_made, b * NBLOCKS + i - UC + 1)
                    for f in range(DC):
                        for d in range(DC):
                            w_hi, w_lo = [w_1[:, x, ds(e, 1), d, f * P:f * P + P].rearrange("p o n -> p (o n)")
                                          for x in range(2)]
                            mm = three(pe, half(1 + s, f), w_hi, w_lo, xT[s][:, d, :], xT[s][:, 2 + d, :],
                                       d == 0, d == 1)
                    mm.then_inc(up_made, 1)

                def down(i, n, e):
                    s = n % UC
                    pe.wait_ge(g_split, b * NBLOCKS + i + 1)
                    if n >= UC:
                        pe.wait_ge(y_made, b * NBLOCKS + i - UC + 1)
                    for hh in range(2):
                        o = half(4 + s, hh)
                        for f in range(DC):
                            hi, lo = [x[s][:, f * BLOCK + hh * P:f * BLOCK + hh * P + P] for x in (g_hi, g_lo)]
                            w_hi, w_lo = [w_2[:, x, ds(e, 1), f, :].rearrange("p o n -> p (o n)") for x in range(2)]
                            three(pe, o, hi, lo, w_hi, w_lo, f == 0, False)
                        mm = pe.matmul(o, first2[:, :], row_2[:, ds(e, 1), :].rearrange("p o n -> p (o n)"),
                                       start=False, stop=True)
                    mm.then_inc(down_made, 1)

                def step_c(i, n):
                    e_up = expert(i - 1) if 1 <= n <= NBLOCKS else None
                    e_down = expert(i - 2) if n >= 2 else None
                    if n < NBLOCKS:
                        turn(i, n)
                    if 1 <= n <= NBLOCKS:
                        up(i - 1, n - 1, e_up)
                    if n >= 2:
                        down(i - 2, n - 2, e_down)
                run_c(pe, step_c, NBLOCKS + 2)
                all_meet(pe, 5 + 4 * b)
                all_meet(pe, 6 + 4 * b)

        @block.scalar
        def _(act):
            act.wait_ge(loaded, 16 * SETUP_LOADS)
            for k in range(KC):
                act.wait_ge(w_made, k // 2 + 1)
                ins = act.activation(w_tok[:, 0, k, :], half(k // 2, k % 2), ACT.Copy)
                if k % 2:
                    ins.then_inc(w_kept, 1)
            act.wait_ge(w_made, KC // 2 + 2)
            act.activation(w_vo32[:], bank[4][:, :].rearrange("p (c n) -> p c n", c=DC), ACT.Copy)
            act.activation(bvo[:], half(5, 0), ACT.Copy).then_inc(w_kept, 1)
            act.wait_ge(loaded2, 32)
            act.activation(w_1[:, 0], h[:, 0:16, :].rearrange("p (e c) d -> p e c d", e=E), ACT.Copy, scale=WS)\
               .then_inc(w_kept, 1)
            act.activation(w_2[:, 0], h[:, 16:32, :].rearrange("p (e c) d -> p e c d", e=E), ACT.Copy, scale=WS)\
               .then_inc(w_kept, 1)
            all_meet(act, 1)
            for q in range(4):
                act.wait_ge(x_in[q], 16)
                act.activation(x_hi[:, 0, q * XQ:(q + 1) * XQ], x_raw[:, q, :], ACT.Copy).then_inc(x_hi_done, 1)
            all_meet(act, 2)

            with act.Fori(0, B) as b:
                def step_a(i, n):
                    g = b * TILES + i
                    if n < TILES:
                        q, par = n % 4, n // 4 % 2
                        act.wait_ge(x_in[q], quarter_in(b, i, n))
                        act.wait_ge(h_made, g - q)
                        act.activation(x_hi[:, 1 - par, q * XQ:(q + 1) * XQ], x_raw[:, q, :], ACT.Copy)\
                           .then_inc(x_hi_done, 1)
                    if 4 <= n < TILES + 4:
                        t = g - 4
                        act.wait_ge(xn_turned, t + 1)
                        act.activation(xnT[:, 0, :, ds((i - 4) * P, P)],
                                       half((2, 7)[n % 2], 0).rearrange("p (c t) -> p c t", c=DC), ACT.Copy).then_inc(xnT_hi_made, 1)
                    if n < TILES:
                        act.wait_ge(h_made, g + 1)
                        act.activation(h[:, ds(i, 1), :].rearrange("p o d -> p (o d)"), half(n % 2, 0), ACT.Copy)\
                           .then_inc(h_kept, 1)
                    if 5 <= n < TILES + 5:
                        t, s = g - 5, (n - 5) % 2
                        act.wait_ge(k_made, t + 1)
                        if n >= 7:
                            act.wait_ge(k2_lo_made, t - 1)
                        act.activation(k2[:, s, :], half((3, 6)[s], 0), ACT.Square, scale=1.0 / WS, accum_out=k2s[:, s:s + 1])\
                           .then_inc(k2_made, 1)
                        act.wait_ge(k_scaled, t + 1)
                        if n >= 7:
                            act.wait_ge(kx_added, t - 1)
                        act.activation(k2_hi[:, s, :], k2[:, s, :], ACT.Copy, scale=k_scale[:, s:s + 1]).then_inc(k2_hi_made, 1)
                        if n >= 7:
                            act.wait_ge(k4_added, t - 1)
                        act.activation(k4[:, s, :], k2[:, s, :], ACT.Square, scale=k_scale[:, s:s + 1]).then_inc(k4_made, 1)
                    if n % 4 == 3 and n < TILES:
                        act.wait_ge(var_made, chunk_of(b, i, n) + 1)
                        act.activation(sd[:, :], mv[:, :, 1], ACT.Sqrt, bias=eps_ln[:, 0:1]).then_inc(sd_made, 1)
                        for s in range(4):
                            act.wait_ge(xn_made, g - 3 + s + 1)
                            if n >= 8:
                                act.wait_ge(kx_added, g - 3 + s - 7)
                            act.activation(xn_hi[:, (n - 3 + s) % 8, 0:D], xn32[:, s, :], ACT.Copy).then_inc(xn_hi_made, 1)
                run(act, step_a, LAST_A)
                all_meet(act, 3 + 4 * b)

                def squares(G):
                    act.wait_ge(q_made, G + 1)
                    act.wait_ge(q2_split, G)
                    for f in range(DC):
                        ins = act.activation(q2[:, f, :], bank[6 + f][:, :], ACT.Square, scale=1.0 / WS, bias=col_q[:, f:f + 1])
                    ins.then_inc(q2_made, 1)
                    act.wait_ge(q2_made, G + 1)
                    act.activation(q4[:].rearrange("p c t -> p (c t)"), q2[:].rearrange("p c t -> p (c t)"), ACT.Square)\
                       .then_inc(q4_made, 1)

                def q4_high(G):
                    act.wait_ge(s4_made, G)
                    act.wait_ge(q4_summed, G + 1)
                    act.activation(q4_hi, q4s[:], ACT.Copy).then_inc(q4_hi_made, 1)

                def q2_high(G):
                    act.wait_ge(p2_made, G * 4)
                    act.activation(q2_hi, q2[:], ACT.Copy).then_inc(q2_hi_made, 1)

                squares(b * CHUNKS)
                act.wait_ge(kx_turned, b + 1)
                act.activation(kxT[:], bank[0][:, :], ACT.Copy).then_inc(kxT_kept, 1)
                act.wait_ge(norms_made, b + 1)
                act.activation(minv[:, 0, :], bank[2][:, 0:4:2], ACT.Sqrt).then_inc(norms_rooted, 1)
                q4_high(b * CHUNKS)
                q2_high(b * CHUNKS)

                def step_b(i, n):
                    g = b * TILES + i

                    def normalise():
                        t, s = g - 4, n % 4
                        hi_ = h[:, ds(i - 4, 1), :].rearrange("p o d -> p (o d)")
                        if n >= 8:
                            act.wait_ge(xn2_lo_made, t - 3)
                        settled(act)
                        act.activation(xn2_32[:, s, :], hi_, ACT.Identity, scale=rstd[:, s:s + 1],
                                       bias=norm_by[:, 1, s:s + 1]).then_inc(xn2_made, 1)
                        if n >= 8:
                            act.wait_ge(xn2_stored[(n - 4) % 8], 16 * (b * (TILES // 8)) + 16 * ((i - 4) // 8))
                            settled(act)
                        act.activation(hi_, hi_, ACT.Identity, scale=norm_by[:, 0, s:s + 1], bias=norm_by[:, 1, s:s + 1])\
                           .then_inc(h_added, 1)
                        act.wait_ge(xn2_made, t + 1)
                        act.activation(xn2[:, (n - 4) % 8, 0:D], xn2_32[:, s, :], ACT.Copy).then_inc(xn2_hi_made, 1)

                    if n < TILES and n % 4 == 0:
                        act.wait_ge(s4_made, chunk_of(b, i, n) + 1)
                        if n >= 4:
                            act.wait_ge(p2_used, g - 3)
                        act.activation(q_n[:, :], bank[4][:, D:D + 8:2], ACT.Sqrt).then_inc(q_rooted, 1)
                    if 4 <= n < TILES + 4 and n % 4 != 0:
                        normalise()
                    if n % 4 == 1 and n + 4 < TILES + 1:
                        squares(chunk_of(b, i, n) + 1)
                    if n % 4 == 2 and n + 4 < TILES + 2:
                        q4_high(chunk_of(b, i, n) + 1)
                    if n % 4 == 3 and n + 4 < TILES + 3:
                        q2_high(chunk_of(b, i, n) + 1)
                    if 5 <= n < TILES + 5:
                        t, s = g - 5, (n - 5) % 2
                        act.wait_ge(xn2_turned, t + 1)
                        if n >= 7:
                            act.wait_ge(logits_made, t - 1)
                        act.activation(xn2T[:, s, :], half(4, 0).bitcast(F16), ACT.Copy).then_inc(xn2T_made, 1)
                    if n % 4 == 0 and 4 <= n < TILES + 4:
                        act.wait_ge(var2_made, chunk_of(b, i, n))
                        act.activation(sd[:, :], mv[:, :, 1], ACT.Sqrt, bias=eps_ln[:, 0:1]).then_inc(sd2_made, 1)
                        act.wait_ge(rstd2_made, chunk_of(b, i, n))
                        normalise()
                run(act, step_b, LAST_B, TILES - 8)
                all_meet(act, 4 + 4 * b)

                act.activation(gate[:, 0, :], gap[:, :], ACT.Exp, scale=-1.0 / WS).then_inc(exp_made, 1)
                act.wait_ge(blocks_made, b + 1)
                settled(act)

                def step_c(i, n):
                    if n < NBLOCKS:
                        s = n % UC
                        e = act.value_load(blk_e[0:1, ds(i, 1)], min_val=0, max_val=E - 1)
                        act.wait_ge(up_made, b * NBLOCKS + i + 1)
                        if n >= UC:
                            act.wait_ge(y_stored[s], 16 * (b * (NBLOCKS // UC)) + 16 * (i // UC))
                        for f in range(DC):
                            ins = act.activation(g32[s][:, f * BLOCK:f * BLOCK + BLOCK], half(1 + s, f), ACT.Gelu,
                                                 scale=1.0 / WS,
                                                 bias=col_1[:, ds(e, 1), f:f + 1].rearrange("p o n -> p (o n)"))
                        ins.then_inc(gelu_made, 1)
                    if n >= 1:
                        s = (n - 1) % UC
                        act.wait_ge(down_made, b * NBLOCKS + i - 1 + 1)
                        act.activation(g32[s][:, :], bank[4 + s][:, :], ACT.Copy, scale=1.0 / WS).then_inc(y_made, 1)
                run_c(act, step_c, NBLOCKS + 1)
                all_meet(act, 5 + 4 * b)
                all_meet(act, 6 + 4 * b)

        @block.vector
        def _(dve):
            f_c = xnT[:].rearrange("p a c t -> p (a c t)").bitcast(F32)
            coef = x_raw[:, 0, 128:256]
            pair = x_raw[:, 0, 256:320]
            dve.memset(ones_r[:, :].bitcast(F32), 1.0)
            dve.memset(ones32[:, :], 1.0)
            dve.memset(ones16[:, :], 1.0)
            dve.memset(zeros[:, :], 0.0)
            dve.memset(eps_ln[:, :], EPS_LN)
            dve.drain()
            dve.wait_ge(loaded, 16 * SETUP_LOADS)
            bv_col = scr[:, 5648:5652]
            for c in range(DC):
                dve.tensor_copy(x_raw[:, 2, c * P:c * P + P], bv_col[:, 2 + c:3 + c].to_broadcast([P, P]))
            dve.tensor_tensor(f_c.rearrange("p (n c) -> p n c", c=C),
                              coef.unsqueeze(2).to_broadcast([P, P, C]),
                              pair.unsqueeze(1).to_broadcast([P, P, C]), ALU.mult).then_inc(coef_made, 1)
            dve.tensor_copy(ident16[:, :], ident[:, :])
            dve.tensor_copy(earlier[:, :], x_raw[:, 0, 0:P])
            dve.tensor_scalar(first2[:, :], ones16[:, :], pick[:, 0:1], None, ALU.mult)
            dve.drain()
            dve.scalar_tensor_tensor(out=first2[:, :], in0=ones16[:, :], scalar=pick[:, 1:2], in1=first2[:, :],
                                     op0=ALU.mult, op1=ALU.add)
            w_qkv = scr[:, 2048:3584].rearrange("p (c n) -> p c n", c=DC)
            w_r32 = scr[:, 4608:4624].rearrange("p (c n) -> p c n", c=DC)
            b_qkv = scr[:, 4624:5392]
            b_out = scr[:, 5392:5648]
            means = w_means
            tmp = x_raw[:, 1, 0:D]

            for x in range(2):
                for c in range(DC):
                    dve.tensor_reduce(means[:, 2 * x + c:2 * x + c + 1], w_qkv[:, c, x * D:x * D + D], AX.X, ALU.add)
                dve.tensor_reduce(means[:, 4 + x:5 + x], b_qkv[:, x * D:x * D + D], AX.X, ALU.add)
            dve.drain()
            dve.tensor_scalar(means[:, 0:6], means[:, 0:6], 1.0 / D, None, ALU.mult)
            dve.drain()
            for x, w in ((0, w_q), (1, w_k)):
                for c in range(DC):
                    dve.tensor_scalar(w_qkv[:, c, x * D:x * D + D], w_qkv[:, c, x * D:x * D + D],
                                      means[:, 2 * x + c:2 * x + c + 1], WS, ALU.subtract, ALU.mult)
            dve.tensor_scalar(w_r32, w_r32, WS, None, ALU.mult)
            dve.tensor_scalar(b_qkv[:, D:2 * D], b_qkv[:, D:2 * D], means[:, 5:6], WS, ALU.subtract, ALU.mult)
            dve.tensor_scalar(col_q[:, :], bv_col[:, 0:2], means[:, 4:5], None, ALU.subtract)
            dve.drain()

            def split(hi, lo, x):
                dve.drain()
                dve.tensor_copy(hi, x)
                dve.drain()
                dve.tensor_tensor(lo, x, hi, ALU.subtract)

            def rows(o, x, hi, lo):
                split(hi, lo, x)
                dve.drain()
                dve.tensor_scalar(o, hi, pick[:, 0:1], None, ALU.mult)
                dve.drain()
                dve.scalar_tensor_tensor(out=o, in0=lo, scalar=pick[:, 1:2], in1=o, op0=ALU.mult, op1=ALU.add)
            split(w_q[:, 0], w_q[:, 1], w_qkv[:, :, 0:D])
            split(w_k[:, 0], w_k[:, 1], w_qkv[:, :, D:2 * D])
            split(w_r[:, 0], w_r[:, 1], w_r32)
            hi16, lo16 = [x_raw[:, 3, 128 * x:128 * x + 128].bitcast(F16) for x in range(2)]
            rows(row_k[:, :], b_qkv[:, D:2 * D], hi16, lo16)
            for k in range(KC):
                dve.wait_ge(w_kept, k // 2 + 1)
                dve.tensor_tensor(w_tok[:, 1, k, :], half(k // 2, k % 2), w_tok[:, 0, k, :].bitcast(F32), ALU.subtract)
            dve.wait_ge(w_kept, KC // 2 + 1)
            dve.drain()
            dve.tensor_scalar(scr[:, 3072:3584], w_vo32[:].rearrange("p c n -> p (c n)"), WS, None, ALU.mult)
            dve.tensor_tensor(tmp, bvo[:, :], b_out, ALU.add)
            dve.drain()
            dve.tensor_scalar(tmp, tmp, WS, None, ALU.mult)
            dve.drain()
            split(w_vo[:, 0], w_vo[:, 1], scr[:, 3072:3584].rearrange("p (c n) -> p c n", c=DC))
            rows(row_o[:, :], tmp, hi16, lo16)
            for x, w in ((0, w_1), (1, w_2)):
                dve.wait_ge(w_kept, KC // 2 + 2 + x)
                dve.scalar_tensor_tensor(out=w[:, 1].rearrange("p e c d -> p (e c d)"),
                                         in0=h[:, 16 * x:16 * x + 16, :].rearrange("p t d -> p (t d)"), scalar=WS,
                                         in1=w[:, 0].rearrange("p e c d -> p (e c d)"), op0=ALU.mult, op1=ALU.subtract)
            dve.drain()
            dve.memset(h[:, 8:10, :].bitcast(U32), 0)
            all_meet(dve, 1)
            for q in range(4):
                dve.wait_ge(x_hi_done, q + 1)
                dve.tensor_tensor(x_lo[:, 0, q * XQ:(q + 1) * XQ], x_raw[:, q, :],
                                  x_hi[:, 0, q * XQ:(q + 1) * XQ].bitcast(F32), ALU.subtract).then_inc(x_lo_done, 1)
            dve.wait_ge(loaded2, 64)
            b2 = h[:, 0:8, :].rearrange("p t d -> p (t d)")
            dve.tensor_scalar(b2, b2, WS, None, ALU.mult)
            dve.drain()
            rows(row_2[:].rearrange("p e d -> p (e d)"), b2, h[:, 10:14, :].rearrange("p t d -> p (t d)").bitcast(F16),
                 h[:, 14:18, :].rearrange("p t d -> p (t d)").bitcast(F16))
            all_meet(dve, 2)

            def layernorm(stats_n, sem_var, sem_sd, wait_sd):
                dve.drain()
                for s in range(4):
                    ins = dve.bn_aggr(mv[:, s, :], st[:, s, :])
                ins.then_inc(sem_var, 1)
                dve.wait_ge(sem_sd, wait_sd)
                dve.reciprocal(rstd[:, :], sd[:, :])
                dve.drain()

            with dve.Fori(0, B) as b:
                def step_a(i, n):
                    g = b * TILES + i
                    if 4 <= n < TILES + 4:
                        t = g - 4
                        dve.wait_ge(xnT_hi_made, t + 1)
                        dve.tensor_tensor(xnT[:, 1, :, ds((i - 4) * P, P)],
                                          half((2, 7)[n % 2], 0).rearrange("p (c t) -> p c t", c=DC),
                                          xnT[:, 0, :, ds((i - 4) * P, P)], ALU.subtract).then_inc(xnT_lo_made, 1)
                    if n < TILES:
                        q, par = n % 4, n // 4 % 2
                        dve.wait_ge(x_hi_done, 4 * chunk_of(b, i, n) + 4 + q + 1)
                        dve.tensor_tensor(x_lo[:, 1 - par, q * XQ:(q + 1) * XQ], x_raw[:, q, :],
                                          x_hi[:, 1 - par, q * XQ:(q + 1) * XQ].bitcast(F32), ALU.subtract)\
                           .then_inc(x_lo_done, 1)
                        dve.wait_ge(h_kept, g + 1)
                        dve.bn_stats(st[:, n % 4, :], h[:, ds(i, 1), :].rearrange("p o d -> p (o d)"))
                    if 5 <= n < TILES + 5:
                        t, s = g - 5, (n - 5) % 2
                        dve.wait_ge(k2_made, t + 1)
                        dve.tensor_scalar(k_eps[:, :], k2s[:, s:s + 1], EPS_DIV, 1.0 / KS, ALU.add, ALU.mult)
                        dve.drain()
                        if n >= 7:
                            dve.wait_ge(k4_made, t - 1)
                        dve.reciprocal(k_scale[:, s:s + 1], k_eps[:, :]).then_inc(k_scaled, 1)
                        dve.wait_ge(k2_hi_made, t + 1)
                        dve.scalar_tensor_tensor(out=k2_lo[:, s, :], in0=k2[:, s, :], scalar=k_scale[:, s:s + 1],
                                                 in1=k2_hi[:, s, :], op0=ALU.mult, op1=ALU.subtract).then_inc(k2_lo_made, 1)
                    if n % 4 == 3 and n < TILES:
                        layernorm(n, var_made, sd_made, chunk_of(b, i, n) + 1)
                        for s in range(4):
                            if n >= 4:
                                dve.wait_ge(xn_turned, g - 3 + s - 3)
                                dve.wait_ge(xn_hi_made, g - 3 + s - 3)
                            dve.tensor_scalar(xn32[:, s, :], h[:, ds(i - 3 + s, 1), :].rearrange("p o d -> p (o d)"),
                                              mv[:, s, 0:1], rstd[:, s:s + 1], ALU.subtract, ALU.mult).then_inc(xn_made, 1)
                        for s in range(4):
                            dve.wait_ge(xn_hi_made, g - 3 + s + 1)
                            dve.tensor_tensor(xn_lo[:, (n - 3 + s) % 8, 0:D], xn32[:, s, :], xn_hi[:, (n - 3 + s) % 8, 0:D],
                                              ALU.subtract).then_inc(xn_lo_made, 1)
                dve.memset(xn_hi[:, :, D:D + 1], 1.0)
                dve.memset(xn_lo[:, :, D:D + 1], 0.0)
                run(dve, step_a, LAST_A)
                all_meet(dve, 3 + 4 * b)

                def sum_q4(G):
                    dve.wait_ge(q4_made, G + 1)
                    dve.tensor_tensor(q4s[:], q4[:, 0, :], q4[:, 1, :], ALU.add).then_inc(q4_summed, 1)

                def q4_low(G):
                    dve.wait_ge(q4_hi_made, G + 1)
                    dve.tensor_tensor(q4_lo, q4s[:], q4_hi.bitcast(F32), ALU.subtract).then_inc(q4_split, 1)

                def q2_low(G):
                    dve.wait_ge(q2_hi_made, G + 1)
                    dve.tensor_tensor(q2_lo, q2[:], q2_hi.bitcast(F32), ALU.subtract).then_inc(q2_split, 1)

                for c in range(DC):
                    ins = dve.tensor_copy(kxs[:, c, :], bank[4 + c][:, 0:D + 1])
                ins.then_inc(kx_kept, 1)
                dve.memset(before[:, :], 0.0)
                dve.tensor_copy(ids_f[:, :], ids_0[:, :])
                sum_q4(b * CHUNKS)
                dve.wait_ge(norms_rooted, b + 1)
                dve.tensor_scalar(minv[:, 1, :], minv[:, 0, :], 1.0 / KS, EPS_NORM, ALU.mult, ALU.max)
                dve.drain()
                dve.reciprocal(minv[:, 0, :], minv[:, 1, :])
                dve.drain()
                dve.tensor_scalar(minv[:, 1, :], minv[:, 0, :], 1.0 / (KS * float(NT) ** 0.5), None, ALU.mult)
                dve.wait_ge(m_summed, b + 1)
                for c in range(DC):
                    dve.scalar_tensor_tensor(out=m32[:, c, :], in0=bvo[:, :], scalar=kxs[:, c, D:D + 1], in1=half(1, c),
                                             op0=ALU.mult, op1=ALU.add)
                dve.drain()
                for c in range(DC):
                    dve.tensor_scalar(m_at[:, 0, c, 0:D], m32[:, c, :], minv[:, 1, c:c + 1], None, ALU.mult)
                dve.drain()
                for c in range(DC):
                    ins = dve.scalar_tensor_tensor(out=m_at[:, 1, c, 0:D], in0=m32[:, c, :], scalar=minv[:, 1, c:c + 1],
                                                   in1=m_at[:, 0, c, 0:D].bitcast(F32), op0=ALU.mult, op1=ALU.subtract)
                ins.then_inc(m_ready, 1)
                q4_low(b * CHUNKS)
                q2_low(b * CHUNKS)

                def places_at(b, i, u):
                    dve.wait_ge(ranks_made, b * CHUNKS + (i - 11) // 4 + 1)
                    dve.tensor_tensor(pos[:, :, :], bank[1 + u][:, D:D + 4 * E].rearrange("p (t e) -> p t e", e=E),
                                      region0[:, :].unsqueeze(1).to_broadcast([P, 4, E]), ALU.add)

                def step_b(i, n):
                    g = b * TILES + i
                    if 5 <= n < TILES + 5:
                        t = g - 5
                        dve.wait_ge(xn2_hi_made, t + 1)
                        dve.tensor_tensor(xn2[:, (n - 5) % 8, D:2 * D], xn2_32[:, (n - 5) % 4, :], xn2[:, (n - 5) % 8, 0:D],
                                          ALU.subtract).then_inc(xn2_lo_made, 1)
                    if n % 4 == 2 and n + 4 < TILES + 2:
                        sum_q4(chunk_of(b, i, n) + 1)
                    if n % 4 == 3 and n + 4 < TILES + 3:
                        q4_low(chunk_of(b, i, n) + 1)
                    if n < TILES and n % 4 == 0:
                        dve.wait_ge(q_rooted, chunk_of(b, i, n) + 1)
                        dve.tensor_scalar(q_guard[:, :], q_n[:, :], EPS_NORM * EPS_DIV, None, ALU.max)
                        dve.drain()
                        dve.reciprocal(r_q[:, :], q_guard[:, :])
                        dve.drain()
                    if n % 4 == 2 and n >= 10:
                        G = b * CHUNKS + (i - 10) // 4
                        dve.wait_ge(logits_made, 4 * G + 4)
                        settled(dve)
                        for s in range(4):
                            dve.max(top[:, s, :], bank[5][:, E * s:E * s + E])
                        dve.drain()
                        for s in range(4):
                            ins = dve.max_index(top_i[:, s, :], top[:, s, :], bank[5][:, E * s:E * s + E])
                        ins.then_inc(logits_read, 1)
                        dve.tensor_tensor(gap[:, ds(i - 10, 4)], top[:, :, 0], top[:, :, 1], ALU.subtract)
                        dve.drain()
                        dve.tensor_copy(e_all[:, ds(i - 10, 4), :], top_i[:, :, 0:2])
                        dve.tensor_copy(e_now[:, :, :], top_i[:, :, 0:2])
                        dve.drain()
                        dve.tensor_tensor(hot[:].rearrange("p t s e -> p (t s) e"),
                                          iota_e[:, :].unsqueeze(1).to_broadcast([P, 8, E]),
                                          e_now[:].rearrange("p t s -> p (t s)").unsqueeze(2).to_broadcast([P, 8, E]),
                                          ALU.is_equal)
                        dve.drain()
                        dve.tensor_tensor(sel[:, :, :], hot[:, :, 0, :], hot[:, :, 1, :], ALU.add).then_inc(sel_made, 1)
                    if n < TILES:
                        u = n % 2
                        dve.wait_ge(p2_made, g + 1)
                        if n % 4 == 3 and n >= 11:
                            places_at(b, i, u)
                        dve.scalar_tensor_tensor(out=att[:, u, :], in0=half(1 + u, 0), scalar=r_q[:, n % 4:n % 4 + 1],
                                                 in1=h[:, ds(i, 1), :].rearrange("p o d -> p (o d)"),
                                                 op0=ALU.mult, op1=ALU.add).then_inc(p2_used, 1)
                    if 1 <= n <= TILES:
                        u = (n - 1) % 2
                        hi_ = h[:, ds(i - 1, 1), :].rearrange("p o d -> p (o d)")
                        dve.wait_ge(p1_made, g)
                        dve.wait_ge(p2_used, g)
                        dve.scalar_tensor_tensor(out=hi_, in0=half(3 * u, 0), scalar=1.0 / WS, in1=att[:, u, :],
                                                 op0=ALU.mult, op1=ALU.add).then_inc(p1_used, 1)
                    if n % 4 == 3 and n >= 11:
                        G = b * CHUNKS + (i - 11) // 4
                        if n >= TILES:
                            places_at(b, i, n % 2)
                        dve.tensor_reduce(chunk_sel[:, :], sel[:].rearrange("p t e -> p e t"), AX.X, ALU.add)
                        dve.drain()
                        dve.tensor_tensor(before[:, :], before[:, :], chunk_sel[:, :], ALU.add).then_inc(before_made, 1)
                        dve.tensor_tensor(hot_pos[:, :, :, :], hot[:, :, :, :],
                                          pos[:, :, :].unsqueeze(2).to_broadcast([P, 4, 2, E]), ALU.mult)
                        dve.drain()
                        dve.tensor_reduce(slot_f[:, :, :], hot_pos[:, :, :, :], AX.X, ALU.add)
                        dve.drain()
                        dve.wait_ge(ids_stored, 128 * G)
                        dve.tensor_copy(slots[:, ds(i - 11, 4), :], slot_f[:, :, :])
                        dve.tensor_copy(id_u[:, :], ids_f[:, :])
                        dve.tensor_copy(slot_u[:, :, :], slot_f[:, :, :]).then_inc(slots_made, 1)
                        dve.tensor_scalar(ids_f[:, :], ids_f[:, :], float(CT), None, ALU.add)
                    if 1 <= n <= TILES:
                        dve.wait_ge(p1_used, g)
                        settled(dve)
                        dve.bn_stats(st[:, (n - 1) % 4, :], hi_)
                    if n % 4 == 0 and 4 <= n <= TILES:
                        if n >= 8:
                            dve.wait_ge(h_added, g - 4)
                            settled(dve)
                        layernorm(n, var2_made, sd2_made, chunk_of(b, i, n))
                        dve.tensor_scalar(norm_by[:, 0, :], rstd[:, :], 1.0, None, ALU.add)
                        dve.scalar_tensor_tensor(out=norm_by[:, 1, :], in0=mv[:, :, 0], scalar=-1.0, in1=rstd[:, :],
                                                 op0=ALU.mult, op1=ALU.mult).then_inc(rstd2_made, 1)
                    if n % 4 == 3 and n + 4 < TILES + 3:
                        q2_low(chunk_of(b, i, n) + 1)
                run(dve, step_b, LAST_B, TILES - 8)
                all_meet(dve, 4 + 4 * b)

                dve.tensor_copy(cnt[:, :], bank[5][:, 0:E])
                dve.drain()
                dve.tensor_tensor(cmp_t[:, :, :], cnt[:, :].unsqueeze(2).to_broadcast([P, E, REGION]),
                                  thr[:, :].unsqueeze(1).to_broadcast([P, E, REGION]), ALU.is_gt)
                dve.drain()
                dve.tensor_reduce(n_blk[:, :], cmp_t[:, :, :], AX.X, ALU.add)
                dve.drain()
                dve.tensor_tensor(cum_m[:, :, :], n_blk[:, :].unsqueeze(1).to_broadcast([P, E, E]), upto[:, :, :], ALU.mult)
                dve.drain()
                dve.tensor_reduce(cum[:, :], cum_m[:, :, :], AX.X, ALU.add)
                dve.drain()
                dve.tensor_tensor(c_cmp[:, 0, :], ids_0[:, 0:1].to_broadcast([P, E]), cum[:, :], ALU.is_ge)
                dve.drain()
                dve.tensor_tensor(c_cmp[:, 1, :], c_cmp[:, 0, :], n_blk[:, :], ALU.mult)
                dve.drain()
                dve.tensor_reduce(c_sum[:, 0:2], c_cmp[:, :, :], AX.X, ALU.add)
                dve.drain()
                dve.tensor_tensor(c_sum[:, 2:3], ids_0[:, 0:1], c_sum[:, 1:2], ALU.subtract)
                dve.drain()
                dve.scalar_tensor_tensor(out=c_sum[:, 1:2], in0=c_sum[:, 0:1], scalar=float(REGION), in1=c_sum[:, 2:3],
                                         op0=ALU.mult, op1=ALU.add)
                dve.drain()
                dve.tensor_scalar(blk_at[:, :], c_sum[:, 1:2], float(PLACES // BLOCK - 1), None, ALU.min)\
                   .then_inc(block_rows_made, 1)
                dve.tensor_tensor(b_cmp[:, :, :], iota_b[:, :].unsqueeze(2).to_broadcast([P, NBLOCKS, E]),
                                  cum[:, :].unsqueeze(1).to_broadcast([P, NBLOCKS, E]), ALU.is_ge)
                dve.drain()
                dve.tensor_reduce(b_e[:, :], b_cmp[:, :, :], AX.X, ALU.add)
                dve.drain()
                dve.tensor_scalar(blk_e[:, :], b_e[:, :], float(E - 1), None, ALU.min).then_inc(blocks_made, 1)
                dve.wait_ge(ids_in, 16 * (b + 1))
                settled(dve)
                dve.tensor_copy(ids_rows32[:, :], ids_rows[:, :]).then_inc(ids_read, 1)
                dve.wait_ge(ids_turned, b + 1)
                settled(dve)
                dve.tensor_copy(ids_all[:, :, :], bank[7][:, 0:2 * P].rearrange("p (h n) -> p n h", h=2)[:, 0:NBLOCKS, :])\
                   .then_inc(ids_kept, 1)
                dve.wait_ge(exp_made, b + 1)
                dve.tensor_scalar(gate[:, 2, :], gate[:, 0, :], 1.0, None, ALU.add)
                dve.drain()
                dve.reciprocal(gate[:, 1, :], gate[:, 2, :])
                dve.drain()
                dve.tensor_tensor(gate[:, 2, :], gate[:, 0, :], gate[:, 1, :], ALU.mult)
                dve.tensor_tensor(e_shift[:, :], cum[:, :], n_blk[:, :], ALU.subtract)
                dve.drain()
                dve.scalar_tensor_tensor(out=e_shift[:, :], in0=e_shift[:, :], scalar=float(BLOCK), in1=region0[:, :],
                                         op0=ALU.mult, op1=ALU.subtract)
                is_e, shift = [x_raw[:, x, 0:2 * TILES * E].rearrange("p (t e) -> p t e", e=E) for x in range(2)]
                dve.tensor_tensor(is_e, iota_e[:, :].unsqueeze(1).to_broadcast([P, 2 * TILES, E]),
                                  e_all[:].rearrange("p t s -> p (t s)").unsqueeze(2).to_broadcast([P, 2 * TILES, E]),
                                  ALU.is_equal)
                dve.drain()
                dve.tensor_tensor(shift, is_e, e_shift[:, :].unsqueeze(1).to_broadcast([P, 2 * TILES, E]), ALU.mult)
                dve.drain()
                dve.tensor_reduce(x_raw[:, 2, 0:2 * TILES], shift, AX.X, ALU.add)
                dve.drain()
                dve.tensor_tensor(rows_at[:].rearrange("p t s -> p (t s)"), x_raw[:, 2, 0:2 * TILES],
                                  slots[:].rearrange("p t s -> p (t s)"), ALU.add)

                def step_c(i, n):
                    if n < NBLOCKS:
                        s = n % UC
                        dve.wait_ge(xg_turned, b * NBLOCKS + i + 1)
                        if n >= UC:
                            dve.wait_ge(up_made, b * NBLOCKS + i - UC + 1)
                        dve.tensor_copy(xT[s].rearrange("p c t -> p (c t)"), bank[0][:, :].bitcast(F16)).then_inc(xT_made, 1)
                    if n >= 1:
                        s = (n - 1) % UC
                        dve.wait_ge(gelu_made, b * NBLOCKS + i - 1 + 1)
                        if n >= UC + 1:
                            dve.wait_ge(down_made, b * NBLOCKS + i - 1 - UC + 1)
                        dve.tensor_copy(g_hi[s], g32[s])
                        dve.drain()
                        dve.tensor_tensor(g_lo[s], g32[s], g_hi[s], ALU.subtract).then_inc(g_split, 1)
                run_c(dve, step_c, NBLOCKS + 1)
                all_meet(dve, 5 + 4 * b)

                with dve.Fori(0, CHUNKS) as c:
                    for s in range(4):
                        t = c * 4 + s
                        dve.wait_ge(y_in[s], 32 * (b * CHUNKS + c) + 32)
                        dve.scalar_tensor_tensor(out=mixed[s], in0=yg[s][0], scalar=gate[:, 1, ds(t, 1)],
                                                 in1=h[:, ds(t, 1), :].rearrange("p o d -> p (o d)"), op0=ALU.mult, op1=ALU.add)
                        dve.drain()
                        dve.wait_ge(out_stored[s], 16 * (b * CHUNKS + c))
                        dve.scalar_tensor_tensor(out=summed[s], in0=yg[s][1], scalar=gate[:, 2, ds(t, 1)],
                                                 in1=mixed[s], op0=ALU.mult, op1=ALU.add).then_inc(out_made, 1)
                all_meet(dve, 6 + 4 * b)

        @block.gpsimd
        def _(pool):
            all_meet(pool, 1)
            all_meet(pool, 2)
            with pool.Fori(0, B) as b:
                pool.memset(k4acc[:, :], 0.0)
                pool.drain()

                def step_a(i, n):
                    if 5 <= n < TILES + 5:
                        t = b * TILES + i - 5
                        pool.wait_ge(k4_made, t + 1)
                        settled(pool)
                        pool.tensor_tensor(k4acc[:, :], k4acc[:, :], k4[:, (n - 5) % 2, :], ALU.add).then_inc(k4_added, 1)
                        pool.drain()
                run(pool, step_a, LAST_A)
                all_meet(pool, 3 + 4 * b)

                with pool.Fori(0, CHUNKS) as c:
                    pool.wait_ge(slots_made, b * CHUNKS + c + 1)
                    settled(pool)
                    for s in range(4):
                        for x in range(2):
                            pool.indirect_dma_start(place_ids, bass.IndirectOffsetOnAxis(slot_u[:, s, x:x + 1], 0),
                                                    id_u[:, s:s + 1], None).then_inc(ids_stored, 16)
                pool.wait_ge(ids_stored, 128 * CHUNKS * (b + 1))
                settled(pool)
                all_meet(pool, 4 + 4 * b)

                pool.wait_ge(block_rows_made, b + 1)
                settled(pool)
                pool.indirect_dma_start(ids_rows[:, :], None, place_ids.rearrange("(r n) o -> r (n o)", n=BLOCK),
                                        bass.IndirectOffsetOnAxis(blk_at[:, 0:1], 0)).then_inc(ids_in, 16)
                pool.wait_ge(ids_kept, b + 1)
                settled(pool)
                def gather_blocks(it, first):
                    for n in range(UC):
                        pool.wait_ge(xg_in[n], 32 * (b * (NBLOCKS // UC) + it))
                        settled(pool)
                        pool.tensor_copy(ids_now[:, n, :], ids_all[:, ds(it * UC + n, 1), :].rearrange("p o h -> p (o h)"))\
                            .then_inc(ids_copied, 1)
                        pool.wait_ge(ids_copied, b * NBLOCKS + it * UC + n + 1)
                        settled(pool)
                        if not first:
                            pool.wait_ge(xg_turned, b * NBLOCKS + it * UC + n - UC + 1)
                            settled(pool)
                        for hh in range(2):
                            pool.indirect_dma_start(xg[n][:, hh, :], None, xn2_rows,
                                                    bass.IndirectOffsetOnAxis(ids_now[:, n, hh:hh + 1], 0))\
                                .then_inc(xg_in[n], 16)
                gather_blocks(0, True)
                with pool.Fori(1, NBLOCKS // UC) as it:
                    gather_blocks(it, False)
                all_meet(pool, 5 + 4 * b)

                def gather_results(c, first):
                    for s in range(4):
                        pool.wait_ge(y_in[s], 32 * (b * CHUNKS + c))
                        settled(pool)
                        pool.tensor_copy(slot_now[:, s, :], rows_at[:, ds(c * 4 + s, 1), :].rearrange("p o h -> p (o h)"))\
                            .then_inc(slot_copied, 1)
                        pool.wait_ge(slot_copied, b * TILES + c * 4 + s + 1)
                        settled(pool)
                        if not first:
                            pool.wait_ge(out_made, b * TILES + c * 4 + s - 3)
                            settled(pool)
                        for x in range(2):
                            pool.indirect_dma_start(yg[s][x], None, y_rows,
                                                    bass.IndirectOffsetOnAxis(slot_now[:, s, x:x + 1], 0))\
                                .then_inc(y_in[s], 16)
                gather_results(0, True)
                with pool.Fori(1, CHUNKS) as c:
                    gather_results(c, False)
                all_meet(pool, 6 + 4 * b)


def kernel(x, L0_tok_W, L0_attn_W_qkv, L0_attn_b_qkv, L0_attn_W_out, L0_attn_b_out, L0_ffn_router_w,
           L0_ffn_w1, L0_ffn_b1, L0_ffn_w2, L0_ffn_b2):
    import numpy as np
    import concourse.bacc as bacc
    from concourse.bass_utils import run_bass_kernel_spmd

    def cols(w, n):
        return w.reshape(n, P, -1).transpose(1, 0, 2)

    x = np.asarray(x)
    xp = np.pad(x, ((0, 0), (0, 0), (0, PATCH - STRIDE), (0, 0)), mode="edge")
    steps = 2 * (ROWS - STRIDE // 2)
    chunks = [xp[b, :, c * steps:c * steps + 2 * ROWS, :].reshape(C, ROWS // 4, 4, 2, V)
              .transpose(3, 0, 2, 1, 4).reshape(P, XC)
              for b in range(B) for c in range(CHUNKS)]
    chunks.append(chunks[0])
    w = np.asarray(L0_tok_W).reshape(D, 2, PATCH // 2 + 1, C)
    w_tok = np.stack([w[:, r, f, :].T for r, f in FREQ])
    w_qkv, w_out = np.asarray(L0_attn_W_qkv), np.asarray(L0_attn_W_out)
    b_qkv = np.asarray(L0_attn_b_qkv)
    b_col = b_qkv.reshape(3, DC, P)
    arrays = {
        "x": np.stack(chunks),
        "w_tok": cols(w_tok.reshape(len(FREQ) * C, D), KW),
        "w_qkv": cols(w_qkv, DC),
        "w_out": cols(w_out, DC),
        "w_vT": cols(w_qkv[:, 2 * D:].T, DC),
        "w_r": cols(np.asarray(L0_ffn_router_w).T, DC),
        "b_qkv": np.broadcast_to(b_qkv, (P, 3 * D)),
        "b_out": np.broadcast_to(np.asarray(L0_attn_b_out), (P, D)),
        "b_qv_col": np.concatenate([b_col[0], b_col[2]]).T,
        "b_1": np.asarray(L0_ffn_b1).reshape(E * DC, P).T,
        "b_2": np.broadcast_to(np.asarray(L0_ffn_b2).reshape(1, E, D), (P, E, D)),
        "w_1": np.asarray(L0_ffn_w1).reshape(E, DC, P, D).transpose(2, 0, 1, 3),
        "w_2": np.asarray(L0_ffn_w2).reshape(E, DC, P, D).transpose(2, 0, 1, 3),
    }
    p = np.arange(P)
    coef = np.zeros((P, KW, PATCH))
    for n, (r, f) in enumerate(FREQ):
        angle = 2 * np.pi * ((f * np.arange(PATCH)) % PATCH) / PATCH
        coef[(n % 2) * C:(n % 2 + 1) * C, n // 2] = (-np.sin(angle) if r else np.cos(angle)) / np.sqrt(PATCH)
    e = np.arange(E)
    constants = {
        "ident": np.eye(P),
        "tri": p[:, None] < p[None, :],
        "coef": coef.reshape(P, P),
        "pair": (p[:, None] % C) == np.arange(C)[None, :],
        "pick": p[:, None] == np.arange(2)[None, :],
        "iota_e": np.broadcast_to(e, (P, E)),
        "region0": np.broadcast_to(e * NT, (P, E)),
        "thr": np.broadcast_to(np.arange(REGION) * BLOCK, (P, REGION)),
        "upto": np.broadcast_to(e[None, :] <= e[:, None], (P, E, E)),
        "iota_b": np.broadcast_to(np.arange(NBLOCKS), (P, NBLOCKS)),
        "ids_0": p[:, None] + P * np.arange(CHUNK_TILES)[None, :],
    }
    arrays.update({"c_" + k: np.asarray(v, np.float32) for k, v in constants.items()})
    arrays = {k: np.ascontiguousarray(v) for k, v in arrays.items()}

    nc = bacc.Bacc("TRN2", target_bir_lowering=False, num_devices=1, dynamic_dma_scratch_size=8192)
    ins = {k: nc.dram_tensor(k + "_in", v.shape, F32, kind="ExternalInput").ap() for k, v in arrays.items()}
    out = nc.dram_tensor("out", (B * NT, D), F32, kind="ExternalOutput").ap()
    build(nc, ins, out)
    r = run_bass_kernel_spmd(nc, [{k + "_in": v for k, v in arrays.items()}], core_ids=[0])
    got = r.results[0]["out"]
    return got.reshape(B, NPATCH, V, D).transpose(0, 2, 1, 3).reshape(B, NT, D)
```

```python
from contextlib import ExitStack

import concourse.bass as bass
from concourse import mybir

F32 = mybir.dt.float32
F32R = mybir.dt.float32r
F16 = mybir.dt.float16
U32 = mybir.dt.uint32
ALU = mybir.AluOpType
ACT = mybir.ActivationFunctionType
AX = mybir.AxisListType
ds = bass.ds

P = 128
B, C, T, V = 4, 64, 512, 64
D = 256
E = 8
PATCH, STRIDE = 16, 8
NPATCH = T // STRIDE
NT = V * NPATCH
TILES = NT // P
CHUNK_TILES = 4
CHUNKS = TILES // CHUNK_TILES
CT = CHUNK_TILES * P
KC = C * PATCH // P
ROWS = CT // V * STRIDE // 2 + STRIDE // 2
XC = ROWS * V
XQ = XC // 4
DC = D // P
FREQ = [(0, f) for f in range(PATCH // 2 + 1)] + [(1, f) for f in range(1, PATCH // 2)]
KW = len(FREQ) * C // P

WS = 64.0
KS = 256.0
EPS_LN, EPS_DIV, EPS_NORM = 1e-5, 1e-7, 1e-12

BLOCK = 256
REGION = NT // BLOCK
NBLOCKS = 2 * NT // BLOCK + E - 1
PLACES = (E + 1) * NT
SETUP_LOADS = 15
UC = 3
assert NBLOCKS % UC == 0


def build(nc, a, out):
    ctx = ExitStack()
    with ctx:
        def sb(name, shape, dt):
            return ctx.enter_context(nc.sbuf_tensor(name, shape, dt))

        def sem(name):
            return ctx.enter_context(nc.semaphore(name))

        xn2_rows = nc.dram_tensor("xn2_rows", (NT, 2 * D), F16, kind="Internal").ap()
        place_ids = nc.dram_tensor("place_ids", (PLACES, 1), U32, kind="Internal").ap()
        y_rows = nc.dram_tensor("y_rows", (NBLOCKS * BLOCK, D), F32, kind="Internal").ap()

        w_tok = sb("w_tok", [P, 2, KC, D], F32R)
        w_k = sb("w_k", [P, 2, DC, D], F16)
        w_q = sb("w_q", [P, 2, DC, D], F16)
        w_vo = sb("w_vo", [P, 2, DC, D], F16)
        w_vo32 = sb("w_vo32", [P, DC, D], F32)
        w_r = sb("w_r", [P, 2, DC, E], F16)
        w_1 = sb("w_1", [P, 2, E, DC, D], F16)
        w_2 = sb("w_2", [P, 2, E, DC, D], F16)
        bvo = sb("bvo", [P, D], F32)
        row_k = sb("row_k", [P, D], F16)
        row_o = sb("row_o", [P, D], F16)
        row_2 = sb("row_2", [P, E, D], F16)
        col_q = sb("col_q", [P, DC], F32)
        col_1 = sb("col_1", [P, E, DC], F32)
        m_at = sb("m_at", [P, 2, DC, D], F32R)
        ones_r = sb("ones_r", [P, 2], F32R)
        ones32 = sb("ones32", [P, 2], F32)
        first2 = sb("first2", [P, P], F16)
        zeros = sb("zeros", [P, D + 2], F16)
        ident = sb("ident", [P, P], F32)
        ident16 = sb("ident16", [P, P], F16)
        earlier = sb("earlier", [P, P], F16)
        ones16 = sb("ones16", [P, P], F16)
        pick = sb("pick", [P, 2], F32)
        eps_ln = sb("eps_ln", [P, 1], F32)
        iota_e = sb("iota_e", [P, E], F32)
        region0 = sb("region0", [P, E], F32)
        thr = sb("thr", [P, REGION], F32)
        upto = sb("upto", [P, E, E], F32)
        iota_b = sb("iota_b", [P, NBLOCKS], F32)
        ids_0 = sb("ids_0", [P, CHUNK_TILES], F32)
        ids_f = sb("ids_f", [P, CHUNK_TILES], F32)

        h = sb("h", [P, TILES, D], F32)
        xnT = sb("xnT", [P, 2, DC, NT], F16)
        x_raw = sb("x_raw", [P, 4, XQ], F32)
        x_hi = sb("x_hi", [P, 2, XC], F32R)
        x_lo = sb("x_lo", [P, 2, XC], F32R)
        k4acc = sb("k4acc", [P, D], F32)
        scr = sb("scr", [P, 6144], F32)

        def view(at, words, dt=F32):
            v = scr[:, at:at + words]
            return v if dt == F32 else v.bitcast(dt)

        xn32 = view(0, 1024).rearrange("p (t d) -> p t d", t=4)
        xn_hi = view(1024, 1032, F16).rearrange("p (t d) -> p t d", t=8)
        xn_lo = view(2056, 1032, F16).rearrange("p (t d) -> p t d", t=8)
        k2 = view(3088, 512).rearrange("p (t d) -> p t d", t=2)
        k2_hi = view(3600, 256, F16).rearrange("p (t d) -> p t d", t=2)
        k2_lo = view(3856, 256, F16).rearrange("p (t d) -> p t d", t=2)
        k4 = view(4112, 512).rearrange("p (t d) -> p t d", t=2)
        q2 = view(0, 1024).rearrange("p (c t) -> p c t", c=DC)
        q4 = view(1024, 1024).rearrange("p (c t) -> p c t", c=DC)
        q4s = view(2048, 512)
        xn2_32 = view(2560, 1024).rearrange("p (t d) -> p t d", t=4)
        xn2 = view(3584, 2048, F16).rearrange("p (t d) -> p t d", t=8)
        xn2T = view(5632, 512, F16).rearrange("p (t d) -> p t d", t=2)
        kxs = view(2560, 514).rearrange("p (c d) -> p c d", c=DC)
        kxT = view(3584, 512)
        m32 = view(4096, 512).rearrange("p (c d) -> p c d", c=DC)
        q2_hi = x_hi[:, 1, 0:1024].rearrange("p (c t) -> p c t", c=DC)
        q2_lo = x_lo[:, 1, 0:1024].rearrange("p (c t) -> p c t", c=DC)
        q4_hi = x_hi[:, 1, 1024:1536]
        q4_lo = x_lo[:, 1, 1024:1536]
        xg = [view(512 * n, 512, F16).rearrange("p (h d) -> p h d", h=2) for n in range(UC)]
        xT = [view(1536 + 512 * n, 512, F16).rearrange("p (c t) -> p c t", c=4) for n in range(UC)]
        g32 = [view(3072 + 512 * n, 512) for n in range(UC)]
        g_hi = [view(4608 + 512 * n, 256, F16) for n in range(UC)]
        g_lo = [view(4864 + 512 * n, 256, F16) for n in range(UC)]
        yg = [[view(4624 + 512 * n + 256 * s, 256) for s in range(2)] for n in range(2)]
        yg_last = [[view(512 * n + 256 * s, 256) for s in range(2)] for n in range(4)]

        st = sb("st", [P, 4, 6], F32)
        mv = sb("mv", [P, 4, 2], F32)
        sd = sb("sd", [P, 4], F32)
        rstd = sb("rstd", [P, 4], F32)
        norm_by = sb("norm_by", [P, 2, 4], F32)
        k2s = sb("k2s", [P, 2], F32)
        k_eps = sb("k_eps", [P, 1], F32)
        k_scale = sb("k_scale", [P, 2], F32)
        q_n = sb("q_n", [P, 4], F32)
        q_guard = sb("q_guard", [P, 4], F32)
        r_q = sb("r_q", [P, 4], F32)
        w_means = sb("w_means", [P, 6], F32)
        att = sb("att", [P, 2, D], F32)
        top = sb("top", [P, 4, 8], F32)
        top_i = sb("top_i", [P, 4, 8], U32)
        gap = sb("gap", [P, TILES], F32)
        e_now = sb("e_now", [P, 4, 2], F32)
        hot = sb("hot", [P, 4, 2, E], F32)
        sel = sb("sel", [P, 4, E], F16)
        chunk_sel = sb("chunk_sel", [P, E], F32)
        before = sb("before", [P, E], F16)
        pos = sb("pos", [P, 4, E], F32)
        hot_pos = sb("hot_pos", [P, 4, 2, E], F32)
        slot_f = sb("slot_f", [P, 4, 2], F32)
        slot_u = sb("slot_u", [P, 2, 4, 2], U32)
        slots = sb("slots", [P, TILES, 2], F32)
        e_all = sb("e_all", [P, TILES, 2], F32)
        rows_at = sb("rows_at", [P, TILES, 2], U32)
        e_shift = sb("e_shift", [P, E], F32)
        id_u = sb("id_u", [P, 2, CHUNK_TILES], U32)
        gate = sb("gate", [P, 3, TILES], F32)
        cnt = sb("cnt", [P, E], F32)
        cmp_t = x_raw[:, 3, 0:128].rearrange("p (e r) -> p e r", e=E)
        n_blk = sb("n_blk", [P, E], F32)
        cum_m = x_raw[:, 3, 128:192].rearrange("p (e r) -> p e r", e=E)
        cum = sb("cum", [P, E], F32)
        b_cmp = x_raw[:, 3, 192:504].rearrange("p (n e) -> p n e", e=E)
        c_cmp = sb("c_cmp", [P, 2, E], F32)
        c_sum = sb("c_sum", [P, 3], F32)
        blk_at = sb("blk_at", [P, 1], U32)
        ids_rows = view(3584, 256, U32)
        ids_rows32 = view(3840, 256)
        b_e = sb("b_e", [P, NBLOCKS], F32)
        blk_e = sb("blk_e", [P, NBLOCKS], U32)
        ids_all = sb("ids_all", [P, NBLOCKS, 2], U32)
        ids_now = sb("ids_now", [P, UC, 2], U32)
        slot_now = sb("slot_now", [P, 4, 2], U32)
        slots_last = sb("slots_last", [P, 2, 8], U32)
        minv = sb("minv", [P, 2, DC], F32)

        bank = [ctx.enter_context(nc.psum_tensor(f"bank{n}", [P, 512], F32)) for n in range(8)]

        def half(n, s):
            return bank[n][:, D * s:D * s + D]

        phase_end, waited = sem("phase_end"), sem("waited")
        coef_made, w_made, w_kept = sem("coef_made"), sem("w_made"), sem("w_kept")
        loaded = sem("loaded")
        coef_loaded, w_tok_loaded = sem("coef_loaded"), sem("w_tok_loaded")
        loaded2, h_free, w_12_high = sem("loaded2"), sem("h_free"), sem("w_12_high")
        x_in = [sem(f"x_in{q}") for q in range(4)]
        x_hi_done, x_lo_done = sem("x_hi_done"), sem("x_lo_done")
        h_made, h_kept = sem("h_made"), sem("h_kept")
        var_made, sd_made = sem("var_made"), sem("sd_made")
        xn_made, xn_hi_made, xn_lo_made = sem("xn_made"), sem("xn_hi_made"), sem("xn_lo_made")
        xn_turned, xnT_hi_made, xnT_lo_made = sem("xn_turned"), sem("xnT_hi_made"), sem("xnT_lo_made")
        k_made, k2_made, k_scaled = sem("k_made"), sem("k2_made"), sem("k_scaled")
        k2_hi_made, k2_lo_made, k4_made = sem("k2_hi_made"), sem("k2_lo_made"), sem("k4_made")
        k4_added, kx_added = sem("k4_added"), sem("kx_added")
        q_made, q2_made, q4_made, q4_summed = sem("q_made"), sem("q2_made"), sem("q4_made"), sem("q4_summed")
        q2_hi_made, q2_split, q4_hi_made, q4_split = sem("q2_hi_made"), sem("q2_split"), sem("q4_hi_made"), sem("q4_split")
        s4_made = sem("s4_made")
        kx_kept, kx_turned, kxT_kept = sem("kx_kept"), sem("kx_turned"), sem("kxT_kept")
        norms_made, norms_rooted, m_summed, m_ready = (
            sem("norms_made"), sem("norms_rooted"), sem("m_summed"), sem("m_ready"))
        p2_made, p1_made, q_rooted = sem("p2_made"), sem("p1_made"), sem("q_rooted")
        p2_used, p1_used = sem("p2_used"), sem("p1_used")
        var2_made, sd2_made, rstd2_made, h_added = sem("var2_made"), sem("sd2_made"), sem("rstd2_made"), sem("h_added")
        xn2_made, xn2_hi_made, xn2_lo_made = sem("xn2_made"), sem("xn2_hi_made"), sem("xn2_lo_made")
        xn2_stored = [sem(f"xn2_stored{n}") for n in range(8)]
        xn2_turned, xn2T_made, logits_made, logits_read = (
            sem("xn2_turned"), sem("xn2T_made"), sem("logits_made"), sem("logits_read"))
        sel_made, ranks_made, slots_made = sem("sel_made"), sem("ranks_made"), sem("slots_made")
        ids_stored = [sem(f"ids_stored{n}") for n in range(2)]
        counts_made, exp_made, blocks_made = sem("counts_made"), sem("exp_made"), sem("blocks_made")
        before_made = sem("before_made")
        block_rows_made, ids_in, ids_read, ids_turned, ids_kept = (
            sem("block_rows_made"), sem("ids_in"), sem("ids_read"), sem("ids_turned"), sem("ids_kept"))
        ids_copied = sem("ids_copied")
        xg_in = [sem(f"xg_in{n}") for n in range(UC)]
        xg_turned, xT_made = sem("xg_turned"), sem("xT_made")
        up_made, gelu_made, g_hi_made, g_split = sem("up_made"), sem("gelu_made"), sem("g_hi_made"), sem("g_split")
        down_made, y_made = sem("down_made"), sem("y_made")
        y_stored = [sem(f"y_stored{n}") for n in range(UC)]
        slot_copied = sem("slot_copied")
        y_in = [sem(f"y_in{n}") for n in range(2)]
        y_in_last = [sem(f"y_in_last{n}") for n in range(4)]
        first_added, out_made = sem("first_added"), sem("out_made")
        rstd_made = sem("rstd_made")
        out_stored = [sem(f"out_stored{n}") for n in range(4)]

        def all_meet(eng, k):
            settled(eng)
            eng.drain().then_inc(phase_end, 1)
            eng.wait_ge(phase_end, 5 * k)
            settled(eng)

        def settled(eng):
            eng.sem_inc(waited, 1)

        def three(eng, o, hi, lo, w_hi, w_lo, first, last, free=False):
            eng.matmul(o, hi, w_hi, start=first, stop=False, skip_group_check=free)
            eng.matmul(o, lo, w_hi, start=False, stop=False, skip_group_check=free)
            return eng.matmul(o, hi, w_lo, start=False, stop=last, skip_group_check=free)

        def run(eng, step, last, looped=TILES):
            for n in range(8):
                step(n, n)
            with eng.Fori(1, looped // 8) as it:
                for n in range(8):
                    step(it * 8 + n, 8 + n)
            for n in range(looped, last):
                step(n, n)

        def run_c(eng, step, last):
            for n in range(2 * UC):
                step(n, n)
            with eng.Fori(2, NBLOCKS // UC) as it:
                for n in range(UC):
                    step(it * UC + n, 2 * UC + n)
            for n in range(NBLOCKS, last):
                step(n, n)

        def batches(eng, phase_a, phase_b, phase_c, phase_d):
            phase_a(0, None)
            with eng.Fori(0, B - 1) as b:
                phase_b(b)
                phase_c(b)
                phase_a(b + 1, b)
            phase_b(B - 1)
            phase_c(B - 1)
            phase_d(B - 1)

        def results_in(d, t, deep):
            if deep == 2:
                return 32 * (d * (TILES // 2) + t // 2) + 32
            return 32 * (t // 4) + 32

        def chunk_of(b, i, n):
            return b * CHUNKS + i // 4

        def quarter_in(b, i, n):
            return 16 * (chunk_of(b, i, n) + 2)

        LAST_A = TILES + 6
        LAST_B = TILES + 8

        block = ctx.enter_context(nc.Block())

        @block.sync
        def _(sp):
            def load(o, i):
                sp.dma_start(o, i).then_inc(loaded, 16)
            for t, name in ((ident[:], "ident"), (x_raw[:, 0, 0:P], "tri"), (x_raw[:, 0, 128:256], "coef"),
                            (x_raw[:, 0, 256:320], "pair")):
                sp.dma_start(t, a["c_" + name]).then_inc(coef_loaded, 16)
            sp.dma_start(scr[:, 0:2048].rearrange("p (q d) -> p q d", q=KW), a["w_tok"]).then_inc(w_tok_loaded, 16)
            for name, t in (("pick", pick), ("iota_e", iota_e), ("region0", region0),
                            ("thr", thr), ("upto", upto), ("iota_b", iota_b), ("ids_0", ids_0)):
                load(t[:], a["c_" + name])
            load(scr[:, 2048:3584].rearrange("p (c n) -> p c n", c=DC), a["w_qkv"])
            load(scr[:, 3584:4096].rearrange("p (c n) -> p c n", c=DC), a["w_out"])
            load(scr[:, 4096:4608].rearrange("p (c n) -> p c n", c=DC), a["w_vT"])
            load(scr[:, 4608:4624].rearrange("p (c n) -> p c n", c=DC), a["w_r"])
            load(scr[:, 4624:5392], a["b_qkv"])
            load(scr[:, 5392:5648], a["b_out"])
            load(scr[:, 5648:5652], a["b_qv_col"])
            load(col_1[:].rearrange("p e c -> p (e c)"), a["b_1"])
            sp.dma_start(h[:, 0:16, :].rearrange("p (e c) d -> p e c d", e=E), a["w_1"]).then_inc(loaded2, 16)
            sp.dma_start(h[:, 16:32, :].rearrange("p (e c) d -> p e c d", e=E), a["w_2"]).then_inc(loaded2, 16)
            sp.wait_ge(coef_made, KC // 2)
            for q in range(4):
                sp.dma_start(x_raw[:, q, :], a["x"][0][:, q * XQ:(q + 1) * XQ]).then_inc(x_in[q], 16)
            sp.wait_ge(h_free, 1)
            sp.dma_start(h[:, 0:8, :], a["b_2"]).then_inc(loaded2, 16)
            sp.dma_start(place_ids.rearrange("(p n) o -> p (n o)", p=P), h[:, 8:10, :].rearrange(
                "p t d -> p (t d)")[:, 0:PLACES // P].bitcast(U32)).then_inc(loaded2, 16)
            sp.wait_ge(loaded2, 64)
            all_meet(sp, 1)

            def store_sums(d, t, n):
                sp.wait_ge(out_made, d * TILES + t + 1)
                sp.dma_start(out[ds((d * TILES + t) * P, P), :], h[:, ds(t, 1), :].rearrange("p o d -> p (o d)"))\
                  .then_inc(out_stored[n % 4], 16)

            def phase_a(b, d):
                def load_x(c, q):
                    sp.wait_ge(x_hi_done, 4 * (b * CHUNKS + c) + q + 1)
                    sp.wait_ge(x_lo_done, 4 * (b * CHUNKS + c) + q + 1)
                    sp.dma_start(x_raw[:, q, :], a["x"][ds(b * CHUNKS + c + 1, 1), :, q * XQ:(q + 1) * XQ]
                                 .rearrange("o p n -> (o p) n")).then_inc(x_in[q], 16)

                def step_a(c, q, last):
                    if not last or q < 2:
                        load_x(c + (q + 2) // 4, (q + 2) % 4)
                    if d is not None and not (last and q == 3):
                        store_sums(d, c * 4 + q + 1, q + 1)
                load_x(0, 0)
                load_x(0, 1)
                if d is not None:
                    store_sums(d, 0, 0)
                with sp.Fori(0, CHUNKS - 1) as c:
                    for q in range(4):
                        step_a(c, q, False)
                for q in range(4):
                    step_a(CHUNKS - 1, q, True)
                all_meet(sp, 2 + 3 * b)

            def phase_b(b):
                def store_rows(i, n):
                    sp.wait_ge(xn2_hi_made, b * TILES + i + 1)
                    sp.wait_ge(xn2_lo_made, b * TILES + i + 1)
                    sp.dma_start(xn2_rows[ds(i * P, P), :], xn2[:, n % 8, :])\
                      .then_inc(xn2_stored[n % 8], 16)
                run(sp, store_rows, TILES, TILES - 8)
                for n in range(8):
                    sp.wait_ge(xn2_stored[n], 16 * (TILES // 8) * (b + 1))
                all_meet(sp, 3 + 3 * b)

            def phase_c(b):
                with sp.Fori(0, NBLOCKS // UC) as it:
                    for n in range(UC):
                        sp.wait_ge(y_made, b * NBLOCKS + it * UC + n + 1)
                        sp.dma_start(y_rows[ds((it * UC + n) * BLOCK, BLOCK), :].rearrange("(h p) d -> p h d", p=P),
                                     g32[n].rearrange("p (h d) -> p h d", h=2)).then_inc(y_stored[n], 16)
                for n in range(UC):
                    sp.wait_ge(y_stored[n], 16 * (NBLOCKS // UC) * (b + 1))
                all_meet(sp, 4 + 3 * b)

            def phase_d(b):
                with sp.Fori(0, CHUNKS) as c:
                    for n in range(4):
                        store_sums(b, c * 4 + n, n)
                all_meet(sp, 5 + 3 * b)
            batches(sp, phase_a, phase_b, phase_c, phase_d)
            for n in range(4):
                sp.wait_ge(out_stored[n], 16 * CHUNKS * B)
            for q in range(4):
                sp.wait_ge(x_in[q], 16 * (B * CHUNKS + 1))

        @block.tensor
        def _(pe):
            f_w = scr[:, 0:2048].rearrange("p (q d) -> p q d", q=KW)
            f_c = xnT[:].rearrange("p a c t -> p (a c t)").bitcast(F32).rearrange(
                "p (q k m) -> p q k m", q=KW, k=KC)
            w_out_f = scr[:, 3584:4096].rearrange("p (c n) -> p c n", c=DC)
            w_vT_f = scr[:, 4096:4608].rearrange("p (c n) -> p c n", c=DC)
            bv_b = scr[:, 5652:5652 + 2 * P].rearrange("p (c m) -> p c m", c=DC)
            pe.wait_ge(w_tok_loaded, 16)
            for k in range(KC):
                if k == 2:
                    pe.wait_ge(loaded, 16 * SETUP_LOADS)
                pe.wait_ge(coef_made, k // 2 + 1)
                for q in range(KW):
                    mm = pe.matmul(half(k // 2, k % 2), f_c[:, q, k, :], f_w[:, q, :], start=q == 0, stop=q == KW - 1)
                if k % 2:
                    mm.then_inc(w_made, 1)
            for d in range(DC):
                for c in range(DC):
                    mm = pe.matmul(half(4, d), w_vT_f[:, c, d * P:d * P + P], w_out_f[:, c, :], start=c == 0, stop=c == 1)
            mm.then_inc(w_made, 1)
            pe.wait_ge(coef_made, KC // 2 + 1)
            for c in range(DC):
                mm = pe.matmul(half(5, 0), bv_b[:, c, :], w_out_f[:, c, :], start=c == 0, stop=c == 1)
            mm.then_inc(w_made, 1)
            all_meet(pe, 1)

            def phase_a(b, d):
                for c in range(DC):
                    pe.matmul(bank[4 + c][:, 0:D + 1], zeros[:, 0:P], zeros[:, 0:D + 1], start=True, stop=False,
                              skip_group_check=True)

                def step_a(i, n):
                    g = b * TILES + i
                    if n < TILES:
                        s, par = n % 4, n // 4 % 2
                        if s == 0:
                            pe.wait_ge(x_hi_done, g + 4)
                            pe.wait_ge(x_lo_done, g + 4)
                        if n >= 2:
                            pe.wait_ge(h_kept, g - 1)
                        o = half(n % 2, 0)
                        for k in range(KC):
                            at = k % 4 * XQ + (2 * s + k // 4) * V
                            hi, lo = x_hi[:, par, at:at + P], x_lo[:, par, at:at + P]
                            mm = three(pe, o, hi, lo, w_tok[:, 0, k, :], w_tok[:, 1, k, :], k == 0, k == KC - 1)
                        mm.then_inc(h_made, 1)
                    if 4 <= n < TILES + 4:
                        t = g - 4
                        pe.wait_ge(xn_made, t + 1)
                        if n >= 6:
                            pe.wait_ge(xnT_lo_made, t - 1)
                        for d in range(DC):
                            mm = pe.transpose(half((2, 7)[n % 2], 0)[:, d * P:d * P + P], xn32[:, n % 4, d * P:d * P + P],
                                              ident[:, :])
                        mm.then_inc(xn_turned, 1)
                    if 5 <= n < TILES + 5:
                        t = g - 5
                        pe.wait_ge(xnT_hi_made, t + 1)
                        pe.wait_ge(xnT_lo_made, t + 1)
                        if n >= 7:
                            pe.wait_ge(k2_made, t - 1)
                        o = half((3, 6)[(n - 5) % 2], 0)
                        for d in range(DC):
                            hi, lo = [xnT[:, x, d, ds((i - 5) * P, P)] for x in range(2)]
                            three(pe, o, hi, lo, w_k[:, 0, d, :], w_k[:, 1, d, :], d == 0, False)
                        pe.matmul(o, first2[:, :], row_k[:, :], start=False, stop=True).then_inc(k_made, 1)
                    if n >= 6:
                        t, s, r = g - 6, (n - 6) % 2, (n - 6) % 8
                        pe.wait_ge(k2_hi_made, t + 1)
                        pe.wait_ge(k2_lo_made, t + 1)
                        for c in range(DC):
                            hi, lo = [k[:, s, c * P:c * P + P] for k in (k2_hi, k2_lo)]
                            mm = three(pe, bank[4 + c][:, 0:D + 1], hi, lo, xn_hi[:, r, 0:D + 1], xn_lo[:, r, 0:D + 1],
                                       False, n == TILES + 5, free=True)
                        mm.then_inc(kx_added, 1)
                run(pe, step_a, LAST_A)
                all_meet(pe, 2 + 3 * b)

            def phase_b(b):
                def queries(first, before):
                    pe.wait_ge(q2_made, before)
                    for f in range(DC):
                        for d in range(DC):
                            hi, lo = [xnT[:, x, d, ds(first * P, CT)] for x in range(2)]
                            w_hi, w_lo = [w_q[:, x, d, f * P:f * P + P] for x in range(2)]
                            mm = three(pe, bank[6 + f][:, :], w_hi, w_lo, hi, lo, d == 0, d == 1)
                    mm.then_inc(q_made, 1)

                queries(0, b * CHUNKS)
                pe.wait_ge(kx_kept, b + 1)
                for c in range(DC):
                    for d in range(DC):
                        mm = pe.transpose(bank[0][:, d * D + c * P:d * D + c * P + P], kxs[:, c, d * P:d * P + P],
                                          ident[:, :])
                mm.then_inc(kx_turned, 1)
                for c in range(DC):
                    mm = pe.matmul(bank[2][:, 2 * c:2 * c + 2], k4acc[:, c * P:c * P + P], ones32[:, :], start=True, stop=True)
                mm.then_inc(norms_made, 1)
                pe.wait_ge(kxT_kept, b + 1)
                for c in range(DC):
                    for d in range(DC):
                        mm = pe.matmul(half(1, c), kxT[:, d * D + c * P:d * D + c * P + P], w_vo32[:, d, :],
                                       start=d == 0, stop=d == 1)
                mm.then_inc(m_summed, 1)
                pe.wait_ge(m_ready, b + 1)

                def step_b(i, n):
                    g = b * TILES + i
                    def turn_and_route():
                        if 6 <= n < TILES + 6:
                            t = g - 6
                            pe.wait_ge(xn2_lo_made, t + 1)
                            if n >= 7:
                                pe.wait_ge(xn2T_made, t)
                            if n == 6 or n < TILES and n % 4 == 1:
                                pe.wait_ge(q_rooted, step_chunk(b, i) + 1)
                            o = half(4, 0).bitcast(F16)
                            for x in range(4):
                                mm = pe.transpose(o[:, x * P:x * P + P], xn2[:, (n - 6) % 8, x * P:x * P + P], ident16[:, :])
                            mm.then_inc(xn2_turned, 1)
                        if 7 <= n < TILES + 7:
                            t, s, r = g - 7, (n - 7) % 2, (n - 7) % 4
                            pe.wait_ge(xn2T_made, t + 1)
                            if n >= 11 and r == 0:
                                pe.wait_ge(logits_read, b * CHUNKS + (i - 11) // 4 + 1)
                            o = bank[5][:, E * r:E * r + E]
                            for d in range(DC):
                                hi, lo = [xn2T[:, s, (2 * x + d) * P:(2 * x + d) * P + P] for x in range(2)]
                                mm = three(pe, o, hi, lo, w_r[:, 0, d, :], w_r[:, 1, d, :], d == 0, d == 1)
                            mm.then_inc(logits_made, 1)
                    if n >= TILES:
                        turn_and_route()
                    if n < TILES:
                        s, u = n % 4, n % 2
                        if s == 0:
                            if n + 4 < TILES:
                                queries(i + 4, step_chunk(b, i) + 1)
                            turn_and_route()
                            pe.wait_ge(q4_split, step_chunk(b, i) + 1)
                            if n >= 8:
                                pe.wait_ge(xn2T_made, g - 5)
                            for t in range(4):
                                o = bank[4][:, D + 2 * t:D + 2 * t + 2]
                                pe.matmul(o, q4_hi[:, t * P:t * P + P], ones_r[:, :], start=True, stop=False)
                                mm = pe.matmul(o, q4_lo[:, t * P:t * P + P], ones_r[:, :], start=False, stop=True)
                            mm.then_inc(s4_made, 1)
                            pe.wait_ge(q2_split, step_chunk(b, i) + 1)
                        if n >= 2:
                            pe.wait_ge(p2_used, g - 1)
                        o = half(1 + u, 0)
                        for c in range(DC):
                            hi, lo = [q[:, c, s * P:s * P + P] for q in (q2_hi, q2_lo)]
                            mm = three(pe, o, hi, lo, m_at[:, 0, c, :], m_at[:, 1, c, :], c == 0, c == 1)
                        mm.then_inc(p2_made, 1)
                        if n >= 2:
                            pe.wait_ge(p1_used, g - 1)
                        o = half(3 * u, 0)
                        for d in range(DC):
                            hi, lo = [xnT[:, x, d, ds(i * P, P)] for x in range(2)]
                            three(pe, o, hi, lo, w_vo[:, 0, d, :], w_vo[:, 1, d, :], d == 0, False)
                        pe.matmul(o, first2[:, :], row_o[:, :], start=False, stop=True).then_inc(p1_made, 1)
                        if s != 0:
                            turn_and_route()
                        if n >= 11 and s == 3:
                            ranks(b, i, u)
                    if n >= TILES and n % 4 == 3:
                        pe.wait_ge(p1_used, (b + 1) * TILES)
                        ranks(b, i, n % 2)

                def ranks(b, i, u):
                    pe.wait_ge(sel_made, b * CHUNKS + (i - 11) // 4 + 1)
                    pe.wait_ge(before_made, b * CHUNKS + (i - 11) // 4)
                    o = bank[3 * u][:, D:D + 4 * E].rearrange("p (t e) -> p t e", e=E)
                    pe.matmul(o, earlier[:, :], sel[:, :, :], start=True, stop=False)
                    for t in range(3):
                        pe.matmul(o[:, t + 1:4, :], ones16[:, :], sel[:, t, :].unsqueeze(1).to_broadcast([P, 3 - t, E]),
                                  start=False, stop=False)
                    pe.matmul(o, ones16[:, :], before[:, :].unsqueeze(1).to_broadcast([P, 4, E]), start=False, stop=True)\
                      .then_inc(ranks_made, 1)

                def step_chunk(b, i):
                    return b * CHUNKS + i // 4

                run(pe, step_b, LAST_B, TILES - 8)
                pe.wait_ge(before_made, (b + 1) * CHUNKS)
                pe.matmul(bank[5][:, 0:E], ones16[:, :], before[:, :], start=True, stop=True).then_inc(counts_made, 1)
                all_meet(pe, 3 + 3 * b)

            def phase_c(b):
                pe.wait_ge(ids_read, b + 1)
                for hh in range(2):
                    mm = pe.transpose(bank[7][:, hh * P:hh * P + P], ids_rows32[:, hh * P:hh * P + P], ident[:, :])
                mm.then_inc(ids_turned, 1)
                pe.wait_ge(blocks_made, b + 1)

                def turn(i, n):
                    if n >= UC or not isinstance(i, int):
                        pe.wait_ge(xT_made, b * NBLOCKS + i)
                    elif n >= 1:
                        pe.wait_ge(xT_made, b * NBLOCKS + i)
                    pe.wait_ge(xg_in[n % UC], 32 * (b * (NBLOCKS // UC) + i // UC) + 32 if isinstance(i, int)
                               else 32 * (b * (NBLOCKS // UC)) + 32 + i // UC * 32)
                    o = bank[0][:, :].bitcast(F16)
                    for hh in range(2):
                        for x in range(4):
                            mm = pe.transpose(o[:, x * BLOCK + hh * P:x * BLOCK + hh * P + P],
                                              xg[n % UC][:, hh, x * P:x * P + P], ident16[:, :])
                    mm.then_inc(xg_turned, 1)

                def expert(i):
                    return pe.value_load(blk_e[0:1, ds(i, 1)], min_val=0, max_val=E - 1)

                def up(i, n, e):
                    s = n % UC
                    pe.wait_ge(xT_made, b * NBLOCKS + i + 1)
                    if n >= UC:
                        pe.wait_ge(gelu_made, b * NBLOCKS + i - UC + 1)
                    for f in range(DC):
                        for d in range(DC):
                            w_hi, w_lo = [w_1[:, x, ds(e, 1), d, f * P:f * P + P].rearrange("p o n -> p (o n)")
                                          for x in range(2)]
                            mm = three(pe, half(1 + s, f), w_hi, w_lo, xT[s][:, d, :], xT[s][:, 2 + d, :],
                                       d == 0, d == 1)
                    mm.then_inc(up_made, 1)

                def down(i, n, e):
                    s = n % UC
                    pe.wait_ge(g_split, b * NBLOCKS + i + 1)
                    if n >= UC:
                        pe.wait_ge(y_made, b * NBLOCKS + i - UC + 1)
                    for hh in range(2):
                        o = half(4 + s, hh)
                        for f in range(DC):
                            hi, lo = [x[s][:, f * BLOCK + hh * P:f * BLOCK + hh * P + P] for x in (g_hi, g_lo)]
                            w_hi, w_lo = [w_2[:, x, ds(e, 1), f, :].rearrange("p o n -> p (o n)") for x in range(2)]
                            three(pe, o, hi, lo, w_hi, w_lo, f == 0, False)
                        mm = pe.matmul(o, first2[:, :], row_2[:, ds(e, 1), :].rearrange("p o n -> p (o n)"),
                                       start=False, stop=True)
                    mm.then_inc(down_made, 1)

                def blocks(i, n, count):
                    e = {}
                    for k in range(count):
                        if n + k < NBLOCKS:
                            turn(i + k, n + k)
                        for m in (k - 1, k - 2):
                            if m not in e and 0 <= n + m < NBLOCKS:
                                e[m] = expert(i + m)
                        if 1 <= n + k <= NBLOCKS:
                            up(i + k - 1, n + k - 1, e[k - 1])
                        if n + k >= 2:
                            down(i + k - 2, n + k - 2, e[k - 2])

                blocks(0, 0, UC)
                blocks(UC, UC, UC)
                with pe.Fori(2, NBLOCKS // UC) as it:
                    blocks(it * UC, 2 * UC, UC)
                blocks(NBLOCKS, NBLOCKS, 2)
                all_meet(pe, 4 + 3 * b)
            def phase_d(b):
                all_meet(pe, 5 + 3 * b)
            batches(pe, phase_a, phase_b, phase_c, phase_d)

        @block.scalar
        def _(act):
            def w_tok_high(j):
                act.wait_ge(w_made, j + 1)
                for k in (2 * j, 2 * j + 1):
                    ins = act.activation(w_tok[:, 0, k, :], half(j, k % 2), ACT.Copy)
                ins.then_inc(w_kept, 1)

            act.wait_ge(loaded2, 32)
            act.activation(w_1[:, 0], h[:, 0:16, :].rearrange("p (e c) d -> p e c d", e=E), ACT.Copy, scale=WS)\
               .then_inc(w_12_high, 1)
            act.activation(w_2[:, 0], h[:, 16:32, :].rearrange("p (e c) d -> p e c d", e=E), ACT.Copy, scale=WS)\
               .then_inc(w_12_high, 1)
            w_tok_high(0)
            w_tok_high(1)
            for q in range(4):
                act.wait_ge(x_in[q], 16)
                act.activation(x_hi[:, 0, q * XQ:(q + 1) * XQ], x_raw[:, q, :], ACT.Copy).then_inc(x_hi_done, 1)
            w_tok_high(2)
            w_tok_high(3)
            act.wait_ge(w_made, KC // 2 + 2)
            act.activation(w_vo32[:], bank[4][:, :].rearrange("p (c n) -> p c n", c=DC), ACT.Copy)
            act.activation(bvo[:], half(5, 0), ACT.Copy).then_inc(w_kept, 1)
            all_meet(act, 1)

            def phase_a(b, d):
                def step_a(i, n):
                    g = b * TILES + i
                    if 4 <= n < TILES + 4:
                        t, s = g - 4, n % 4
                        act.wait_ge(rstd_made, chunk_of(b, i, n))
                        if n >= 8:
                            act.wait_ge(xn_turned, t - 3)
                            act.wait_ge(xn_lo_made, t - 3)
                        settled(act)
                        act.activation(xn32[:, s, :], h[:, ds(i - 4, 1), :].rearrange("p o d -> p (o d)"), ACT.Identity,
                                       scale=rstd[:, s:s + 1], bias=norm_by[:, 1, s:s + 1]).then_inc(xn_made, 1)
                        act.wait_ge(xn_made, t + 1)
                        act.activation(xn_hi[:, (n - 4) % 8, 0:D], xn32[:, s, :], ACT.Copy).then_inc(xn_hi_made, 1)
                    if n >= 6:
                        t, s = g - 6, (n - 6) % 2
                        act.wait_ge(k_scaled, t + 1)
                        if n >= 8:
                            act.wait_ge(kx_added, t - 1)
                        act.activation(k2_hi[:, s, :], k2[:, s, :], ACT.Copy, scale=k_scale[:, s:s + 1]).then_inc(k2_hi_made, 1)
                        if n >= 8:
                            act.wait_ge(k4_added, t - 1)
                        act.activation(k4[:, s, :], k2[:, s, :], ACT.Square, scale=k_scale[:, s:s + 1]).then_inc(k4_made, 1)
                    if n < TILES:
                        q, par = n % 4, n // 4 % 2
                        act.wait_ge(x_in[q], quarter_in(b, i, n))
                        act.wait_ge(h_made, g - q)
                        act.activation(x_hi[:, 1 - par, q * XQ:(q + 1) * XQ], x_raw[:, q, :], ACT.Copy)\
                           .then_inc(x_hi_done, 1)
                        act.wait_ge(h_made, g + 1)
                        if d is not None:
                            act.wait_ge(out_stored[n % 4], 16 * (d * CHUNKS + i // 4) + 16)
                        act.activation(h[:, ds(i, 1), :].rearrange("p o d -> p (o d)"), half(n % 2, 0), ACT.Copy)\
                           .then_inc(h_kept, 1)
                    if 4 <= n < TILES + 4:
                        t = g - 4
                        act.wait_ge(xn_turned, t + 1)
                        act.activation(xnT[:, 0, :, ds((i - 4) * P, P)],
                                       half((2, 7)[n % 2], 0).rearrange("p (c t) -> p c t", c=DC), ACT.Copy).then_inc(xnT_hi_made, 1)
                    if n % 4 == 3 and n < TILES:
                        act.wait_ge(var_made, chunk_of(b, i, n) + 1)
                        act.activation(sd[:, :], mv[:, :, 1], ACT.Sqrt, bias=eps_ln[:, 0:1]).then_inc(sd_made, 1)
                    if 5 <= n < TILES + 5:
                        t, s = g - 5, (n - 5) % 2
                        act.wait_ge(k_made, t + 1)
                        if n >= 7:
                            act.wait_ge(k2_lo_made, t - 1)
                        act.activation(k2[:, s, :], half((3, 6)[s], 0), ACT.Square, scale=1.0 / WS, accum_out=k2s[:, s:s + 1])\
                           .then_inc(k2_made, 1)
                run(act, step_a, LAST_A)
                all_meet(act, 2 + 3 * b)

            def phase_b(b):
                def squares(G):
                    act.wait_ge(q_made, G + 1)
                    act.wait_ge(q2_split, G)
                    for f in range(DC):
                        ins = act.activation(q2[:, f, :], bank[6 + f][:, :], ACT.Square, scale=1.0 / WS, bias=col_q[:, f:f + 1])
                    ins.then_inc(q2_made, 1)

                def fourth_powers(G):
                    act.wait_ge(q2_made, G + 1)
                    act.activation(q4[:].rearrange("p c t -> p (c t)"), q2[:].rearrange("p c t -> p (c t)"), ACT.Square)\
                       .then_inc(q4_made, 1)

                def q4_high(G):
                    act.wait_ge(s4_made, G)
                    act.wait_ge(q4_summed, G + 1)
                    act.activation(q4_hi, q4s[:], ACT.Copy).then_inc(q4_hi_made, 1)

                def q2_high(G):
                    act.wait_ge(p2_made, G * 4)
                    act.activation(q2_hi, q2[:], ACT.Copy).then_inc(q2_hi_made, 1)

                squares(b * CHUNKS)
                fourth_powers(b * CHUNKS)
                act.wait_ge(kx_turned, b + 1)
                act.activation(kxT[:], bank[0][:, :], ACT.Copy).then_inc(kxT_kept, 1)
                act.wait_ge(norms_made, b + 1)
                act.activation(minv[:, 0, :], bank[2][:, 0:4:2], ACT.Sqrt).then_inc(norms_rooted, 1)
                q4_high(b * CHUNKS)
                q2_high(b * CHUNKS)

                def step_b(i, n):
                    g = b * TILES + i

                    t, s = g - 4, n % 4
                    tile_here = 4 <= n < TILES + 4

                    def normalise():
                        if n >= 8:
                            act.wait_ge(xn2_lo_made, t - 3)
                        settled(act)
                        act.activation(xn2_32[:, s, :], h[:, ds(i - 4, 1), :].rearrange("p o d -> p (o d)"), ACT.Identity,
                                       scale=rstd[:, s:s + 1], bias=norm_by[:, 1, s:s + 1]).then_inc(xn2_made, 1)
                        if n >= 8:
                            act.wait_ge(xn2_stored[(n - 4) % 8], 16 * (b * (TILES // 8)) + 16 * ((i - 4) // 8))
                            settled(act)
                        hi_ = h[:, ds(i - 4, 1), :].rearrange("p o d -> p (o d)")
                        act.activation(hi_, hi_, ACT.Identity, scale=norm_by[:, 0, s:s + 1], bias=norm_by[:, 1, s:s + 1])\
                           .then_inc(h_added, 1)
                        act.wait_ge(xn2_made, t + 1)
                        act.activation(xn2[:, (n - 4) % 8, 0:D], xn2_32[:, s, :], ACT.Copy).then_inc(xn2_hi_made, 1)

                    def keep_turned():
                        if 6 <= n < TILES + 6:
                            act.wait_ge(xn2_turned, g - 5)
                            if n >= 8:
                                act.wait_ge(logits_made, g - 7)
                            act.activation(xn2T[:, (n - 6) % 2, :], half(4, 0).bitcast(F16), ACT.Copy).then_inc(xn2T_made, 1)

                    if n >= TILES or s == 0:
                        keep_turned()
                    if tile_here and s != 0:
                        normalise()
                    if s == 0 and n + 4 < TILES:
                        squares(chunk_of(b, i, n) + 1)
                    if n < TILES and s == 0:
                        act.wait_ge(s4_made, chunk_of(b, i, n) + 1)
                        if n >= 4:
                            act.wait_ge(p2_used, g - 3)
                        act.activation(q_n[:, :], bank[4][:, D:D + 8:2], ACT.Sqrt).then_inc(q_rooted, 1)
                    if s == 0 and n + 4 < TILES:
                        fourth_powers(chunk_of(b, i, n) + 1)
                    if tile_here and s == 0:
                        act.wait_ge(var2_made, chunk_of(b, i, n))
                        act.activation(sd[:, :], mv[:, :, 1], ACT.Sqrt, bias=eps_ln[:, 0:1]).then_inc(sd2_made, 1)
                        act.wait_ge(rstd2_made, chunk_of(b, i, n))
                        normalise()
                    if s == 3 and n + 4 < TILES + 3:
                        q2_high(chunk_of(b, i, n) + 1)
                        q4_high(chunk_of(b, i, n) + 1)
                    if n < TILES and s != 0:
                        keep_turned()
                run(act, step_b, LAST_B, TILES - 8)
                act.wait_ge(slots_made, CHUNKS * (b + 1))
                act.activation(gate[:, 0, :], gap[:, :], ACT.Exp, scale=-1.0 / WS).then_inc(exp_made, 1)
                all_meet(act, 3 + 3 * b)

            def phase_c(b):
                act.wait_ge(blocks_made, b + 1)
                settled(act)

                def step_c(i, n):
                    if n < NBLOCKS:
                        s = n % UC
                        e = act.value_load(blk_e[0:1, ds(i, 1)], min_val=0, max_val=E - 1)
                        act.wait_ge(up_made, b * NBLOCKS + i + 1)
                        if n >= UC:
                            act.wait_ge(y_stored[s], 16 * (b * (NBLOCKS // UC)) + 16 * (i // UC))
                        for f in range(DC):
                            ins = act.activation(g32[s][:, f * BLOCK:f * BLOCK + BLOCK], half(1 + s, f), ACT.Gelu,
                                                 scale=1.0 / WS,
                                                 bias=col_1[:, ds(e, 1), f:f + 1].rearrange("p o n -> p (o n)"))
                        ins.then_inc(gelu_made, 1)
                    if n >= 1:
                        s = (n - 1) % UC
                        act.wait_ge(down_made, b * NBLOCKS + i - 1 + 1)
                        act.activation(g32[s][:, :], bank[4 + s][:, :], ACT.Copy, scale=1.0 / WS).then_inc(y_made, 1)
                run_c(act, step_c, NBLOCKS + 1)
                all_meet(act, 4 + 3 * b)

            def phase_d(b):
                all_meet(act, 5 + 3 * b)
            batches(act, phase_a, phase_b, phase_c, phase_d)

        @block.vector
        def _(dve):
            f_c = xnT[:].rearrange("p a c t -> p (a c t)").bitcast(F32)
            coef = x_raw[:, 0, 128:256]
            pair = x_raw[:, 0, 256:320]
            dve.memset(ones_r[:, :].bitcast(F32), 1.0)
            dve.memset(ones32[:, :], 1.0)
            dve.memset(ones16[:, :], 1.0)
            dve.memset(zeros[:, :], 0.0)
            dve.memset(eps_ln[:, :], EPS_LN)
            dve.drain()
            dve.wait_ge(coef_loaded, 64)
            dve.tensor_copy(ident16[:, :], ident[:, :])
            dve.tensor_copy(earlier[:, :], x_raw[:, 0, 0:P])
            for j in range(KC // 2):
                t = PATCH // (KC // 2)
                dve.tensor_tensor(f_c.rearrange("p (q t c) -> p q t c", q=KW, c=C)[:, :, j * t:j * t + t, :],
                                  coef.rearrange("p (q t) -> p q t", q=KW)[:, :, j * t:j * t + t]
                                  .unsqueeze(3).to_broadcast([P, KW, t, C]),
                                  pair.unsqueeze(1).unsqueeze(1).to_broadcast([P, KW, t, C]), ALU.mult).then_inc(coef_made, 1)
            dve.wait_ge(loaded, 16 * SETUP_LOADS)
            bv_col = scr[:, 5648:5652]
            for c in range(DC):
                ins = dve.tensor_copy(scr[:, 5652 + c * P:5652 + c * P + P], bv_col[:, 2 + c:3 + c].to_broadcast([P, P]))
            ins.then_inc(coef_made, 1)
            dve.tensor_scalar(first2[:, :], ones16[:, :], pick[:, 0:1], None, ALU.mult)
            dve.drain()
            dve.scalar_tensor_tensor(out=first2[:, :], in0=ones16[:, :], scalar=pick[:, 1:2], in1=first2[:, :],
                                     op0=ALU.mult, op1=ALU.add)
            w_qkv = scr[:, 2048:3584].rearrange("p (c n) -> p c n", c=DC)
            w_r32 = scr[:, 4608:4624].rearrange("p (c n) -> p c n", c=DC)
            b_qkv = scr[:, 4624:5392]
            b_out = scr[:, 5392:5648]
            means = w_means
            tmp = scr[:, 2304:2560]

            for x in range(2):
                for c in range(DC):
                    dve.tensor_reduce(means[:, 2 * x + c:2 * x + c + 1], w_qkv[:, c, x * D:x * D + D], AX.X, ALU.add)
                dve.tensor_reduce(means[:, 4 + x:5 + x], b_qkv[:, x * D:x * D + D], AX.X, ALU.add)
            dve.drain()
            dve.tensor_scalar(means[:, 0:6], means[:, 0:6], 1.0 / D, None, ALU.mult)
            dve.drain()
            for x, w in ((0, w_q), (1, w_k)):
                for c in range(DC):
                    dve.tensor_scalar(w_qkv[:, c, x * D:x * D + D], w_qkv[:, c, x * D:x * D + D],
                                      means[:, 2 * x + c:2 * x + c + 1], WS, ALU.subtract, ALU.mult)
            dve.tensor_scalar(w_r32, w_r32, WS, None, ALU.mult)
            dve.tensor_scalar(b_qkv[:, D:2 * D], b_qkv[:, D:2 * D], means[:, 5:6], WS, ALU.subtract, ALU.mult)
            dve.tensor_scalar(col_q[:, :], bv_col[:, 0:2], means[:, 4:5], None, ALU.subtract)
            dve.drain()

            def split(hi, lo, x):
                dve.drain()
                dve.tensor_copy(hi, x)
                dve.drain()
                dve.tensor_tensor(lo, x, hi, ALU.subtract)

            def rows(o, x, hi, lo):
                split(hi, lo, x)
                dve.drain()
                dve.tensor_scalar(o, hi, pick[:, 0:1], None, ALU.mult)
                dve.drain()
                dve.scalar_tensor_tensor(out=o, in0=lo, scalar=pick[:, 1:2], in1=o, op0=ALU.mult, op1=ALU.add)
            split(w_q[:, 0], w_q[:, 1], w_qkv[:, :, 0:D])
            split(w_k[:, 0], w_k[:, 1], w_qkv[:, :, D:2 * D])
            split(w_r[:, 0], w_r[:, 1], w_r32)
            hi16, lo16 = [scr[:, 2048 + 128 * x:2176 + 128 * x].bitcast(F16) for x in range(2)]
            dve.drain()
            rows(row_k[:, :], b_qkv[:, D:2 * D], hi16, lo16)

            def w_tok_low(j):
                dve.wait_ge(w_kept, j + 1)
                for k in (2 * j, 2 * j + 1):
                    dve.tensor_tensor(w_tok[:, 1, k, :], half(j, k % 2), w_tok[:, 0, k, :].bitcast(F32), ALU.subtract)

            def w_12_low(x, w):
                dve.wait_ge(w_12_high, x + 1)
                dve.scalar_tensor_tensor(out=w[:, 1].rearrange("p e c d -> p (e c d)"),
                                         in0=h[:, 16 * x:16 * x + 16, :].rearrange("p t d -> p (t d)"), scalar=WS,
                                         in1=w[:, 0].rearrange("p e c d -> p (e c d)"), op0=ALU.mult, op1=ALU.subtract)
            w_12_low(0, w_1)
            w_12_low(1, w_2)
            dve.drain()
            dve.memset(h[:, 8:10, :].bitcast(U32), 0).then_inc(h_free, 1)
            w_tok_low(0)
            w_tok_low(1)
            for q in range(4):
                dve.wait_ge(x_hi_done, q + 1)
                dve.tensor_tensor(x_lo[:, 0, q * XQ:(q + 1) * XQ], x_raw[:, q, :],
                                  x_hi[:, 0, q * XQ:(q + 1) * XQ].bitcast(F32), ALU.subtract).then_inc(x_lo_done, 1)
            dve.wait_ge(loaded2, 64)
            b2 = h[:, 0:8, :].rearrange("p t d -> p (t d)")
            dve.tensor_scalar(b2, b2, WS, None, ALU.mult)
            dve.drain()
            rows(row_2[:].rearrange("p e d -> p (e d)"), b2, h[:, 10:14, :].rearrange("p t d -> p (t d)").bitcast(F16),
                 h[:, 14:18, :].rearrange("p t d -> p (t d)").bitcast(F16))
            w_tok_low(2)
            w_tok_low(3)
            dve.wait_ge(w_kept, KC // 2 + 1)
            dve.tensor_scalar(scr[:, 3072:3584], w_vo32[:].rearrange("p c n -> p (c n)"), WS, None, ALU.mult)
            dve.tensor_tensor(tmp, bvo[:, :], b_out, ALU.add)
            dve.drain()
            dve.tensor_scalar(tmp, tmp, WS, None, ALU.mult)
            dve.drain()
            split(w_vo[:, 0], w_vo[:, 1], scr[:, 3072:3584].rearrange("p (c n) -> p c n", c=DC))
            rows(row_o[:, :], tmp, hi16, lo16)
            all_meet(dve, 1)

            def variances(made):
                dve.drain()
                for s in range(4):
                    ins = dve.bn_aggr(mv[:, s, :], st[:, s, :])
                ins.then_inc(made, 1)

            def scales(rooted, value, made):
                dve.wait_ge(rooted, value)
                dve.reciprocal(rstd[:, :], sd[:, :])
                dve.drain()
                dve.tensor_scalar(norm_by[:, 0, :], rstd[:, :], 1.0, None, ALU.add)
                dve.scalar_tensor_tensor(out=norm_by[:, 1, :], in0=mv[:, :, 0], scalar=-1.0, in1=rstd[:, :],
                                         op0=ALU.mult, op1=ALU.mult).then_inc(made, 1)

            def add_first(d, t, n, y, y_sem, deep):
                hi_ = h[:, ds(t, 1), :].rearrange("p o d -> p (o d)")
                dve.wait_ge(y_sem[n % deep], results_in(d, t, deep))
                dve.scalar_tensor_tensor(out=hi_, in0=y[n % deep][0], scalar=gate[:, 1, ds(t, 1)], in1=hi_,
                                         op0=ALU.mult, op1=ALU.add).then_inc(first_added, 1)

            def add_second(d, t, n, y, deep):
                hi_ = h[:, ds(t, 1), :].rearrange("p o d -> p (o d)")
                dve.wait_ge(first_added, d * TILES + t + 1)
                dve.scalar_tensor_tensor(out=hi_, in0=y[n % deep][1], scalar=gate[:, 2, ds(t, 1)], in1=hi_,
                                         op0=ALU.mult, op1=ALU.add).then_inc(out_made, 1)

            def phase_a(b, d):
                def step_a(i, n):
                    g = b * TILES + i
                    if 4 <= n < TILES + 4:
                        t = g - 4
                        dve.wait_ge(xn_hi_made, t + 1)
                        dve.tensor_tensor(xn_lo[:, (n - 4) % 8, 0:D], xn32[:, n % 4, :], xn_hi[:, (n - 4) % 8, 0:D],
                                          ALU.subtract).then_inc(xn_lo_made, 1)
                    if 6 <= n < TILES + 6:
                        t, s = g - 6, (n - 6) % 2
                        dve.wait_ge(k2_hi_made, t + 1)
                        dve.scalar_tensor_tensor(out=k2_lo[:, s, :], in0=k2[:, s, :], scalar=k_scale[:, s:s + 1],
                                                 in1=k2_hi[:, s, :], op0=ALU.mult, op1=ALU.subtract).then_inc(k2_lo_made, 1)
                    if d is not None and n < TILES - 1:
                        add_first(d, i + 1, n + 1, yg, y_in, 2)
                    if n < TILES:
                        q, par = n % 4, n // 4 % 2
                        dve.wait_ge(x_hi_done, 4 * chunk_of(b, i, n) + 4 + q + 1)
                        dve.tensor_tensor(x_lo[:, 1 - par, q * XQ:(q + 1) * XQ], x_raw[:, q, :],
                                          x_hi[:, 1 - par, q * XQ:(q + 1) * XQ].bitcast(F32), ALU.subtract)\
                           .then_inc(x_lo_done, 1)
                    if d is not None and n < TILES - 1:
                        add_second(d, i + 1, n + 1, yg, 2)
                    if n < TILES:
                        dve.wait_ge(h_kept, g + 1)
                        settled(dve)
                        dve.bn_stats(st[:, n % 4, :], h[:, ds(i, 1), :].rearrange("p o d -> p (o d)"))
                    if n % 4 == 3 and n < TILES:
                        variances(var_made)
                    if 4 <= n < TILES + 4:
                        t = g - 4
                        dve.wait_ge(xnT_hi_made, t + 1)
                        dve.tensor_tensor(xnT[:, 1, :, ds((i - 4) * P, P)],
                                          half((2, 7)[n % 2], 0).rearrange("p (c t) -> p c t", c=DC),
                                          xnT[:, 0, :, ds((i - 4) * P, P)], ALU.subtract).then_inc(xnT_lo_made, 1)
                    if n % 4 == 3 and n < TILES:
                        if n >= 7:
                            dve.wait_ge(xn_made, g - 3)
                        scales(sd_made, chunk_of(b, i, n) + 1, rstd_made)
                    if 5 <= n < TILES + 5:
                        t, s = g - 5, (n - 5) % 2
                        dve.wait_ge(k2_made, t + 1)
                        dve.tensor_scalar(k_eps[:, :], k2s[:, s:s + 1], EPS_DIV, 1.0 / KS, ALU.add, ALU.mult)
                        dve.drain()
                        if n >= 7:
                            dve.wait_ge(k4_made, t - 1)
                        dve.reciprocal(k_scale[:, s:s + 1], k_eps[:, :]).then_inc(k_scaled, 1)
                dve.memset(xn_hi[:, :, D:D + 1], 1.0)
                dve.memset(xn_lo[:, :, D:D + 1], 0.0)
                if d is not None:
                    add_first(d, 0, 0, yg, y_in, 2)
                    add_second(d, 0, 0, yg, 2)
                run(dve, step_a, LAST_A, TILES if d is None else TILES - 8)
                all_meet(dve, 2 + 3 * b)

            def phase_b(b):
                def sum_q4(G):
                    dve.wait_ge(q4_made, G + 1)
                    dve.tensor_tensor(q4s[:], q4[:, 0, :], q4[:, 1, :], ALU.add).then_inc(q4_summed, 1)

                def q4_low(G):
                    dve.wait_ge(q4_hi_made, G + 1)
                    dve.tensor_tensor(q4_lo, q4s[:], q4_hi.bitcast(F32), ALU.subtract).then_inc(q4_split, 1)

                def q2_low(G):
                    dve.wait_ge(q2_hi_made, G + 1)
                    dve.tensor_tensor(q2_lo, q2[:], q2_hi.bitcast(F32), ALU.subtract).then_inc(q2_split, 1)

                for c in range(DC):
                    ins = dve.tensor_copy(kxs[:, c, :], bank[4 + c][:, 0:D + 1])
                ins.then_inc(kx_kept, 1)
                dve.memset(before[:, :], 0.0)
                dve.tensor_copy(ids_f[:, :], ids_0[:, :])
                sum_q4(b * CHUNKS)
                dve.wait_ge(norms_rooted, b + 1)
                dve.tensor_scalar(minv[:, 1, :], minv[:, 0, :], 1.0 / KS, EPS_NORM, ALU.mult, ALU.max)
                dve.drain()
                dve.reciprocal(minv[:, 0, :], minv[:, 1, :])
                dve.drain()
                dve.tensor_scalar(minv[:, 1, :], minv[:, 0, :], 1.0 / (KS * float(NT) ** 0.5), None, ALU.mult)
                dve.wait_ge(m_summed, b + 1)
                for c in range(DC):
                    dve.scalar_tensor_tensor(out=m32[:, c, :], in0=bvo[:, :], scalar=kxs[:, c, D:D + 1], in1=half(1, c),
                                             op0=ALU.mult, op1=ALU.add)
                dve.drain()
                for c in range(DC):
                    dve.tensor_scalar(m_at[:, 0, c, 0:D], m32[:, c, :], minv[:, 1, c:c + 1], None, ALU.mult)
                dve.drain()
                for c in range(DC):
                    ins = dve.scalar_tensor_tensor(out=m_at[:, 1, c, 0:D], in0=m32[:, c, :], scalar=minv[:, 1, c:c + 1],
                                                   in1=m_at[:, 0, c, 0:D].bitcast(F32), op0=ALU.mult, op1=ALU.subtract)
                ins.then_inc(m_ready, 1)
                q4_low(b * CHUNKS)
                q2_low(b * CHUNKS)

                def places_at(b, i, u):
                    dve.wait_ge(ranks_made, b * CHUNKS + (i - 11) // 4 + 1)
                    dve.tensor_tensor(pos[:, :, :], bank[3 * u][:, D:D + 4 * E].rearrange("p (t e) -> p t e", e=E),
                                      region0[:, :].unsqueeze(1).to_broadcast([P, 4, E]), ALU.add)

                def step_b(i, n):
                    g = b * TILES + i

                    def add_attention():
                        u = n % 2
                        dve.wait_ge(p2_made, g + 1)
                        dve.scalar_tensor_tensor(out=att[:, u, :], in0=half(1 + u, 0), scalar=r_q[:, n % 4:n % 4 + 1],
                                                 in1=h[:, ds(i, 1), :].rearrange("p o d -> p (o d)"),
                                                 op0=ALU.mult, op1=ALU.add).then_inc(p2_used, 1)

                    def scales_of_queries():
                        dve.wait_ge(q_rooted, chunk_of(b, i, n) + 1)
                        dve.tensor_scalar(q_guard[:, :], q_n[:, :], EPS_NORM * EPS_DIV, None, ALU.max)
                        dve.drain()
                        dve.reciprocal(r_q[:, :], q_guard[:, :])
                        dve.drain()

                    if n < TILES and n % 4 != 0:
                        add_attention()
                    if 1 <= n <= TILES:
                        u = (n - 1) % 2
                        hi_ = h[:, ds(i - 1, 1), :].rearrange("p o d -> p (o d)")
                        dve.wait_ge(p1_made, g)
                        dve.wait_ge(p2_used, g)
                        dve.scalar_tensor_tensor(out=hi_, in0=half(3 * u, 0), scalar=1.0 / WS, in1=att[:, u, :],
                                                 op0=ALU.mult, op1=ALU.add).then_inc(p1_used, 1)
                    if 5 <= n < TILES + 5:
                        t = g - 5
                        dve.wait_ge(xn2_hi_made, t + 1)
                        dve.tensor_tensor(xn2[:, (n - 5) % 8, D:2 * D], xn2_32[:, (n - 5) % 4, :], xn2[:, (n - 5) % 8, 0:D],
                                          ALU.subtract).then_inc(xn2_lo_made, 1)
                    if 1 <= n <= TILES:
                        dve.wait_ge(p1_used, g)
                        settled(dve)
                        dve.bn_stats(st[:, (n - 1) % 4, :], hi_)
                    if n % 4 == 0 and 4 <= n <= TILES:
                        if n >= 8:
                            dve.wait_ge(h_added, g - 4)
                            settled(dve)
                        variances(var2_made)
                    if n < TILES and n % 4 == 0:
                        scales_of_queries()
                        add_attention()
                    if n % 4 == 0 and 4 <= n <= TILES:
                        scales(sd2_made, chunk_of(b, i, n), rstd2_made)
                    if n % 4 == 2 and n + 4 < TILES + 2:
                        sum_q4(chunk_of(b, i, n) + 1)
                    if n % 4 == 2 and n >= 10:
                        G = b * CHUNKS + (i - 10) // 4
                        dve.wait_ge(logits_made, 4 * G + 4)
                        settled(dve)
                        for s in range(4):
                            dve.max(top[:, s, :], bank[5][:, E * s:E * s + E])
                        dve.drain()
                        for s in range(4):
                            ins = dve.max_index(top_i[:, s, :], top[:, s, :], bank[5][:, E * s:E * s + E])
                        ins.then_inc(logits_read, 1)
                        dve.tensor_tensor(gap[:, ds(i - 10, 4)], top[:, :, 0], top[:, :, 1], ALU.subtract)
                        dve.drain()
                        dve.tensor_copy(e_all[:, ds(i - 10, 4), :], top_i[:, :, 0:2])
                        dve.tensor_copy(e_now[:, :, :], top_i[:, :, 0:2])
                        dve.drain()
                        dve.tensor_tensor(hot[:].rearrange("p t s e -> p (t s) e"),
                                          iota_e[:, :].unsqueeze(1).to_broadcast([P, 8, E]),
                                          e_now[:].rearrange("p t s -> p (t s)").unsqueeze(2).to_broadcast([P, 8, E]),
                                          ALU.is_equal)
                        dve.drain()
                        dve.tensor_tensor(sel[:, :, :], hot[:, :, 0, :], hot[:, :, 1, :], ALU.add).then_inc(sel_made, 1)
                    if n % 4 == 3 and n + 4 < TILES + 3:
                        q2_low(chunk_of(b, i, n) + 1)
                        q4_low(chunk_of(b, i, n) + 1)
                    if n % 4 == 3 and n >= 11:
                        places_at(b, i, n % 2)
                        dve.tensor_reduce(chunk_sel[:, :], sel[:].rearrange("p t e -> p e t"), AX.X, ALU.add)
                        dve.drain()
                        dve.tensor_tensor(before[:, :], before[:, :], chunk_sel[:, :], ALU.add).then_inc(before_made, 1)
                        dve.tensor_tensor(hot_pos[:, :, :, :], hot[:, :, :, :],
                                          pos[:, :, :].unsqueeze(2).to_broadcast([P, 4, 2, E]), ALU.mult)
                        dve.drain()
                        dve.tensor_reduce(slot_f[:, :, :], hot_pos[:, :, :, :], AX.X, ALU.add)
                        dve.drain()
                        c = (n - 11) // 4 % 2
                        dve.wait_ge(ids_stored[c], 128 * (b * (CHUNKS // 2) + (i - 11) // 8))
                        dve.tensor_copy(slots[:, ds(i - 11, 4), :], slot_f[:, :, :])
                        dve.tensor_copy(id_u[:, c, :], ids_f[:, :])
                        dve.tensor_copy(slot_u[:, c, :, :], slot_f[:, :, :]).then_inc(slots_made, 1)
                        dve.tensor_scalar(ids_f[:, :], ids_f[:, :], float(CT), None, ALU.add)
                run(dve, step_b, LAST_B, TILES - 8)
                dve.wait_ge(counts_made, b + 1)
                settled(dve)
                dve.tensor_copy(cnt[:, :], bank[5][:, 0:E])
                dve.drain()
                dve.tensor_tensor(cmp_t[:, :, :], cnt[:, :].unsqueeze(2).to_broadcast([P, E, REGION]),
                                  thr[:, :].unsqueeze(1).to_broadcast([P, E, REGION]), ALU.is_gt)
                dve.drain()
                dve.tensor_reduce(n_blk[:, :], cmp_t[:, :, :], AX.X, ALU.add)
                dve.drain()
                dve.tensor_tensor(cum_m[:, :, :], n_blk[:, :].unsqueeze(1).to_broadcast([P, E, E]), upto[:, :, :], ALU.mult)
                dve.drain()
                dve.tensor_reduce(cum[:, :], cum_m[:, :, :], AX.X, ALU.add)
                dve.drain()
                dve.tensor_tensor(c_cmp[:, 0, :], ids_0[:, 0:1].to_broadcast([P, E]), cum[:, :], ALU.is_ge)
                dve.drain()
                dve.tensor_tensor(c_cmp[:, 1, :], c_cmp[:, 0, :], n_blk[:, :], ALU.mult)
                dve.drain()
                dve.tensor_reduce(c_sum[:, 0:2], c_cmp[:, :, :], AX.X, ALU.add)
                dve.drain()
                dve.tensor_tensor(c_sum[:, 2:3], ids_0[:, 0:1], c_sum[:, 1:2], ALU.subtract)
                dve.drain()
                dve.scalar_tensor_tensor(out=c_sum[:, 1:2], in0=c_sum[:, 0:1], scalar=float(REGION), in1=c_sum[:, 2:3],
                                         op0=ALU.mult, op1=ALU.add)
                dve.drain()
                dve.tensor_scalar(blk_at[:, :], c_sum[:, 1:2], float(PLACES // BLOCK - 1), None, ALU.min)\
                   .then_inc(block_rows_made, 1)
                dve.tensor_tensor(b_cmp[:, :, :], iota_b[:, :].unsqueeze(2).to_broadcast([P, NBLOCKS, E]),
                                  cum[:, :].unsqueeze(1).to_broadcast([P, NBLOCKS, E]), ALU.is_ge)
                dve.drain()
                dve.tensor_reduce(b_e[:, :], b_cmp[:, :, :], AX.X, ALU.add)
                dve.drain()
                dve.tensor_scalar(blk_e[:, :], b_e[:, :], float(E - 1), None, ALU.min).then_inc(blocks_made, 1)
                dve.wait_ge(exp_made, b + 1)
                dve.tensor_scalar(gate[:, 2, :], gate[:, 0, :], 1.0, None, ALU.add)
                dve.drain()
                dve.reciprocal(gate[:, 1, :], gate[:, 2, :])
                dve.drain()
                dve.tensor_tensor(gate[:, 2, :], gate[:, 0, :], gate[:, 1, :], ALU.mult)
                dve.tensor_tensor(e_shift[:, :], cum[:, :], n_blk[:, :], ALU.subtract)
                dve.drain()
                dve.scalar_tensor_tensor(out=e_shift[:, :], in0=e_shift[:, :], scalar=float(BLOCK), in1=region0[:, :],
                                         op0=ALU.mult, op1=ALU.subtract)
                is_e, shift = [x_raw[:, x, 0:2 * TILES * E].rearrange("p (t e) -> p t e", e=E) for x in range(2)]
                dve.tensor_tensor(is_e, iota_e[:, :].unsqueeze(1).to_broadcast([P, 2 * TILES, E]),
                                  e_all[:].rearrange("p t s -> p (t s)").unsqueeze(2).to_broadcast([P, 2 * TILES, E]),
                                  ALU.is_equal)
                dve.drain()
                dve.tensor_tensor(shift, is_e, e_shift[:, :].unsqueeze(1).to_broadcast([P, 2 * TILES, E]), ALU.mult)
                dve.drain()
                dve.tensor_reduce(x_raw[:, 2, 0:2 * TILES], shift, AX.X, ALU.add)
                dve.drain()
                dve.tensor_tensor(rows_at[:].rearrange("p t s -> p (t s)"), x_raw[:, 2, 0:2 * TILES],
                                  slots[:].rearrange("p t s -> p (t s)"), ALU.add)
                all_meet(dve, 3 + 3 * b)

            def phase_c(b):
                dve.wait_ge(ids_in, 16 * (b + 1))
                settled(dve)
                dve.tensor_copy(ids_rows32[:, :], ids_rows[:, :]).then_inc(ids_read, 1)
                dve.wait_ge(ids_turned, b + 1)
                settled(dve)
                dve.tensor_copy(ids_all[:, :, :], bank[7][:, 0:2 * P].rearrange("p (h n) -> p n h", h=2)[:, 0:NBLOCKS, :])\
                   .then_inc(ids_kept, 1)

                def step_c(i, n):
                    if n < NBLOCKS:
                        s = n % UC
                        dve.wait_ge(xg_turned, b * NBLOCKS + i + 1)
                        if n >= UC:
                            dve.wait_ge(up_made, b * NBLOCKS + i - UC + 1)
                        dve.tensor_copy(xT[s].rearrange("p c t -> p (c t)"), bank[0][:, :].bitcast(F16)).then_inc(xT_made, 1)
                    if n >= 1:
                        s = (n - 1) % UC
                        dve.wait_ge(gelu_made, b * NBLOCKS + i - 1 + 1)
                        if n >= UC + 1:
                            dve.wait_ge(down_made, b * NBLOCKS + i - 1 - UC + 1)
                        dve.tensor_copy(g_hi[s], g32[s])
                        dve.drain()
                        dve.tensor_tensor(g_lo[s], g32[s], g_hi[s], ALU.subtract).then_inc(g_split, 1)
                run_c(dve, step_c, NBLOCKS + 1)
                all_meet(dve, 4 + 3 * b)

            def phase_d(b):
                with dve.Fori(0, CHUNKS) as c:
                    for n in range(4):
                        add_first(b, c * 4 + n, n, yg_last, y_in_last, 4)
                        add_second(b, c * 4 + n, n, yg_last, 4)
                all_meet(dve, 5 + 3 * b)
            batches(dve, phase_a, phase_b, phase_c, phase_d)

        @block.gpsimd
        def _(pool):
            all_meet(pool, 1)
            def gather_results(d, t, n, y, y_sem, deep, free):
                if free:
                    pool.wait_ge(out_made, d * TILES + t - deep + 1)
                settled(pool)
                pool.tensor_copy(slot_now[:, n % 4, :], rows_at[:, ds(t, 1), :].rearrange("p o h -> p (o h)"))\
                    .then_inc(slot_copied, 1)
                pool.wait_ge(slot_copied, d * TILES + t + 1)
                settled(pool)
                for x in range(2):
                    pool.indirect_dma_start(y[n % deep][x], None, y_rows,
                                            bass.IndirectOffsetOnAxis(slot_now[:, n % 4, x:x + 1], 0))\
                        .then_inc(y_sem[n % deep], 16)

            def phase_a(b, d):
                pool.memset(k4acc[:, :], 0.0)
                pool.drain()
                if d is not None:
                    gather_results(d, 0, 0, yg, y_in, 2, False)
                    gather_results(d, 1, 1, yg, y_in, 2, False)

                def step_a(i, n):
                    if d is not None and n < TILES - 2:
                        gather_results(d, i + 2, n + 2, yg, y_in, 2, True)
                    if 6 <= n < TILES + 6:
                        t = b * TILES + i - 6
                        pool.wait_ge(k4_made, t + 1)
                        settled(pool)
                        pool.tensor_tensor(k4acc[:, :], k4acc[:, :], k4[:, (n - 6) % 2, :], ALU.add).then_inc(k4_added, 1)
                        pool.drain()
                run(pool, step_a, LAST_A, TILES if d is None else TILES - 8)
                all_meet(pool, 2 + 3 * b)

            def phase_b(b):
                with pool.Fori(0, CHUNKS // 2) as it:
                    for c in range(2):
                        pool.wait_ge(slots_made, b * CHUNKS + it * 2 + c + 1)
                        settled(pool)
                        for s in range(4):
                            for x in range(2):
                                pool.indirect_dma_start(place_ids, bass.IndirectOffsetOnAxis(slot_u[:, c, s, x:x + 1], 0),
                                                        id_u[:, c, s:s + 1], None).then_inc(ids_stored[c], 16)
                for c in range(2):
                    pool.wait_ge(ids_stored[c], 128 * (CHUNKS // 2) * (b + 1))
                settled(pool)
                all_meet(pool, 3 + 3 * b)

            def phase_c(b):
                pool.wait_ge(block_rows_made, b + 1)
                settled(pool)
                pool.indirect_dma_start(ids_rows[:, :], None, place_ids.rearrange("(r n) o -> r (n o)", n=BLOCK),
                                        bass.IndirectOffsetOnAxis(blk_at[:, 0:1], 0)).then_inc(ids_in, 16)
                pool.wait_ge(ids_kept, b + 1)
                settled(pool)
                def gather_blocks(it, first):
                    for n in range(UC):
                        pool.wait_ge(xg_in[n], 32 * (b * (NBLOCKS // UC) + it))
                        settled(pool)
                        pool.tensor_copy(ids_now[:, n, :], ids_all[:, ds(it * UC + n, 1), :].rearrange("p o h -> p (o h)"))\
                            .then_inc(ids_copied, 1)
                        pool.wait_ge(ids_copied, b * NBLOCKS + it * UC + n + 1)
                        settled(pool)
                        if not first:
                            pool.wait_ge(xg_turned, b * NBLOCKS + it * UC + n - UC + 1)
                            settled(pool)
                        for hh in range(2):
                            pool.indirect_dma_start(xg[n][:, hh, :], None, xn2_rows,
                                                    bass.IndirectOffsetOnAxis(ids_now[:, n, hh:hh + 1], 0))\
                                .then_inc(xg_in[n], 16)
                gather_blocks(0, True)
                with pool.Fori(1, NBLOCKS // UC) as it:
                    gather_blocks(it, False)
                all_meet(pool, 4 + 3 * b)

            def phase_d(b):
                def gather_chunk(c, par, first):
                    pool.tensor_copy(slots_last[:, par, :], rows_at[:, ds(c * 4, 4), :].rearrange("p t x -> p (t x)"))\
                        .then_inc(slot_copied, 1)
                    pool.wait_ge(slot_copied, b * TILES + c + 1)
                    settled(pool)
                    for n in range(4):
                        if not first:
                            pool.wait_ge(out_made, b * TILES + (c - 1) * 4 + n + 1)
                            settled(pool)
                        for x in range(2):
                            pool.indirect_dma_start(yg_last[n][x], None, y_rows,
                                                    bass.IndirectOffsetOnAxis(slots_last[:, par, 2 * n + x:2 * n + x + 1], 0))\
                                .then_inc(y_in_last[n], 16)
                gather_chunk(0, 0, True)
                gather_chunk(1, 1, False)
                with pool.Fori(1, CHUNKS // 2) as it:
                    for par in range(2):
                        gather_chunk(it * 2 + par, par, False)
                all_meet(pool, 5 + 3 * b)
            batches(pool, phase_a, phase_b, phase_c, phase_d)


def kernel(x, L0_tok_W, L0_attn_W_qkv, L0_attn_b_qkv, L0_attn_W_out, L0_attn_b_out, L0_ffn_router_w,
           L0_ffn_w1, L0_ffn_b1, L0_ffn_w2, L0_ffn_b2):
    import numpy as np
    import concourse.bacc as bacc
    from concourse.bass_utils import run_bass_kernel_spmd

    def cols(w, n):
        return w.reshape(n, P, -1).transpose(1, 0, 2)

    x = np.asarray(x)
    xp = np.pad(x, ((0, 0), (0, 0), (0, PATCH - STRIDE), (0, 0)), mode="edge")
    steps = 2 * (ROWS - STRIDE // 2)
    chunks = [xp[b, :, c * steps:c * steps + 2 * ROWS, :].reshape(C, ROWS // 4, 4, 2, V)
              .transpose(3, 0, 2, 1, 4).reshape(P, XC)
              for b in range(B) for c in range(CHUNKS)]
    chunks.append(chunks[0])
    w = np.asarray(L0_tok_W).reshape(D, 2, PATCH // 2 + 1, C)
    w_tok = np.stack([w[:, r, f, :].T for r, f in FREQ])
    w_qkv, w_out = np.asarray(L0_attn_W_qkv), np.asarray(L0_attn_W_out)
    b_qkv = np.asarray(L0_attn_b_qkv)
    b_col = b_qkv.reshape(3, DC, P)
    arrays = {
        "x": np.stack(chunks),
        "w_tok": cols(w_tok.reshape(len(FREQ) * C, D), KW),
        "w_qkv": cols(w_qkv, DC),
        "w_out": cols(w_out, DC),
        "w_vT": cols(w_qkv[:, 2 * D:].T, DC),
        "w_r": cols(np.asarray(L0_ffn_router_w).T, DC),
        "b_qkv": np.broadcast_to(b_qkv, (P, 3 * D)),
        "b_out": np.broadcast_to(np.asarray(L0_attn_b_out), (P, D)),
        "b_qv_col": np.concatenate([b_col[0], b_col[2]]).T,
        "b_1": np.asarray(L0_ffn_b1).reshape(E * DC, P).T,
        "b_2": np.broadcast_to(np.asarray(L0_ffn_b2).reshape(1, E, D), (P, E, D)),
        "w_1": np.asarray(L0_ffn_w1).reshape(E, DC, P, D).transpose(2, 0, 1, 3),
        "w_2": np.asarray(L0_ffn_w2).reshape(E, DC, P, D).transpose(2, 0, 1, 3),
    }
    p = np.arange(P)
    coef = np.zeros((P, KW, PATCH))
    for n, (r, f) in enumerate(FREQ):
        angle = 2 * np.pi * ((f * np.arange(PATCH)) % PATCH) / PATCH
        coef[(n % 2) * C:(n % 2 + 1) * C, n // 2] = (-np.sin(angle) if r else np.cos(angle)) / np.sqrt(PATCH)
    e = np.arange(E)
    constants = {
        "ident": np.eye(P),
        "tri": p[:, None] < p[None, :],
        "coef": coef.reshape(P, P),
        "pair": (p[:, None] % C) == np.arange(C)[None, :],
        "pick": p[:, None] == np.arange(2)[None, :],
        "iota_e": np.broadcast_to(e, (P, E)),
        "region0": np.broadcast_to(e * NT, (P, E)),
        "thr": np.broadcast_to(np.arange(REGION) * BLOCK, (P, REGION)),
        "upto": np.broadcast_to(e[None, :] <= e[:, None], (P, E, E)),
        "iota_b": np.broadcast_to(np.arange(NBLOCKS), (P, NBLOCKS)),
        "ids_0": p[:, None] + P * np.arange(CHUNK_TILES)[None, :],
    }
    arrays.update({"c_" + k: np.asarray(v, np.float32) for k, v in constants.items()})
    arrays = {k: np.ascontiguousarray(v) for k, v in arrays.items()}

    nc = bacc.Bacc("TRN2", target_bir_lowering=False, num_devices=1, dynamic_dma_scratch_size=8192)
    ins = {k: nc.dram_tensor(k + "_in", v.shape, F32, kind="ExternalInput").ap() for k, v in arrays.items()}
    out = nc.dram_tensor("out", (B * NT, D), F32, kind="ExternalOutput").ap()
    build(nc, ins, out)
    r = run_bass_kernel_spmd(nc, [{k + "_in": v for k, v in arrays.items()}], core_ids=[0])
    got = r.results[0]["out"]
    return got.reshape(B, NPATCH, V, D).transpose(0, 2, 1, 3).reshape(B, NT, D)
```
